# Optimizing a Trainium2 kernel written in Bass

```python
import numpy as np
import jax
import jax.numpy as jnp

def _softmax(x, axis=-1):
    return jax.nn.softmax(x, axis=axis)

def _gelu(x):
    return jax.nn.gelu(x, approximate=True)

def _silu(x):
    return jax.nn.silu(x)

def _sigmoid(x):
    return jax.nn.sigmoid(x)

def _layernorm(x, axis=-1, eps=1e-05):
    m = jnp.mean(x, axis=axis, keepdims=True)
    v = jnp.var(x, axis=axis, keepdims=True)
    return (x - m) / jnp.sqrt(v + eps)

def _scatter_add(tgt, idx, src, axis=0):
    return tgt.at[idx].add(src)

def _segment_sum(src, seg, n):
    return jax.ops.segment_sum(src, seg, n)
kernel_name = 'mk_early_fusion_d1_tok_img256_r4_139581'

def setup_inputs(seed: int=0):
    np.random.seed(seed)
    _w = jnp.asarray

    def _rec_inputs():
        import jax
        import jax.numpy as jnp
        _rk = jax.random.key(seed)
        x = -0.000798584 + 1.00089 * jax.random.normal(jax.random.fold_in(_rk, 1), (64, 64, 75, 3), jnp.float32)
        txt = 0.0043597 + 0.112233 * jax.random.normal(jax.random.fold_in(_rk, 2), (64, 32, 64), jnp.float32)
        return (x, txt)
    x, txt = _rec_inputs()

    def _L0_tok_setup():
        import jax, jax.numpy as jnp
        import numpy as np
        EPS = 1e-05
        B, T, V = (32, 64, 75)
        DIMS = [3, 128, 128, 64]

        def _layer(x, A, W, b, g, be, m, v, relu):
            x = jnp.einsum('btvc,co->btvo', x, W)
            x = jnp.einsum('uv,btvo->btuo', A, x)
            x = x + b
            x = (x - m) * (g * jax.lax.rsqrt(v + EPS)) + be
            if relu:
                x = jax.nn.relu(x)
            return x
        key = jax.random.key(seed)
        ks = jax.random.split(key, 32)
        inp = {'x': jax.random.normal(ks[0], (B, T, V, DIMS[0]), dtype=jnp.float32), 'A': jax.random.uniform(ks[1], (V, V), dtype=jnp.float32) / V}
        ki = 2
        for i in range(3):
            cin, cout = (DIMS[i], DIMS[i + 1])
            bound = float(np.sqrt(6.0 / (cin + cout)))
            inp[f'W{i}'] = jax.random.uniform(ks[ki], (cin, cout), minval=-bound, maxval=bound, dtype=jnp.float32)
            ki += 1
            inp[f'b{i}'] = jnp.zeros((cout,), dtype=jnp.float32)
            inp[f'g{i}'] = jnp.ones((cout,), dtype=jnp.float32)
            inp[f'be{i}'] = jnp.zeros((cout,), dtype=jnp.float32)
            inp[f'm{i}'] = 0.1 * jax.random.normal(ks[ki], (cout,), dtype=jnp.float32)
            ki += 1
            inp[f'v{i}'] = jax.random.uniform(ks[ki], (cout,), minval=0.5, maxval=1.5, dtype=jnp.float32)
            ki += 1
        return inp
    _L0_tok_all = _L0_tok_setup()
    _L0_tok_in = {k: v for k, v in _L0_tok_all.items() if k in ('A', 'W0', 'b0', 'g0', 'be0', 'm0', 'v0', 'W1', 'b1', 'g1', 'be1', 'm1', 'v1', 'W2', 'b2', 'g2', 'be2', 'm2', 'v2')}
    del _L0_tok_all

    def _L0_attn_setup():
        import jax, jax.numpy as jnp
        import numpy as np
        key = jax.random.key(seed)
        ks = jax.random.split(key, 4)
        B, S, D = (4, 1024, 64)
        x = jax.random.normal(ks[0], (B, S, D), dtype=jnp.float32)
        Wq = jax.random.normal(ks[1], (D, D), dtype=jnp.float32) * 0.02
        Wk = jax.random.normal(ks[2], (D, D), dtype=jnp.float32) * 0.02
        Wv = jax.random.normal(ks[3], (D, D), dtype=jnp.float32) * 0.02
        bq = jnp.zeros((D,), dtype=jnp.float32)
        bk = jnp.zeros((D,), dtype=jnp.float32)
        bv = jnp.zeros((D,), dtype=jnp.float32)
        return {'x': x, 'Wq': Wq, 'bq': bq, 'Wk': Wk, 'bk': bk, 'Wv': Wv, 'bv': bv}
    _L0_attn_all = _L0_attn_setup()
    _L0_attn_in = {k: v for k, v in _L0_attn_all.items() if k in ('Wq', 'bq', 'Wk', 'bk', 'Wv', 'bv')}
    del _L0_attn_all

    def _L0_ffn_setup():
        import jax, jax.numpy as jnp
        import numpy as np
        C = 64
        EPS = 1e-05
        N_ITERS = 30

        def _layernorm(x, w, bias):
            mu = jnp.mean(x, axis=-1, keepdims=True)
            var = jnp.mean(jnp.square(x - mu), axis=-1, keepdims=True)
            return (x - mu) * jax.lax.rsqrt(var + EPS) * w + bias
        key = jax.random.key(seed)
        kx, kw, kb, klw, klb = jax.random.split(key, 5)
        x = jax.random.normal(kx, (8, 512, C), dtype=jnp.float32)
        bound = 1.0 / np.sqrt(C)
        W = jax.random.uniform(kw, (C, C), minval=-bound, maxval=bound, dtype=jnp.float32)
        b = jax.random.uniform(kb, (C,), minval=-bound, maxval=bound, dtype=jnp.float32)
        ln_w = jnp.ones((C,), dtype=jnp.float32)
        ln_b = jnp.zeros((C,), dtype=jnp.float32)
        return {'x': x, 'ln_w': ln_w, 'ln_b': ln_b, 'W': W, 'b': b}
    _L0_ffn_all = _L0_ffn_setup()
    _L0_ffn_in = {k: v for k, v in _L0_ffn_all.items() if k in ('ln_w', 'ln_b', 'W', 'b')}
    del _L0_ffn_all
    return {'x': x, 'txt': txt, 'L0_tok_A': _L0_tok_in['A'], 'L0_tok_W0': _L0_tok_in['W0'], 'L0_tok_b0': _L0_tok_in['b0'], 'L0_tok_g0': _L0_tok_in['g0'], 'L0_tok_be0': _L0_tok_in['be0'], 'L0_tok_m0': _L0_tok_in['m0'], 'L0_tok_v0': _L0_tok_in['v0'], 'L0_tok_W1': _L0_tok_in['W1'], 'L0_tok_b1': _L0_tok_in['b1'], 'L0_tok_g1': _L0_tok_in['g1'], 'L0_tok_be1': _L0_tok_in['be1'], 'L0_tok_m1': _L0_tok_in['m1'], 'L0_tok_v1': _L0_tok_in['v1'], 'L0_tok_W2': _L0_tok_in['W2'], 'L0_tok_b2': _L0_tok_in['b2'], 'L0_tok_g2': _L0_tok_in['g2'], 'L0_tok_be2': _L0_tok_in['be2'], 'L0_tok_m2': _L0_tok_in['m2'], 'L0_tok_v2': _L0_tok_in['v2'], 'L0_attn_Wq': _L0_attn_in['Wq'], 'L0_attn_bq': _L0_attn_in['bq'], 'L0_attn_Wk': _L0_attn_in['Wk'], 'L0_attn_bk': _L0_attn_in['bk'], 'L0_attn_Wv': _L0_attn_in['Wv'], 'L0_attn_bv': _L0_attn_in['bv'], 'L0_ffn_ln_w': _L0_ffn_in['ln_w'], 'L0_ffn_ln_b': _L0_ffn_in['ln_b'], 'L0_ffn_W': _L0_ffn_in['W'], 'L0_ffn_b': _L0_ffn_in['b']}

def reference(x, txt, L0_tok_A, L0_tok_W0, L0_tok_b0, L0_tok_g0, L0_tok_be0, L0_tok_m0, L0_tok_v0, L0_tok_W1, L0_tok_b1, L0_tok_g1, L0_tok_be1, L0_tok_m1, L0_tok_v1, L0_tok_W2, L0_tok_b2, L0_tok_g2, L0_tok_be2, L0_tok_m2, L0_tok_v2, L0_attn_Wq, L0_attn_bq, L0_attn_Wk, L0_attn_bk, L0_attn_Wv, L0_attn_bv, L0_ffn_ln_w, L0_ffn_ln_b, L0_ffn_W, L0_ffn_b):
    import jax
    import jax.numpy as jnp

    def _L0_tok_ref(x, A, W0, b0, g0, be0, m0, v0, W1, b1, g1, be1, m1, v1, W2, b2, g2, be2, m2, v2):
        import jax, jax.numpy as jnp
        import numpy as np
        EPS = 1e-05
        B, T, V = (32, 64, 75)
        DIMS = [3, 128, 128, 64]

        def _layer(x, A, W, b, g, be, m, v, relu):
            x = jnp.einsum('btvc,co->btvo', x, W)
            x = jnp.einsum('uv,btvo->btuo', A, x)
            x = x + b
            x = (x - m) * (g * jax.lax.rsqrt(v + EPS)) + be
            if relu:
                x = jax.nn.relu(x)
            return x
        x = _layer(x, A, W0, b0, g0, be0, m0, v0, relu=True)
        x = _layer(x, A, W1, b1, g1, be1, m1, v1, relu=True)
        x = _layer(x, A, W2, b2, g2, be2, m2, v2, relu=False)
        return x.mean(axis=2)

    def _L0_attn_ref(x, Wq, bq, Wk, bk, Wv, bv):
        import jax, jax.numpy as jnp
        import numpy as np
        Q = jnp.einsum('bsd,de->bse', x, Wq) + bq
        K = jnp.einsum('bsd,de,->bse'.replace(',->', '->'), x, Wk) + bk
        V = jnp.einsum('bsd,de->bse', x, Wv) + bv
        scale = 1.0 / jnp.sqrt(jnp.asarray(Q.shape[-1], dtype=jnp.float32))
        scores = jnp.einsum('bqd,bkd->bqk', Q, K) * scale
        weights = jax.nn.softmax(scores, axis=-1)
        return jnp.einsum('bqk,bkd->bqd', weights, V)

    def _L0_ffn_ref(x, ln_w, ln_b, W, b):
        import jax, jax.numpy as jnp
        import numpy as np
        C = 64
        EPS = 1e-05
        N_ITERS = 30

        def _layernorm(x, w, bias):
            mu = jnp.mean(x, axis=-1, keepdims=True)
            var = jnp.mean(jnp.square(x - mu), axis=-1, keepdims=True)
            return (x - mu) * jax.lax.rsqrt(var + EPS) * w + bias

        def step(h, _):
            h = h + 0.01 * jnp.tanh(h)
            h = h * jax.nn.sigmoid(h)
            h = _layernorm(h, ln_w, ln_b)
            h = jnp.einsum('bsc,dc->bsd', h, W) + b
            return (h, None)
        x, _ = jax.lax.scan(step, x, None, length=N_ITERS)
        return x
    h = _L0_tok_ref(x, L0_tok_A, L0_tok_W0, L0_tok_b0, L0_tok_g0, L0_tok_be0, L0_tok_m0, L0_tok_v0, L0_tok_W1, L0_tok_b1, L0_tok_g1, L0_tok_be1, L0_tok_m1, L0_tok_v1, L0_tok_W2, L0_tok_b2, L0_tok_g2, L0_tok_be2, L0_tok_m2, L0_tok_v2)
    h = jnp.concatenate([h, txt], axis=1)
    h = h + _L0_attn_ref(_layernorm(h, axis=-1), L0_attn_Wq, L0_attn_bq, L0_attn_Wk, L0_attn_bk, L0_attn_Wv, L0_attn_bv)
    h = h + _L0_ffn_ref(_layernorm(h, axis=-1), L0_ffn_ln_w, L0_ffn_ln_b, L0_ffn_W, L0_ffn_b)
    return h

_drawn_inputs = setup_inputs


def setup_inputs(seed=0):
    import zlib

    import numpy as np

    out = dict(_drawn_inputs(seed))
    spreads = {'L0_tok_b0': (0.0, 0.1),
     'L0_tok_g0': (1.0, 0.2),
     'L0_tok_be0': (0.0, 0.1),
     'L0_tok_b1': (0.0, 0.1),
     'L0_tok_g1': (1.0, 0.2),
     'L0_tok_be1': (0.0, 0.1),
     'L0_tok_b2': (0.0, 0.1),
     'L0_tok_g2': (1.0, 0.2),
     'L0_tok_be2': (0.0, 0.1),
     'L0_attn_bq': (0.0, 0.472),
     'L0_attn_bk': (0.0, 2.0),
     'L0_attn_bv': (0.0, 0.1),
     'L0_ffn_ln_w': (1.0, 0.2),
     'L0_ffn_ln_b': (0.0, 0.1)}
    factors = {'L0_tok_A': 8.0, 'L0_attn_Wq': 5.698}
    for name, (base, spread) in spreads.items():
        noise = np.random.default_rng([zlib.crc32(name.encode()), seed]).standard_normal(out[name].shape)
        drawn = base * np.exp(spread * noise) if base else spread * noise
        out[name] = jnp.asarray(drawn.astype(out[name].dtype))
    for name, factor in factors.items():
        out[name] = (out[name] * factor).astype(out[name].dtype)
    return out
```

```python
from contextlib import ExitStack

import numpy as np

import concourse.bass as bass
from concourse import mybir

F32 = mybir.dt.float32
F16 = mybir.dt.float16
I32 = mybir.dt.int32
ALU = mybir.AluOpType
ACT = mybir.ActivationFunctionType
AX_X = mybir.AxisListType.X
RMAX = bass.bass_isa.ReduceOp.max

P = 128
B, T, V, CIN = 64, 64, 75, 3
FRAMES = B * T
C = 128
D = 64
TXT = 32
S = T + TXT
EPS = 1e-5
QUART = 4
GF = 5
PH = 3
R = GF * V // PH
GV = GF * V
GROUPS = 205
QF = GROUPS * GF
QROWS = QF * V
ZF = 41
ZS = QF // ZF
ZB = 5
ZCOLS = ZB * ZF * V
ZPAD = P - R
ITERS = 30
SPAN = [(0, 2), (1, 3), (3, 2)]
BAND0 = [0, 2 * V, 5 * V]
BANDW = 7 * V


def band_pieces():
    out = []
    for ph in range(PH):
        r = 0
        while r < R:
            flat = ph * R + r
            f, v = divmod(flat, V)
            n = min(V - v, R - r)
            out.append((ph, f, r, v, n))
            r += n
    return out


def build(nc, x_v, txt, AT, A, W0T, W1, W2, par0, par1, par2, attn, ffn, out):
    zs = nc.dram_tensor("z_parts", [2, CIN, QUART * QROWS], F16, kind="Internal").ap()
    h2_dram = nc.dram_tensor("h2_rows", [B * S, D], F32, kind="Internal").ap()
    pooled_dram = nc.dram_tensor("pooled_parts", [PH, QUART * QF, C], F32, kind="Internal").ap()
    ctx = ExitStack()

    def sb(name, shape, dt=F32):
        return ctx.enter_context(nc.sbuf_tensor(name, shape, dt))

    def sem(name):
        return ctx.enter_context(nc.semaphore(name))

    with ctx:
        ps = ctx.enter_context(nc.psum_tensor("ps", [P, 8, 512], F32))
        AThi = sb("AThi", [P, BANDW], F16)
        ATlo = sb("ATlo", [P, BANDW], F16)
        abar = sb("abar", [P, PH, 32])
        W0K = sb("W0K", [P, QUART, C], F16)
        W1hi = sb("W1hi", [P, C], F16)
        W1lo = sb("W1lo", [P, C], F16)
        negb1 = sb("negb1", [P, QUART, C])
        W2s = sb("W2s", [P, D])
        b2row = sb("b2row", [P, D])
        ident = sb("ident", [P, P])
        sz = sb("sz", [P, 1])

        setup(nc, ps, x_v, AT, A, W0T, W1, W2, par0, par1, par2, zs,
              AThi, ATlo, abar, W0K, W1hi, W1lo, negb1, W2s, b2row, ident, sz)
        tokenise(nc, ps, zs, pooled_dram, AThi, ATlo, abar, W0K, W1hi, W1lo, negb1)
        fuse(nc, ps, pooled_dram, h2_dram, txt, attn, ffn, W2s, b2row, ident, out)


def setup(nc, ps, x_v, AT, A, W0T, W1, W2, par0, par1, par2, zs,
          AThi, ATlo, abar, W0K, W1hi, W1lo, negb1, W2s, b2row, ident, sz):
    with ExitStack() as ctx:
        def sb(name, shape, dt=F32):
            return ctx.enter_context(nc.sbuf_tensor(name, shape, dt))

        def sem(name):
            return ctx.enter_context(nc.semaphore(name))

        xs = sb("xs", [V, QUART, ZS, CIN * ZF])
        at = sb("at", [V, V])
        a_rows = sb("a_rows", [V, V])
        band = sb("band", [P, BANDW])
        bandc = sb("bandc", [P, 7])
        w0 = sb("w0", [P, CIN])
        w1 = sb("w1", [P, C])
        w2 = sb("w2", [P, D])
        cols = sb("cols", [P, 2, 5])
        row1 = sb("row1", [P, 5, C])
        row2 = sb("row2", [P, 5, D])
        rc = sb("rc", [P, 4, 2])
        r1 = sb("r1", [P, 4, C])
        r2 = sb("r2", [P, 4, D])
        bc = sb("bc", [P, 2])
        b1r = sb("b1r", [P, C])
        b2r = sb("b2r", [P, D])
        mx = sb("mx", [P, 8])
        mxa = sb("mxa", [P, 8])
        sc = sb("sc", [P, 16])
        stack = sb("stack", [P, P])
        part = sb("part", [P, 2, CIN], F16)
        bpart = sb("bpart", [P, 3], F16)
        ones = sb("ones", [P, P])
        acol = sb("acol", [V, 2])
        cvec = sb("cvec", [P, P])
        zhi = sb("zhi", [P, 2, ZB * V], F16)
        zlo = sb("zlo", [P, 2, ZB * V], F16)

        loaded = sem("params_loaded")
        x_loaded = sem("x_loaded")
        band_clear = sem("band_clear")
        band_loaded = sem("band_loaded")
        chain = sem("vector_chain")
        id_made = sem("ident_made")
        var_ready = sem("var_ready")
        root_ready = sem("root_ready")
        max_ready = sem("max_ready")
        max_all = sem("max_all")
        stack_ready = sem("stack_ready")
        stack_t = sem("stack_transposed")
        cvec_ready = sem("cvec_ready")
        const_ready = sem("const_ready")
        abar_ready = sem("abar_ready")
        asum_ready = sem("asum_ready")
        sz_ready = sem("sz_ready")
        z_ready = sem("z_product_ready")
        zhi_done = sem("z_hi_done")
        zlo_done = sem("z_lo_done")
        z_stored = [sem(f"z_stored{i}") for i in range(2)]

        pieces = band_pieces()
        NPAR = 5 + 4 * 5
        ZN = QUART * (ZS // ZB)

        with nc.Block() as block:
            @block.sync
            def _(sp):
                for q in range(QUART):
                    sp.dma_start(xs[:, q], x_v[:, q]).then_inc(x_loaded, 16)
                sp.wait_ge(band_clear, 1)
                for ph, f, r, v, n in pieces:
                    c0 = BAND0[ph] + (f - SPAN[ph][0]) * V
                    sp.dma_start(band[r:r + n, c0:c0 + V], AT[v:v + n, :]).then_inc(band_loaded, 16)
                for n in range(ZN):
                    k, q = divmod(n, QUART)
                    sp.wait_ge(zhi_done, n + 1)
                    sp.wait_ge(zlo_done, n + 1)
                    for w, src in ((0, zhi), (1, zlo)):
                        for c in range(CIN):
                            base = q * QROWS + k * ZCOLS
                            dst = zs[w, c, base:base + ZCOLS].rearrange("(s f u) -> f s u", s=ZB, f=ZF)
                            s_ = src[c * ZF:(c + 1) * ZF, n % 2, :].rearrange("p (s u) -> p s u", s=ZB)
                            sp.dma_start(dst, s_).then_inc(z_stored[n % 2], 16)
                for slot in z_stored:
                    sp.wait_ge(slot, ZN // 2 * 2 * CIN * 16)

            @block.scalar
            def _(act):
                act.dma_start(at[:], AT).then_inc(loaded, 16)
                act.dma_start(a_rows[:], A).then_inc(loaded, 16)
                act.dma_start(w0[:], W0T).then_inc(loaded, 16)
                act.dma_start(w1[:], W1).then_inc(loaded, 16)
                act.dma_start(w2[:], W2).then_inc(loaded, 16)
                for i, p_ in enumerate(par0):
                    act.dma_start(cols[:, 0, i:i + 1], p_.rearrange("(c one) -> c one", one=1)).then_inc(loaded, 16)
                for i, p_ in enumerate(par1):
                    act.dma_start(cols[:, 1, i:i + 1], p_.rearrange("(c one) -> c one", one=1)).then_inc(loaded, 16)
                for i, p_ in enumerate(par1):
                    act.dma_start(row1[:, i, :], p_.partition_broadcast(P)).then_inc(loaded, 16)
                for i, p_ in enumerate(par2):
                    act.dma_start(row2[:, i, :], p_.partition_broadcast(P)).then_inc(loaded, 16)
                act.wait_ge(var_ready, 3)
                nc.scalar.activation(rc[:, 1, :], rc[:, 0, :], ACT.Sqrt).then_inc(root_ready, 1)
                nc.scalar.activation(r1[:, 1, :], r1[:, 0, :], ACT.Sqrt).then_inc(root_ready, 1)
                nc.scalar.activation(r2[:, 1, :], r2[:, 0, :], ACT.Sqrt).then_inc(root_ready, 1)
                act.wait_ge(sz_ready, 1)
                for n in range(ZN):
                    act.wait_ge(z_ready, n + 1)
                    if n >= 2:
                        act.wait_ge(z_stored[n % 2], n // 2 * 2 * CIN * 16)
                    nc.scalar.activation(zhi[0:CIN * ZF, n % 2, :], ps[0:CIN * ZF, n % 2, 0:ZB * V], ACT.Identity,
                                         scale=sz[0:CIN * ZF, :]).then_inc(zhi_done, 1)

            @block.gpsimd
            def _(pool):
                pool.memset(ident[:], 0.0).then_inc(id_made, 1)
                pool.wait_ge(id_made, 1)
                pool.affine_select(out=ident[:], in_=ident[:], compare_op=ALU.not_equal, fill=1.0, base=0,
                                   pattern=[[-1, P]], channel_multiplier=1).then_inc(id_made, 1)
                pool.wait_ge(max_ready, 1)
                pool.partition_all_reduce(mxa[:], mx[:], P, RMAX).then_inc(max_all, 1)

            @block.vector
            def _(dve):
                done = [0]

                def link(ins):
                    done[0] += 1
                    ins.then_inc(chain, 1)
                    dve.wait_ge(chain, done[0])

                v_ = nc.vector
                v_.memset(band[:], 0.0).then_inc(band_clear, 1)
                link(v_.memset(mx[:], 0.0))
                link(v_.memset(ones[:], 1.0))
                link(v_.memset(stack[:], 0.0))
                link(v_.memset(abar[:], 0.0))
                link(v_.memset(W0K[:], 0.0))
                dve.wait_ge(loaded, NPAR * 16)
                v_.tensor_scalar(rc[:, 0, :], cols[:, :, 4], EPS, None, ALU.add).then_inc(var_ready, 1)
                v_.tensor_scalar(r1[:, 0, :], row1[:, 4, :], EPS, None, ALU.add).then_inc(var_ready, 1)
                v_.tensor_scalar(r2[:, 0, :], row2[:, 4, :], EPS, None, ALU.add).then_inc(var_ready, 1)
                dve.wait_ge(root_ready, 3)
                for r, g, b, be, m, bias in ((rc, cols[:, :, 1], cols[:, :, 0], cols[:, :, 2], cols[:, :, 3], bc[:]),
                                             (r1, row1[:, 1, :], row1[:, 0, :], row1[:, 2, :], row1[:, 3, :], b1r[:]),
                                             (r2, row2[:, 1, :], row2[:, 0, :], row2[:, 2, :], row2[:, 3, :], b2r[:])):
                    link(v_.reciprocal(r[:, 2, :], r[:, 1, :]))
                    link(v_.tensor_tensor(r[:, 3, :], r[:, 2, :], r[:, 2, :], ALU.mult))
                    link(v_.tensor_tensor(r[:, 3, :], r[:, 3, :], r[:, 0, :], ALU.mult))
                    link(v_.tensor_scalar(r[:, 3, :], r[:, 3, :], -0.5, 1.5, ALU.mult, ALU.add))
                    link(v_.tensor_tensor(r[:, 2, :], r[:, 2, :], r[:, 3, :], ALU.mult))
                    link(v_.tensor_tensor(r[:, 2, :], r[:, 2, :], g, ALU.mult))
                    link(v_.tensor_tensor(r[:, 3, :], b, m, ALU.subtract))
                    link(v_.tensor_tensor(r[:, 3, :], r[:, 3, :], r[:, 2, :], ALU.mult))
                    link(v_.tensor_tensor(bias, r[:, 3, :], be, ALU.add))
                link(v_.tensor_scalar(w0[:], w0[:], rc[:, 2, 0:1], None, ALU.mult))
                link(v_.tensor_tensor(w1[:], w1[:], r1[:, 2, :], ALU.mult))
                link(v_.tensor_tensor(w2[:], w2[:], r2[:, 2, :], ALU.mult))
                link(v_.tensor_reduce(mx[0:V, 0:1], a_rows[:], AX_X, ALU.add, apply_absolute_value=True))
                dve.wait_ge(x_loaded, QUART * 16)
                link(v_.tensor_reduce(mx[0:V, 1:2], xs[:].rearrange("p q s f -> p (q s f)"), AX_X, ALU.max,
                                      apply_absolute_value=True))
                link(v_.tensor_reduce(mx[:, 2:3], w0[:], AX_X, ALU.add, apply_absolute_value=True))
                link(v_.tensor_reduce(mx[:, 3:4], bc[:, 0:1], AX_X, ALU.max, apply_absolute_value=True))
                v_.tensor_reduce(mx[:, 4:5], w1[:], AX_X, ALU.max, apply_absolute_value=True).then_inc(max_ready, 1)
                dve.wait_ge(max_all, 1)
                link(v_.tensor_copy(sc[:, 0:1], mxa[:, 0:1]))
                link(v_.tensor_tensor(sc[:, 1:2], mxa[:, 1:2], mxa[:, 0:1], ALU.mult))
                link(v_.scalar_tensor_tensor(sc[:, 2:3], sc[:, 1:2], mxa[:, 2:3], mxa[:, 3:4], ALU.mult, ALU.add))
                link(v_.tensor_copy(sc[:, 3:4], mxa[:, 4:5]))
                link(v_.tensor_scalar(sc[:, 0:4], sc[:, 0:4], 1e-30, None, ALU.max))
                link(v_.reciprocal(sc[:, 8:12], sc[:, 0:4]))
                link(v_.tensor_scalar(sc[:, 4:8].bitcast(I32), sc[:, 8:12].bitcast(I32), 0x7F800000, None,
                                      ALU.bitwise_and))
                link(v_.tensor_scalar(sc[:, 4:5], sc[:, 4:5], 2.0 ** 7, None, ALU.mult))
                link(v_.tensor_scalar(sc[:, 5:7], sc[:, 5:7], 2.0 ** 8, None, ALU.mult))
                link(v_.tensor_scalar(sc[:, 7:8], sc[:, 7:8], 2.0 ** 4, None, ALU.mult))
                v_.tensor_copy(sz[:], sc[:, 5:6]).then_inc(sz_ready, 1)
                link(v_.reciprocal(sc[:, 12:13], sc[:, 5:6]))
                link(v_.tensor_tensor(sc[:, 12:13], sc[:, 12:13], sc[:, 6:7], ALU.mult))
                link(v_.tensor_tensor(sc[:, 13:14], sc[:, 4:5], sc[:, 6:7], ALU.mult))
                link(v_.tensor_tensor(sc[:, 13:14], sc[:, 13:14], sc[:, 7:8], ALU.mult))
                link(v_.reciprocal(sc[:, 14:15], sc[:, 13:14]))

                def z_low(n):
                    dve.wait_ge(zhi_done, n + 1)
                    v_.scalar_tensor_tensor(zlo[0:CIN * ZF, n % 2, :], ps[0:CIN * ZF, n % 2, 0:ZB * V],
                                            sz[0:CIN * ZF, :], zhi[0:CIN * ZF, n % 2, :],
                                            ALU.mult, ALU.subtract).then_inc(zlo_done, 1)
                for n in range(ZN):
                    if n >= 2:
                        dve.wait_ge(z_stored[n % 2], n // 2 * 2 * CIN * 16)
                    z_low(n)

                dve.wait_ge(band_loaded, len(pieces) * 16)
                link(v_.tensor_reduce(bandc[:], band[:].rearrange("p (f u) -> p f u", u=V), AX_X, ALU.add))
                at_col = 0
                for ph in range(PH):
                    f0, n = SPAN[ph]
                    link(v_.tensor_scalar(abar[:, ph, f0:f0 + n], bandc[:, at_col:at_col + n], 1.0 / V, None, ALU.mult))
                    at_col += n
                link(v_.tensor_scalar(band[:], band[:], sc[:, 4:5], None, ALU.mult))
                link(v_.tensor_copy(AThi[:], band[:]))
                link(v_.tensor_tensor(ATlo[:], band[:], AThi[:], ALU.subtract))
                link(v_.tensor_scalar(w1[:], w1[:], sc[:, 7:8], None, ALU.mult))
                link(v_.tensor_copy(W1hi[:], w1[:]))
                link(v_.tensor_tensor(W1lo[:], w1[:], W1hi[:], ALU.subtract))
                for q in range(QUART):
                    link(v_.tensor_scalar(negb1[:, q, :], b1r[:], sc[:, 13:14], -1.0, ALU.mult, ALU.mult))
                link(v_.tensor_scalar(w0[:], w0[:], sc[:, 12:13], None, ALU.mult))
                link(v_.tensor_copy(part[:, 0, :], w0[:]))
                link(v_.tensor_tensor(part[:, 1, :], w0[:], part[:, 0, :], ALU.subtract))
                link(v_.tensor_tensor(bc[:, 0:1], bc[:, 0:1], sc[:, 6:7], ALU.mult))
                for i in range(3):
                    link(v_.tensor_copy(bpart[:, i:i + 1], bc[:, 0:1]))
                    link(v_.tensor_tensor(bc[:, 0:1], bc[:, 0:1], bpart[:, i:i + 1], ALU.subtract))
                for q in range(QUART):
                    for i, w in enumerate((0, 0, 1, 1)):
                        link(v_.tensor_copy(stack[:, 32 * q + 3 * i:32 * q + 3 * i + 3], part[:, w, :]))
                    link(v_.tensor_copy(stack[:, 32 * q + 12:32 * q + 15], bpart[:]))
                link(v_.tensor_reduce(acol[:, 0:1], at[:], AX_X, ALU.add))
                v_.tensor_scalar(acol[:, 1:2], acol[:, 0:1], 1.0 / V, None, ALU.mult).then_inc(abar_ready, 1)
                dve.wait_ge(asum_ready, 1)
                link(v_.tensor_copy(sc[:, 15:16], ps[:, 4, 0:1]))
                link(v_.tensor_tensor(sc[:, 15:16], sc[:, 15:16], bc[:, 1:2], ALU.mult))
                v_.tensor_copy(cvec[:], sc[:, 15:16].to_broadcast([P, P])).then_inc(cvec_ready, 1)
                v_.tensor_copy(stack[:, 15:16], stack[:, 15:16]).then_inc(stack_ready, 1)
                dve.wait_ge(stack_t, 1)
                for q in range(QUART):
                    link(v_.tensor_copy(W0K[32 * q:32 * q + 32, q, :], ps[32 * q:32 * q + 32, 5, 0:C]))
                dve.wait_ge(const_ready, 1)
                link(v_.tensor_tensor(b2row[:], ps[:, 6, 0:D], b2r[:], ALU.add))
                link(v_.tensor_scalar(W2s[:], w2[:], sc[:, 14:15], None, ALU.mult))

            @block.tensor
            def _(pe):
                pe.wait_ge(loaded, NPAR * 16)
                pe.wait_ge(x_loaded, QUART * 16)
                for n in range(ZN):
                    k, q = divmod(n, QUART)
                    if n >= 2:
                        pe.wait_ge(zlo_done, n - 1)
                    for s in range(ZB):
                        last = nc.tensor.matmul(ps[0:CIN * ZF, n % 2, s * V:(s + 1) * V],
                                                xs[:, q, k * ZB + s, :], at[:], start=True, stop=True)
                    last.then_inc(z_ready, 1)
                pe.wait_ge(abar_ready, 1)
                nc.tensor.matmul(ps[:, 4, 0:1], ones[0:V, :], acol[:, 1:2], start=True, stop=True).then_inc(asum_ready, 1)
                pe.wait_ge(cvec_ready, 1)
                nc.tensor.matmul(ps[:, 6, 0:D], cvec[:], w2[:], start=True, stop=True).then_inc(const_ready, 1)
                pe.wait_ge(stack_ready, 1)
                pe.wait_ge(id_made, 2)
                nc.tensor.transpose(ps[:, 5, 0:C], stack[:], ident[:]).then_inc(stack_t, 1)


def tokenise(nc, ps, zs, pooled_dram, AThi, ATlo, abar, W0K, W1hi, W1lo, negb1):
    with ExitStack() as ctx:
        def sb(name, shape, dt=F32):
            return ctx.enter_context(nc.sbuf_tensor(name, shape, dt))

        def sem(name):
            return ctx.enter_context(nc.semaphore(name))

        zk = sb("zk", [P, QROWS + ZPAD + 1], F16)
        y0hi = sb("y0hi", [P, 2, PH, QUART * C], F16)
        y0lo = sb("y0lo", [P, 2, PH, QUART * C], F16)
        z1hi = sb("z1hi", [P, 2, PH * P], F16)
        z1lo = sb("z1lo", [P, 2, PH * P], F16)
        y1 = sb("y1", [P, PH, QUART * C])
        stage = sb("stage", [96, 2, QUART, C])

        filled = sem("ones_filled")
        loaded = sem("z_loaded")
        y0_ready = sem("y0_ready")
        y0hi_done = sem("y0hi_done")
        y0lo_done = sem("y0lo_done")
        z1_ready = sem("z1_ready")
        z1hi_done = sem("z1hi_done")
        z1lo_done = sem("z1lo_done")
        y1_ready = sem("y1_ready")
        y1_done = sem("y1_done")
        pooled_ready = sem("pooled_ready")
        staged = sem("staged")
        stored = [sem(f"pooled_stored{i}") for i in range(2)]

        Y0B, Z1B, Y1B, PLB = 0, 2, 4, 7
        LAST = GROUPS - 1
        CH = 5
        CW = (QROWS // CH + 1) // 2 * 2

        def steps(eng, body):
            body(0, 0, 0, first=True)
            body(1, 1, 0)
            body(2, 0, 0)
            with eng.Fori(1, LAST // 2 - 1) as k:
                body(k * 2 + 1, 1, k)
                body(k * 2 + 2, 0, k)
            body(LAST - 1, 1, LAST // 2 - 1)
            body(LAST, 0, LAST // 2 - 1, last=True)

        with nc.Block() as block:
            @block.gpsimd
            def _(pool):
                for k in range(CH):
                    hi_ = QROWS + ZPAD + 1 if k == CH - 1 else (k + 1) * CW
                    pool.memset(zk[:, k * CW:hi_], 1.0).then_inc(filled, 1)

            @block.sync
            def _(sp):
                for k in range(CH):
                    sp.wait_ge(filled, k + 1)
                    for q in range(QUART):
                        for rep in range(2):
                            for w in range(2):
                                r0 = 32 * q + 6 * rep + 3 * w
                                end = min((k + 1) * CW, QROWS)
                                sp.dma_start(zk[r0:r0 + 3, k * CW:end],
                                             zs[w, :, q * QROWS + k * CW:q * QROWS + end]).then_inc(loaded, 16)

                def body(it, par, pair, first=False, last=False):
                    sp.wait_ge(staged, it + 1)
                    for ph in range(PH):
                        dst = pooled_dram[ph].rearrange("(q f) c -> f q c", q=QUART)[bass.ds(it * GF, GF)]
                        sp.dma_start(dst, stage[32 * ph:32 * ph + GF, par]).then_inc(stored[par], 16)
                steps(sp, body)
                for par in range(2):
                    sp.wait_ge(stored[par], (GROUPS + 1 - par) // 2 * PH * 16)

            @block.tensor
            def _(pe):
                def layer0(n, it, par, ph):
                    if not isinstance(n, int) or n >= 2:
                        pe.wait_ge(y0lo_done, n - 1)
                    nc.tensor.matmul(ps[:, Y0B + (par * PH + ph) % 2, :], zk[:, bass.ds(it * GV + ph * R, P)],
                                     W0K[:].rearrange("p q c -> p (q c)"), start=True, stop=True).then_inc(y0_ready, 1)

                def mix(it, par, q):
                    if q == 0:
                        pe.wait_ge(y0hi_done, it * PH + PH)
                        pe.wait_ge(y0lo_done, it * PH + PH)
                    m = it * QUART + q
                    if not isinstance(m, int) or m >= 2:
                        pe.wait_ge(z1lo_done, m - 1)
                    for ph in range(PH):
                        w = SPAN[ph][1] * V
                        o = ps[:, Z1B + q % 2, SPAN[ph][0] * V:SPAN[ph][0] * V + w]
                        hi = y0hi[0:R, par, ph, q * C:(q + 1) * C]
                        lo = y0lo[0:R, par, ph, q * C:(q + 1) * C]
                        ahi = AThi[0:R, BAND0[ph]:BAND0[ph] + w]
                        alo = ATlo[0:R, BAND0[ph]:BAND0[ph] + w]
                        nc.tensor.matmul(o, hi, ahi, start=(ph == 0), stop=False, skip_group_check=True)
                        nc.tensor.matmul(o, hi, alo, start=False, stop=False, skip_group_check=True)
                        last = nc.tensor.matmul(o, lo, ahi, start=False, stop=(ph == PH - 1), skip_group_check=True)
                    last.then_inc(z1_ready, 1)

                def layer1(it, q, first):
                    pe.wait_ge(z1hi_done, it * QUART + q + 1)
                    pe.wait_ge(z1lo_done, it * QUART + q + 1)
                    for ph in range(PH):
                        if q == 0 and not first:
                            pe.wait_ge(y1_done, it * PH + ph - PH + 1)
                        o = ps[:, Y1B + ph, q * C:(q + 1) * C]
                        hi = z1hi[:, q % 2, ph * R:ph * R + P]
                        lo = z1lo[:, q % 2, ph * R:ph * R + P]
                        nc.tensor.matmul(o, hi, W1hi[:], start=True, stop=False)
                        nc.tensor.matmul(o, hi, W1lo[:], start=False, stop=False)
                        last = nc.tensor.matmul(o, lo, W1hi[:], start=False, stop=True)
                        if q == QUART - 1:
                            last.then_inc(y1_ready, 1)

                def pool_joints(it):
                    pe.wait_ge(y1_done, it * PH + PH)
                    if not isinstance(it, int) or it >= 1:
                        pe.wait_ge(staged, it)
                    for ph in range(PH):
                        last = nc.tensor.matmul(ps[32 * ph:32 * ph + 32, PLB, :], abar[0:R, ph, :], y1[0:R, ph, :],
                                                start=True, stop=True)
                    last.then_inc(pooled_ready, 1)

                pe.wait_ge(loaded, CH * QUART * 4 * 16)
                for ph in range(PH):
                    layer0(ph, 0, 0, ph)

                def body(it, par, pair, first=False, last=False):
                    def ahead(ph):
                        if not last:
                            layer0(it * PH + PH + ph, it + 1, 1 - par, ph)
                    mix(it, par, 0)
                    ahead(0)
                    mix(it, par, 1)
                    layer1(it, 0, first)
                    ahead(1)
                    mix(it, par, 2)
                    if not first:
                        pool_joints(it - 1)
                    layer1(it, 1, first)
                    mix(it, par, 3)
                    layer1(it, 2, first)
                    ahead(2)
                    layer1(it, 3, first)
                steps(pe, body)
                pool_joints(LAST)

            @block.scalar
            def _(act):
                def y0_high(n, par, ph):
                    act.wait_ge(y0_ready, n + 1)
                    nc.scalar.activation(y0hi[0:R, par, ph, :], ps[0:R, Y0B + (par * PH + ph) % 2, :],
                                         ACT.Relu).then_inc(y0hi_done, 1)

                def z1_high(it, q):
                    act.wait_ge(z1_ready, it * QUART + q + 1)
                    nc.scalar.activation(z1hi[:, q % 2, 0:GV], ps[:, Z1B + q % 2, 0:GV],
                                         ACT.Identity).then_inc(z1hi_done, 1)

                def stage_pool(it, par, half):
                    act.wait_ge(pooled_ready, it + 1)
                    if not isinstance(half, int) or half >= 1:
                        act.wait_ge(stored[par], half * (PH * 16))
                    nc.scalar.activation(stage[:, par].rearrange("p q c -> p (q c)"), ps[0:96, PLB, :],
                                         ACT.Identity).then_inc(staged, 1)

                for ph in range(PH):
                    y0_high(ph, 0, ph)

                def body(it, par, pair, first=False, last=False):
                    def ahead(ph):
                        if not last:
                            y0_high(it * PH + PH + ph, 1 - par, ph)
                    z1_high(it, 0)
                    ahead(0)
                    z1_high(it, 1)
                    ahead(1)
                    z1_high(it, 2)
                    if not first:
                        stage_pool(it - 1, 1 - par, pair)
                    z1_high(it, 3)
                    ahead(2)
                steps(act, body)
                stage_pool(LAST, LAST % 2, LAST // 2)

            @block.vector
            def _(dve):
                nc.vector.memset(z1hi[:, :, GV:PH * P], 0.0)
                nc.vector.memset(z1lo[:, :, GV:PH * P], 0.0)

                def y0_low(n, par, ph):
                    dve.wait_ge(y0hi_done, n + 1)
                    nc.vector.scalar_tensor_tensor(y0lo[0:R, par, ph, :], ps[0:R, Y0B + (par * PH + ph) % 2, :], 0.0,
                                                   y0hi[0:R, par, ph, :], ALU.max, ALU.subtract).then_inc(y0lo_done, 1)

                def z1_low(it, q):
                    dve.wait_ge(z1hi_done, it * QUART + q + 1)
                    nc.vector.tensor_tensor(z1lo[:, q % 2, 0:GV], ps[:, Z1B + q % 2, 0:GV],
                                            z1hi[:, q % 2, 0:GV], ALU.subtract).then_inc(z1lo_done, 1)

                def relu1(it, ph):
                    dve.wait_ge(y1_ready, it * PH + ph + 1)
                    nc.vector.tensor_tensor(y1[0:R, ph, :], ps[0:R, Y1B + ph, :],
                                            negb1[0:R].rearrange("p q c -> p (q c)"), ALU.max).then_inc(y1_done, 1)

                for ph in range(PH):
                    y0_low(ph, 0, ph)

                def body(it, par, pair, first=False, last=False):
                    def ahead(ph):
                        if not last:
                            y0_low(it * PH + PH + ph, 1 - par, ph)
                    if not first:
                        relu1(it - 1, 0)
                        relu1(it - 1, 1)
                    z1_low(it, 0)
                    if not first:
                        relu1(it - 1, 2)
                    ahead(0)
                    z1_low(it, 1)
                    ahead(1)
                    z1_low(it, 2)
                    z1_low(it, 3)
                    ahead(2)
                steps(dve, body)
                for ph in range(PH):
                    relu1(LAST, ph)


def fuse(nc, ps, pooled_dram, h2_dram, txt, attn, ffn, W2s, b2row, ident, out):
    Wq, bq, Wk, bk, Wv, bv = attn
    WfT, ln_w, ln_b, bf = ffn
    v_ = nc.vector
    with ExitStack() as keep:
        def kept(name, shape, dt=F32):
            return keep.enter_context(nc.sbuf_tensor(name, shape, dt))

        wq = kept("wq", [P, P])
        wk = kept("wk", [P, P])
        wv = kept("wv", [P, P])
        bqk = kept("bqk", [P, 2])
        bvrow = kept("bvrow", [P, D])
        wf = kept("wf", [P, P + 2])
        bfrow = kept("bfrow", [P, D])
        h = kept("h", [S, B, D])

        tokens(nc, ps, pooled_dram, txt, attn, ffn, W2s, b2row, ident, wq, wk, wv, bqk, bvrow, wf, bfrow, h)
        attention(nc, ps, h2_dram, ident, wq, wk, wv, bqk, bvrow, h)
        feed_forward(nc, ps, h2_dram, ident, wf, bfrow, out)


def tokens(nc, ps, pooled_dram, txt, attn, ffn, W2s, b2row, ident, wq, wk, wv, bqk, bvrow, wf, bfrow, h):
    Wq, bq, Wk, bk, Wv, bv = attn
    WfT, ln_w, ln_b, bf = ffn
    v_ = nc.vector
    NT = FRAMES // P
    TG = 4
    BG = 8
    with ExitStack() as ctx:
        def sb(name, shape, dt=F32):
            return ctx.enter_context(nc.sbuf_tensor(name, shape, dt))

        def sem(name):
            return ctx.enter_context(nc.semaphore(name))

        parts = sb("parts", [P, PH, NT, C])
        pooledT = sb("pooledT", [P, FRAMES])
        halves = sb("halves", [P, P])
        lncol = sb("lncol", [P, 2])
        wfT = sb("wfT", [D, D])
        lbx = sb("lbx", [D, P])

        parts_loaded = [sem(f"parts_loaded{i}") for i in range(NT // TG)]
        w_clear = sem("w_clear")
        w_loaded = sem("w_loaded")
        txt_loaded = sem("txt_loaded")
        chain = sem("vector_chain2")
        summed = sem("summed")
        turned = sem("turned")
        turned_out = sem("turned_out")
        tok_ready = sem("tok_ready")
        tok_done = sem("tok_done")
        wl_ready = sem("wl_ready")
        mean_ready = sem("mean_ready")

        with nc.Block() as block:
            @block.sync
            def _(sp):
                for g in range(NT // TG):
                    for ph in range(PH):
                        src = pooled_dram[ph, g * TG * P:(g + 1) * TG * P, :].rearrange("(n p) c -> p n c", p=P)
                        sp.dma_start(parts[:, ph, g * TG:(g + 1) * TG], src).then_inc(parts_loaded[g], 16)
                sp.dma_start(h[T:S], txt.rearrange("b s d -> s b d")).then_inc(txt_loaded, 16)
                sp.wait_ge(txt_loaded, 16)

            @block.scalar
            def _(act):
                act.wait_ge(w_clear, 1)
                for w, src in ((wq, Wq), (wk, Wk), (wv, Wv), (wf, WfT)):
                    for i in range(2):
                        act.dma_start(w[D * i:D * i + D, D * i:D * i + D], src).then_inc(w_loaded, 16)
                for i in range(2):
                    for dst, src in ((bqk[:, 0:1], bq), (bqk[:, 1:2], bk), (lncol[:, 0:1], ln_w), (lncol[:, 1:2], ln_b)):
                        act.dma_start(dst[D * i:D * i + D], src.rearrange("(c one) -> c one", one=1)).then_inc(w_loaded, 16)
                act.dma_start(wfT[:], WfT).then_inc(w_loaded, 16)
                act.dma_start(bvrow[:], bv.partition_broadcast(P)).then_inc(w_loaded, 16)
                act.dma_start(bfrow[:], bf.partition_broadcast(P)).then_inc(w_loaded, 16)
                for g in range(NT // TG):
                    act.wait_ge(turned, g + 1)
                    nc.scalar.activation(pooledT[:, g * TG * P:(g + 1) * TG * P], ps[:, g % 2, :],
                                         ACT.Identity).then_inc(turned_out, 1)

            @block.vector
            def _(dve):
                done = [0]

                def link(ins):
                    done[0] += 1
                    ins.then_inc(chain, 1)
                    dve.wait_ge(chain, done[0])

                for w in (wq, wk, wv, wf, halves):
                    link(v_.memset(w[:], 0.0))
                for i in range(2):
                    link(v_.memset(halves[D * i:D * i + D, D * i:D * i + D], 1.0 / D))
                v_.tensor_copy(wf[:, P:P + 2], halves[:, 0:P:D]).then_inc(w_clear, 1)
                for g in range(NT // TG):
                    t = slice(g * TG, (g + 1) * TG)
                    dve.wait_ge(parts_loaded[g], PH * 16)
                    link(v_.tensor_tensor(parts[:, 0, t], parts[:, 0, t], parts[:, 1, t], ALU.add))
                    v_.tensor_tensor(parts[:, 0, t], parts[:, 0, t], parts[:, 2, t], ALU.add).then_inc(summed, 1)
                dve.wait_ge(w_loaded, (8 + 8 + 3) * 16)
                link(v_.tensor_scalar(wf[:, 0:P], wf[:, 0:P], lncol[:, 0:1], None, ALU.mult))
                v_.tensor_copy(lbx[:], lncol[0:D, 1:2].to_broadcast([D, P])).then_inc(wl_ready, 1)
                dve.wait_ge(mean_ready, 1)
                link(v_.tensor_tensor(wf[:, 0:P], wf[:, 0:P], ps[:, 4, 0:P], ALU.subtract))
                dve.wait_ge(mean_ready, 2)
                link(v_.tensor_tensor(bfrow[:], bfrow[:], ps[:, 5, 0:D], ALU.add))
                for g in range(B // BG):
                    dve.wait_ge(tok_ready, g + 1)
                    v_.tensor_tensor(h[0:T, g * BG:(g + 1) * BG, :],
                                     ps[0:T, 2 + g % 2, :].rearrange("p (b d) -> p b d", b=BG),
                                     b2row[0:T].rearrange("p (one d) -> p one d", one=1).to_broadcast([T, BG, D]),
                                     ALU.add).then_inc(tok_done, 1)

            @block.tensor
            def _(pe):
                for g in range(NT // TG):
                    pe.wait_ge(summed, g + 1)
                    if g >= 2:
                        pe.wait_ge(turned_out, g - 1)
                    for j in range(TG):
                        last = nc.tensor.transpose(ps[:, g % 2, j * P:(j + 1) * P], parts[:, 0, g * TG + j, :], ident[:])
                    last.then_inc(turned, 1)
                pe.wait_ge(wl_ready, 1)
                nc.tensor.matmul(ps[:, 4, 0:P], halves[:], wf[:, 0:P], start=True, stop=True).then_inc(mean_ready, 1)
                nc.tensor.matmul(ps[:, 5, 0:D], lbx[:], wfT[:], start=True, stop=True).then_inc(mean_ready, 1)
                for g in range(B // BG):
                    pe.wait_ge(turned_out, min(g * BG * T // (TG * P) + 1, NT // TG))
                    if g >= 2:
                        pe.wait_ge(tok_done, g - 1)
                    for j in range(BG):
                        b = g * BG + j
                        last = nc.tensor.matmul(ps[0:T, 2 + g % 2, j * D:(j + 1) * D], pooledT[:, b * T:(b + 1) * T],
                                                W2s[:], start=True, stop=True)
                    last.then_inc(tok_ready, 1)


def inverse_root(link, v_, root, x, out, tmp):
    link(v_.reciprocal(out, root))
    link(v_.tensor_tensor(tmp, out, out, ALU.mult))
    link(v_.tensor_tensor(tmp, tmp, x, ALU.mult))
    link(v_.tensor_scalar(tmp, tmp, -0.5, 1.5, ALU.mult, ALU.add))
    link(v_.tensor_tensor(out, out, tmp, ALU.mult))


def spread(ap, rows, n):
    return ap.rearrange("p (n one) -> p n one", one=1).to_broadcast([rows, n, D])


def attention(nc, ps, h2_dram, ident, wq, wk, wv, bqk, bvrow, h):
    v_ = nc.vector
    NG = 16
    GB = B // NG
    GP = GB // 2
    LC = 4
    LB = B // LC
    SCALE = float(D) ** -0.5
    with ExitStack() as ctx:
        def sb(name, shape, dt=F32):
            return ctx.enter_context(nc.sbuf_tensor(name, shape, dt))

        def sem(name):
            return ctx.enter_context(nc.semaphore(name))

        hc = sb("hc", [S, B, D])
        sq = sb("sq", [S, 2, LB * D])
        st = sb("st", [S, 6, B])
        hn = sb("hn", [S, GB, D])
        hT = sb("hT", [P, GP, S])
        qT = sb("qT", [P, GP, S])
        kT = sb("kT", [P, GP, S])
        val = sb("val", [S, B, D])
        dif = sb("dif", [S, GB, S])
        pr = sb("pr", [S, GB, S])
        prT = sb("prT", [S, GB, S])
        top = sb("top", [S, GB])
        den = sb("den", [S, B])
        inv = sb("inv", [S, B])
        h2 = sb("h2", [S, B, D])

        chain = sem("vector_chain3")
        centred = sem("centred")
        squared = sem("squared")
        var_ready = sem("var_ready2")
        root_ready = sem("root_ready2")
        hn_ready = sem("hn_ready")
        hT_ready = sem("hT_ready")
        hT_done = sem("hT_done")
        qk_ready = sem("qk_ready")
        val_ready = sem("val_ready")
        qk_done = sem("qk_done")
        val_done = sem("val_done")
        score_ready = sem("score_ready")
        top_done = sem("top_done")
        dif_done = sem("dif_done")
        exp_done = sem("exp_done")
        den_done = sem("den_done")
        inv_done = sem("inv_done")
        prT_ready = sem("prT_ready")
        prT_done = sem("prT_done")
        av_ready = sem("av_ready")
        av_done = sem("av_done")
        h2_done = sem("h2_done")
        stored = sem("h2_stored")

        HT, QK, VB, SC, PT, AV = 0, 1, 2, 3, 5, 6
        ORDER = [j for i in range(2) for j in range(i, GB, 2)]
        def steps(eng, body):
            for t in range(4):
                body(t, lambda lag, t=t: t - lag >= 0)
            with eng.Fori(4, NG) as t:
                body(t, lambda lag: True)
            for t in range(NG, NG + 4):
                body(t, lambda lag, t=t: t - lag < NG)

        def grp(g, n=GB):
            return bass.ds(g * n, n)

        with nc.Block() as block:
            @block.sync
            def _(sp):
                def body(g):
                    sp.wait_ge(h2_done, g + 1)
                    sp.dma_start(h2_dram.rearrange("(b s) d -> s b d", s=S)[:, grp(g)], h2[:, grp(g)]).then_inc(stored, 16)
                with sp.Fori(0, NG) as g:
                    body(g)
                sp.wait_ge(stored, NG * 16)

            @block.tensor
            def _(pe):
                def body(t, on):
                    if on(4):
                        g = t - 4
                        pe.wait_ge(prT_done, g + 1)
                        if not isinstance(g, int) or g >= 1:
                            pe.wait_ge(av_done, g)
                        for i, j in enumerate(ORDER):
                            last = nc.tensor.matmul(ps[0:S, AV, j * D:(j + 1) * D], prT[:, i, :], val[:, bass.ds(g * GB + j, 1), :].rearrange("p one d -> p (one d)"),
                                                    start=True, stop=True)
                        last.then_inc(av_ready, 1)
                    if on(3):
                        g = t - 3
                        pe.wait_ge(exp_done, g + 1)
                        if not isinstance(g, int) or g >= 1:
                            pe.wait_ge(prT_done, g)
                        for j in range(GB):
                            last = nc.tensor.transpose(ps[0:S, PT, j * S:(j + 1) * S], pr[:, j, :], ident[0:S, 0:S])
                        last.then_inc(prT_ready, 1)
                    if on(2):
                        g = t - 2
                        pe.wait_ge(qk_done, 2 * g + 2)
                        if not isinstance(g, int) or g >= 1:
                            pe.wait_ge(dif_done, g)
                        for j in ORDER:
                            half = slice(D * (j % 2), D * (j % 2) + D)
                            last = nc.tensor.matmul(ps[0:S, SC + j % 2, j // 2 * S:(j // 2 + 1) * S], qT[half, j // 2, :],
                                                    kT[half, j // 2, :], start=True, stop=True)
                        last.then_inc(score_ready, 1)
                    if on(1):
                        g = t - 1
                        pe.wait_ge(hT_done, g + 1)
                        if not isinstance(g, int) or g >= 1:
                            pe.wait_ge(qk_done, 2 * g)
                            pe.wait_ge(val_done, g)
                        for i, w in enumerate((wq, wk)):
                            last = nc.tensor.matmul(ps[:, QK, i * GP * S:(i + 1) * GP * S], w[:],
                                                    hT[:].rearrange("p g s -> p (g s)"), start=True, stop=True)
                        last.then_inc(qk_ready, 1)
                        for i in range(GP):
                            last = nc.tensor.matmul(ps[0:S, VB, i * P:(i + 1) * P], hT[:, i, :], wv[:], start=True, stop=True)
                        last.then_inc(val_ready, 1)
                    if on(0):
                        g = t
                        pe.wait_ge(hn_ready, g + 1)
                        if not isinstance(g, int) or g >= 1:
                            pe.wait_ge(hT_done, g)
                        for i in range(GP):
                            last = nc.tensor.transpose(ps[:, HT, i * S:(i + 1) * S],
                                                       hn[:, 2 * i:2 * i + 2, :].rearrange("p b d -> p (b d)"), ident[0:S, 0:S])
                        last.then_inc(hT_ready, 1)
                steps(pe, body)

            @block.scalar
            def _(act):
                for c in range(LC):
                    act.wait_ge(centred, c + 1)
                    if c >= 2:
                        act.wait_ge(var_ready, c - 1)
                    nc.scalar.activation(sq[:, c % 2, :], hc[:, c * LB:(c + 1) * LB, :].rearrange("p b d -> p (b d)"),
                                         ACT.Square).then_inc(squared, 1)
                act.wait_ge(var_ready, LC + 1)
                nc.scalar.activation(st[:, 2, :], st[:, 1, :], ACT.Sqrt).then_inc(root_ready, 1)

                def body(t, on):
                    if on(3):
                        g = t - 3
                        act.wait_ge(prT_ready, g + 1)
                        nc.scalar.activation(prT[:].rearrange("p b s -> p (b s)"), ps[0:S, PT, 0:GB * S],
                                             ACT.Identity).then_inc(prT_done, 1)
                    if on(2):
                        g = t - 2
                        act.wait_ge(dif_done, g + 1)
                        if not isinstance(g, int) or g >= 1:
                            act.wait_ge(den_done, g)
                        nc.scalar.activation(pr[:].rearrange("p b s -> p (b s)"), dif[:].rearrange("p b s -> p (b s)"),
                                             ACT.Exp, scale=SCALE).then_inc(exp_done, 1)
                    if on(1):
                        g = t - 1
                        act.wait_ge(qk_ready, g + 1)
                        for i, o in enumerate((qT, kT)):
                            nc.scalar.activation(o[:].rearrange("p g s -> p (g s)"), ps[:, QK, i * GP * S:(i + 1) * GP * S],
                                                 ACT.Identity, bias=bqk[:, i:i + 1]).then_inc(qk_done, 1)
                    if on(0):
                        g = t
                        act.wait_ge(hT_ready, g + 1)
                        nc.scalar.activation(hT[:].rearrange("p g s -> p (g s)"), ps[:, HT, 0:GP * S],
                                             ACT.Identity).then_inc(hT_done, 1)
                steps(act, body)

            @block.vector
            def _(dve):
                done = [0]

                def link(ins):
                    done[0] += 1
                    ins.then_inc(chain, 1)
                    dve.wait_ge(chain, done[0])

                for c in range(LC):
                    b = slice(c * LB, (c + 1) * LB)
                    link(v_.tensor_reduce(st[:, 0, b], h[:, b, :], AX_X, ALU.add))
                    link(v_.tensor_scalar(st[:, 0, b], st[:, 0, b], 1.0 / D, None, ALU.mult))
                    v_.tensor_tensor(hc[:, b, :], h[:, b, :], spread(st[:, 0, b], S, LB), ALU.subtract).then_inc(centred, 1)
                for c in range(LC):
                    b = slice(c * LB, (c + 1) * LB)
                    dve.wait_ge(squared, c + 1)
                    v_.tensor_reduce(st[:, 5, b], sq[:, c % 2, :].rearrange("p (b d) -> p b d", d=D), AX_X,
                                     ALU.add).then_inc(var_ready, 1)
                dve.wait_ge(var_ready, LC)
                v_.tensor_scalar(st[:, 1, :], st[:, 5, :], 1.0 / D, EPS, ALU.mult, ALU.add).then_inc(var_ready, 1)
                dve.wait_ge(root_ready, 1)
                inverse_root(link, v_, st[:, 2, :], st[:, 1, :], st[:, 3, :], st[:, 4, :])

                def normalise(g):
                    if not isinstance(g, int) or g >= 1:
                        dve.wait_ge(hT_ready, g)
                    v_.tensor_tensor(hn[:], hc[:, grp(g), :], spread(st[:, 3, grp(g)], S, GB),
                                     ALU.mult).then_inc(hn_ready, 1)

                normalise(0)

                def body(t, on):
                    if on(4):
                        g = t - 4
                        dve.wait_ge(av_ready, g + 1)
                        dve.wait_ge(inv_done, g + 1)
                        v_.tensor_tensor(h2[:, grp(g), :], ps[0:S, AV, 0:GB * D].rearrange("p (b d) -> p b d", d=D),
                                         spread(inv[:, grp(g)], S, GB), ALU.mult).then_inc(av_done, 1)
                    if on(2):
                        g = t - 2
                        scores = ps[0:S, SC:SC + 2, 0:GP * S].rearrange("p i (j s) -> p i j s", s=S)
                        dve.wait_ge(score_ready, g + 1)
                        v_.tensor_reduce(top[:].rearrange("p (i j) -> p i j", i=2), scores, AX_X, ALU.max).then_inc(top_done, 1)
                    if on(4):
                        g = t - 4
                        dve.wait_ge(av_done, g + 1)
                        v_.tensor_tensor(h2[:, grp(g), :], h2[:, grp(g), :], h[:, grp(g), :], ALU.add).then_inc(h2_done, 1)
                    if on(2):
                        g = t - 2
                        dve.wait_ge(top_done, g + 1)
                        if not isinstance(g, int) or g >= 1:
                            dve.wait_ge(exp_done, g)
                        v_.tensor_tensor(dif[:].rearrange("p (i j) s -> p i j s", i=2), scores,
                                         top[:].rearrange("p (i j one) -> p i j one", i=2, one=1).to_broadcast([S, 2, GP, S]),
                                         ALU.subtract).then_inc(dif_done, 1)
                    if on(1):
                        g = t - 1
                        dve.wait_ge(val_ready, g + 1)
                        v_.tensor_tensor(val[:, grp(g), :], ps[0:S, VB, 0:GB * D].rearrange("p (b d) -> p b d", d=D),
                                         bvrow[0:S].rearrange("p (one d) -> p one d", one=1).to_broadcast([S, GB, D]),
                                         ALU.add).then_inc(val_done, 1)
                    if on(-1):
                        normalise(t + 1)
                    if on(2):
                        g = t - 2
                        dve.wait_ge(exp_done, g + 1)
                        v_.tensor_reduce(den[:, grp(g)].rearrange("p (j i) -> p i j", i=2), pr[:].rearrange("p (i j) s -> p i j s", i=2),
                                         AX_X, ALU.add).then_inc(den_done, 1)
                        dve.wait_ge(den_done, g + 1)
                        v_.reciprocal(inv[:, grp(g)], den[:, grp(g)]).then_inc(inv_done, 1)

                for t in range(4):
                    body(t, lambda lag, t=t: t - lag >= 0)
                with dve.Fori(4, NG - 1) as t:
                    body(t, lambda lag: True)
                for t in range(NG - 1, NG + 4):
                    body(t, lambda lag, t=t: t - lag < NG)


def feed_forward(nc, ps, h2_dram, ident, wf, bfrow, out):
    v_ = nc.vector
    ROWS = B * S // P
    CH = 4
    CR = ROWS // CH
    CP = CR // 2
    HP = CP // 2
    W = CR * D
    PW = P + 2
    N = ITERS * CH
    with ExitStack() as ctx:
        def sb(name, shape, dt=F32):
            return ctx.enter_context(nc.sbuf_tensor(name, shape, dt))

        def sem(name):
            return ctx.enter_context(nc.semaphore(name))

        h2 = sb("h2r", [P, CH, W])
        x = sb("x", [P, CH, W])
        xs = sb("x_scaled", [P, 2, W])
        th = sb("th", [P, 2, W])
        y = sb("y", [P, 2, W])
        sg = sb("sg", [P, 2, W])
        g_ = sb("g", [P, 2, CP, P])
        gT = sb("gT", [P, 2, CP, P])
        gsq = sb("gsq", [P, 2, CP, P])
        mom = sb("mom", [P, 2, 2, CR])
        var = sb("var", [P, 2, 2, CR])
        rs = sb("rs", [P, 2, CR])
        st = sb("st2", [P, 6, ROWS])
        expo = sb("expo", [P, CR])

        chain = sem("vector_chain4")
        loaded = sem("h2_loaded")
        centred = sem("centred2")
        squared = sem("squared2")
        var_ready = sem("var_ready3")
        root_ready = sem("root_ready3")
        expo_made = sem("expo_made")
        x_ready = sem("x_ready")
        th_done = sem("th_done")
        y_done = sem("y_done")
        sg_done = sem("sg_done")
        g_done = sem("g_done")
        gT_ready = sem("gT_ready")
        gT_done = sem("gT_done")
        gsq_done = sem("gsq_done")
        prod_ready = sem("prod_ready")
        mom_done = sem("mom_done")
        pool_chain = sem("pool_chain")
        rs_done = sem("rs_done")
        scaled = sem("scaled")
        out_done = sem("out_done")
        stored = sem("out_stored")

        def steps(eng, body):
            for s in range(CH):
                body(s, s, lambda lag, s=s: s - lag >= 0)
            with eng.Fori(1, ITERS) as it:
                for c in range(CH):
                    body(it * CH + c, c, lambda lag: True)
            for s in range(N, N + 3):
                body(s, s % CH, lambda lag, s=s: s - lag < N)

        rows = h2_dram.rearrange("(p n) d -> p (n d)", p=P)
        out_rows = out.rearrange("b s d -> (b s d)").rearrange("(p n) -> p n", p=P)

        with nc.Block() as block:
            @block.sync
            def _(sp):
                sp.dma_start(h2[:].rearrange("p c w -> p (c w)"), rows).then_inc(loaded, 16)
                for c in range(CH):
                    sp.wait_ge(out_done, c + 1)
                    sp.dma_start(out_rows[:, c * W:(c + 1) * W], h2[:, c, :]).then_inc(stored, 16)
                sp.wait_ge(stored, CH * 16)

            @block.gpsimd
            def _(pool):
                pool.memset(expo[:], -0.25).then_inc(expo_made, 1)
                pool.wait_ge(expo_made, 1)

                def body(s, c, on):
                    if on(2):
                        n, b = s - 2, (c - 2) % 2
                        pool.wait_ge(mom_done, 2 * n + 2)
                        if not isinstance(n, int) or n >= 2:
                            pool.wait_ge(scaled, 2 * n - 2)
                        nc.gpsimd.tensor_tensor(var[:, b, 0, :], mom[:, b, 0, :], mom[:, b, 0, :], ALU.mult).then_inc(pool_chain, 1)
                        pool.wait_ge(pool_chain, 3 * n + 1)
                        nc.gpsimd.tensor_tensor(var[:, b, 1, :], mom[:, b, 1, :], var[:, b, 0, :], ALU.subtract).then_inc(pool_chain, 1)
                        pool.wait_ge(pool_chain, 3 * n + 2)
                        nc.gpsimd.tensor_tensor(var[:, b, 0, :], var[:, b, 1, :], var[:, b, 1, :], ALU.mult).then_inc(pool_chain, 1)
                        pool.wait_ge(pool_chain, 3 * n + 3)
                        nc.gpsimd.tensor_tensor(rs[:, b, :], var[:, b, 0, :], expo[:], ALU.pow).then_inc(rs_done, 1)
                steps(pool, body)

            @block.scalar
            def _(act):
                for c in range(CH):
                    act.wait_ge(centred, c + 1)
                    nc.scalar.activation(y[:, c % 2, :], x[:, c, :], ACT.Square).then_inc(squared, 1)
                    if c >= 1:
                        act.wait_ge(var_ready, c)
                act.wait_ge(var_ready, CH + 1)
                nc.scalar.activation(st[:, 2, :], st[:, 1, :], ACT.Sqrt).then_inc(root_ready, 1)

                def body(s, c, on):
                    b = c % 2
                    if on(0):
                        act.wait_ge(x_ready, s + 1)
                        nc.scalar.activation(th[:, b, :], x[:, c, :], ACT.Tanh).then_inc(th_done, 1)
                    if on(1):
                        n, b1 = s - 1, (c - 1) % 2
                        act.wait_ge(gT_ready, n + 1)
                        if not isinstance(n, int) or n >= 2:
                            act.wait_ge(prod_ready, n - 1)
                        src = ps[:, 2 * b1:2 * b1 + 2, 0:HP * P].rearrange("p k w -> p k w")
                        nc.scalar.activation(gT[:, b1].rearrange("p (k j) r -> p k (j r)", k=2), src, ACT.Identity).then_inc(gT_done, 1)
                        nc.scalar.activation(gsq[:, b1].rearrange("p (k j) r -> p k (j r)", k=2), src, ACT.Square).then_inc(gsq_done, 1)
                    if on(0):
                        act.wait_ge(y_done, s + 1)
                        if not isinstance(s, int) or s >= 2:
                            act.wait_ge(g_done, s - 1)
                        nc.scalar.activation(sg[:, b, :], y[:, b, :], ACT.Sigmoid).then_inc(sg_done, 1)
                steps(act, body)

            @block.tensor
            def _(pe):
                def body(s, c, on):
                    if on(1):
                        n, b = s - 1, (c - 1) % 2
                        pe.wait_ge(g_done, n + 1)
                        if not isinstance(n, int) or n >= 2:
                            pe.wait_ge(gsq_done, n - 1)
                        for j in range(CP):
                            last = nc.tensor.transpose(ps[:, 2 * b + j // HP, (j % HP) * P:(j % HP) * P + P],
                                                       g_[:, b, j, :], ident[:])
                        last.then_inc(gT_ready, 1)
                        pe.wait_ge(gT_done, n + 1)
                        if not isinstance(n, int) or n >= 2:
                            pe.wait_ge(scaled, 2 * n - 2)
                            pe.wait_ge(mom_done, 2 * n - 2)
                        for j in range(CP):
                            nc.tensor.matmul(ps[:, 4 + 2 * b + j // HP, (j % HP) * PW:(j % HP) * PW + PW], gT[:, b, j, :],
                                             wf[:], start=True, stop=True)
                        pe.wait_ge(gsq_done, n + 1)
                        for j in range(CP):
                            at = HP * PW + (j % HP) * 2
                            last = nc.tensor.matmul(ps[:, 4 + 2 * b + j // HP, at:at + 2], gsq[:, b, j, :],
                                                    wf[:, P:P + 2], start=True, stop=True)
                        last.then_inc(prod_ready, 1)
                steps(pe, body)

            @block.vector
            def _(dve):
                done = [0]

                def link(ins):
                    done[0] += 1
                    ins.then_inc(chain, 1)
                    dve.wait_ge(chain, done[0])

                dve.wait_ge(loaded, 16)
                for c in range(CH):
                    r = slice(c * CR, (c + 1) * CR)
                    hv = h2[:, c, :].rearrange("p (r d) -> p r d", d=D)
                    link(v_.tensor_reduce(st[:, 0, r], hv, AX_X, ALU.add))
                    link(v_.tensor_scalar(st[:, 0, r], st[:, 0, r], 1.0 / D, None, ALU.mult))
                    v_.tensor_tensor(x[:, c, :].rearrange("p (r d) -> p r d", d=D), hv, spread(st[:, 0, r], P, CR),
                                     ALU.subtract).then_inc(centred, 1)
                    dve.wait_ge(squared, c + 1)
                    v_.tensor_reduce(st[:, 5, r], y[:, c % 2, :].rearrange("p (r d) -> p r d", d=D), AX_X,
                                     ALU.add).then_inc(var_ready, 1)
                dve.wait_ge(var_ready, CH)
                v_.tensor_scalar(st[:, 1, :], st[:, 5, :], 1.0 / D, EPS, ALU.mult, ALU.add).then_inc(var_ready, 1)
                dve.wait_ge(root_ready, 1)
                inverse_root(link, v_, st[:, 2, :], st[:, 1, :], st[:, 3, :], st[:, 4, :])
                for c in range(CH):
                    r = slice(c * CR, (c + 1) * CR)
                    xv = x[:, c, :].rearrange("p (r d) -> p r d", d=D)
                    v_.tensor_tensor(xv, xv, spread(st[:, 3, r], P, CR), ALU.mult).then_inc(x_ready, 1)

                def body(s, c, on):
                    b = c % 2
                    if on(2):
                        n, b2 = s - 2, (c - 2) % 2
                        dve.wait_ge(prod_ready, n + 1)
                        if not isinstance(n, int) or n >= 2:
                            dve.wait_ge(rs_done, n - 1)
                        prod = ps[:, 4 + 2 * b2:6 + 2 * b2, :]
                        v_.tensor_copy(mom[:, b2, 0, :].rearrange("p (k j i) -> p k j i", k=2, j=HP),
                                       prod[:, :, 0:HP * PW].rearrange("p k (j w) -> p k j w", w=PW)[:, :, :, P:PW]).then_inc(mom_done, 1)
                        v_.tensor_scalar(mom[:, b2, 1, :].rearrange("p (k i) -> p k i", k=2),
                                         prod[:, :, HP * PW:HP * PW + 2 * HP], EPS, None, ALU.add).then_inc(mom_done, 1)
                    if on(3):
                        n, b3 = s - 3, (c - 3) % 2
                        dve.wait_ge(rs_done, n + 1)
                        for k in range(2):
                            v_.tensor_tensor(
                                xs[:, b3, k * HP * P:(k + 1) * HP * P].rearrange("p (j i d) -> p j i d", i=2, d=D),
                                ps[:, 4 + 2 * b3 + k, 0:HP * PW].rearrange("p (j w) -> p j w", w=PW)[:, :, 0:P].rearrange("p j (i d) -> p j i d", d=D),
                                rs[:, b3, k * 2 * HP:(k + 1) * 2 * HP].rearrange("p (j i one) -> p j i one", i=2, one=1).to_broadcast([P, HP, 2, D]),
                                ALU.mult).then_inc(scaled, 1)
                    if on(0):
                        dve.wait_ge(th_done, s + 1)
                        v_.scalar_tensor_tensor(y[:, b, :], th[:, b, :], 0.01, x[:, c, :], ALU.mult, ALU.add).then_inc(y_done, 1)
                    if on(3):
                        dve.wait_ge(scaled, 2 * (s - 3) + 2)
                        v_.tensor_tensor(x[:, (c - 3) % CH, :].rearrange("p (r d) -> p r d", d=D),
                                         xs[:, b3, :].rearrange("p (r d) -> p r d", d=D),
                                         bfrow[:].rearrange("p (one d) -> p one d", one=1).to_broadcast([P, CR, D]),
                                         ALU.add).then_inc(x_ready, 1)
                    if on(0):
                        dve.wait_ge(sg_done, s + 1)
                        if not isinstance(s, int) or s >= 2:
                            dve.wait_ge(gT_ready, s - 1)
                        v_.tensor_tensor(g_[:, b].rearrange("p j r -> p (j r)"), y[:, b, :], sg[:, b, :],
                                         ALU.mult).then_inc(g_done, 1)
                steps(dve, body)
                for c in range(CH):
                    dve.wait_ge(x_ready, N + CH)
                    v_.tensor_tensor(h2[:, c, :], h2[:, c, :], x[:, c, :], ALU.add).then_inc(out_done, 1)


TOK = ["b", "g", "be", "m", "v"]


def kernel(**inputs):
    import concourse.bacc as _bacc
    from concourse.bass_utils import run_bass_kernel_spmd as _run

    a = {k: np.asarray(v) for k, v in inputs.items()}
    frames = a["x"].reshape(FRAMES, V, CIN)[np.minimum(np.arange(QUART * QF), FRAMES - 1)]
    x_v = frames.reshape(QUART, ZS, ZF, V, CIN).transpose(3, 0, 1, 4, 2).reshape(V, QUART, ZS, CIN * ZF)
    arrays = {
        "x_v": x_v,
        "txt": a["txt"],
        "AT": a["L0_tok_A"].T,
        "A": a["L0_tok_A"],
        "W0T": a["L0_tok_W0"].T,
        "W1": a["L0_tok_W1"],
        "W2": a["L0_tok_W2"],
    }
    for layer in range(3):
        for p in TOK:
            arrays[f"{p}{layer}"] = a[f"L0_tok_{p}{layer}"]
    for k in ("Wq", "bq", "Wk", "bk", "Wv", "bv"):
        arrays[k] = a[f"L0_attn_{k}"]
    arrays["WfT"] = a["L0_ffn_W"].T
    for k in ("ln_w", "ln_b", "b"):
        arrays[f"f_{k}"] = a[f"L0_ffn_{k}"]
    arrays = {k: np.ascontiguousarray(v) for k, v in arrays.items()}

    nc = _bacc.Bacc("TRN2", target_bir_lowering=False, num_devices=1)
    ap = {k: nc.dram_tensor(f"in_{k}", v.shape, mybir.dt.from_np(v.dtype), kind="ExternalInput").ap()
          for k, v in arrays.items()}
    out = nc.dram_tensor("out_0", (B, S, D), F32, kind="ExternalOutput").ap()
    build(nc, ap["x_v"], ap["txt"], ap["AT"], ap["A"], ap["W0T"], ap["W1"], ap["W2"],
          *[[ap[f"{p}{layer}"] for p in TOK] for layer in range(3)],
          [ap[k] for k in ("Wq", "bq", "Wk", "bk", "Wv", "bv")],
          [ap[k] for k in ("WfT", "f_ln_w", "f_ln_b", "f_b")], out)
    r = _run(nc, [{f"in_{k}": v for k, v in arrays.items()}], core_ids=[0])
    return r.results[0]["out_0"]
```

```python
from contextlib import ExitStack

import numpy as np

import concourse.bass as bass
from concourse import mybir

F32 = mybir.dt.float32
F16 = mybir.dt.float16
BF16 = mybir.dt.bfloat16
I32 = mybir.dt.int32
ALU = mybir.AluOpType
ACT = mybir.ActivationFunctionType
AX_X = mybir.AxisListType.X
RMAX = bass.bass_isa.ReduceOp.max

P = 128
B, T, V, CIN = 64, 64, 75, 3
FRAMES = B * T
C = 128
D = 64
TXT = 32
S = T + TXT
EPS = 1e-5
QUART = 4
GF = 5
PH = 3
R = GF * V // PH
GV = GF * V
GROUPS = 205
QF = GROUPS * GF
QROWS = QF * V
ZF = 41
ZS = QF // ZF
ZB = 5
ZCOLS = ZB * ZF * V
ZPAD = P - R
ITERS = 30
SPAN = [(0, 2), (1, 3), (3, 2)]
BAND0 = [0, 2 * V, 5 * V]
BANDW = 7 * V


def band_pieces():
    out = []
    for ph in range(PH):
        r = 0
        while r < R:
            flat = ph * R + r
            f, v = divmod(flat, V)
            n = min(V - v, R - r)
            out.append((ph, f, r, v, n))
            r += n
    return out


def build(nc, x_v, txt, AT, A, W0T, W1, W2, par0, par1, par2, attn, ffn, out):
    zs = nc.dram_tensor("z_parts", [2, CIN, QUART * QROWS], F16, kind="Internal").ap()
    h2_dram = nc.dram_tensor("h2_rows", [B * S, D], F32, kind="Internal").ap()
    pooled_dram = nc.dram_tensor("pooled_parts", [PH, QUART * QF, C], F32, kind="Internal").ap()
    ctx = ExitStack()

    def sb(name, shape, dt=F32):
        return ctx.enter_context(nc.sbuf_tensor(name, shape, dt))

    def sem(name):
        return ctx.enter_context(nc.semaphore(name))

    with ctx:
        ps = ctx.enter_context(nc.psum_tensor("ps", [P, 8, 512], F32))
        AThi = sb("AThi", [P, BANDW], F16)
        ATlo = sb("ATlo", [P, BANDW], F16)
        abar = sb("abar", [P, PH, 32])
        W0K = sb("W0K", [P, QUART, C], F16)
        W1hi = sb("W1hi", [P, C], F16)
        W1lo = sb("W1lo", [P, C], F16)
        negb1 = sb("negb1", [P, PH, C])
        W2s = sb("W2s", [P, D])
        b2row = sb("b2row", [P, D])
        ident = sb("ident", [P, P])
        sz = sb("sz", [P, 1])

        setup(nc, ps, x_v, AT, A, W0T, W1, W2, par0, par1, par2, zs,
              AThi, ATlo, abar, W0K, W1hi, W1lo, negb1, W2s, b2row, ident, sz)
        tokenise(nc, ps, zs, pooled_dram, AThi, ATlo, abar, W0K, W1hi, W1lo, negb1)
        fuse(nc, ps, pooled_dram, h2_dram, txt, attn, ffn, W2s, b2row, ident, out)


def setup(nc, ps, x_v, AT, A, W0T, W1, W2, par0, par1, par2, zs,
          AThi, ATlo, abar, W0K, W1hi, W1lo, negb1, W2s, b2row, ident, sz):
    with ExitStack() as ctx:
        def sb(name, shape, dt=F32):
            return ctx.enter_context(nc.sbuf_tensor(name, shape, dt))

        def sem(name):
            return ctx.enter_context(nc.semaphore(name))

        xs = sb("xs", [V, QUART, ZS, CIN * ZF])
        at = sb("at", [V, V])
        a_rows = sb("a_rows", [V, V])
        band = sb("band", [P, BANDW])
        bandc = sb("bandc", [P, 7])
        w0 = sb("w0", [P, CIN])
        w1 = sb("w1", [P, C])
        w2 = sb("w2", [P, D])
        cols = sb("cols", [P, 2, 5])
        row1 = sb("row1", [P, 5, C])
        row2 = sb("row2", [P, 5, D])
        rc = sb("rc", [P, 4, 2])
        r1 = sb("r1", [P, 4, C])
        r2 = sb("r2", [P, 4, D])
        bc = sb("bc", [P, 2])
        b1r = sb("b1r", [P, C])
        b2r = sb("b2r", [P, D])
        mx = sb("mx", [P, 8])
        mxa = sb("mxa", [P, 8])
        sc = sb("sc", [P, 16])
        stack = sb("stack", [P, P])
        part = sb("part", [P, 2, CIN], F16)
        bpart = sb("bpart", [P, 3], F16)
        ones = sb("ones", [P, P])
        acol = sb("acol", [V, 2])
        cvec = sb("cvec", [P, P])
        zhi = sb("zhi", [P, 2, ZB * V], F16)
        zlo = sb("zlo", [P, 2, ZB * V], F16)

        loaded = sem("params_loaded")
        x_loaded = sem("x_loaded")
        band_clear = sem("band_clear")
        band_loaded = sem("band_loaded")
        chain = sem("vector_chain")
        id_made = sem("ident_made")
        var_ready = sem("var_ready")
        root_ready = sem("root_ready")
        max_ready = sem("max_ready")
        max_all = sem("max_all")
        stack_ready = sem("stack_ready")
        stack_t = sem("stack_transposed")
        cvec_ready = sem("cvec_ready")
        const_ready = sem("const_ready")
        abar_ready = sem("abar_ready")
        asum_ready = sem("asum_ready")
        sz_ready = sem("sz_ready")
        z_ready = sem("z_product_ready")
        zhi_done = sem("z_hi_done")
        zlo_done = sem("z_lo_done")
        z_stored = [sem(f"z_stored{i}") for i in range(2)]

        pieces = band_pieces()
        NPAR = 5 + 4 * 5
        ZN = QUART * (ZS // ZB)

        with nc.Block() as block:
            @block.sync
            def _(sp):
                for q in range(QUART):
                    sp.dma_start(xs[:, q], x_v[:, q]).then_inc(x_loaded, 16)
                sp.wait_ge(band_clear, 1)
                for ph, f, r, v, n in pieces:
                    c0 = BAND0[ph] + (f - SPAN[ph][0]) * V
                    sp.dma_start(band[r:r + n, c0:c0 + V], AT[v:v + n, :]).then_inc(band_loaded, 16)
                for n in range(ZN):
                    k, q = divmod(n, QUART)
                    sp.wait_ge(zhi_done, n + 1)
                    sp.wait_ge(zlo_done, n + 1)
                    for w, src in ((0, zhi), (1, zlo)):
                        for c in range(CIN):
                            base = q * QROWS + k * ZCOLS
                            dst = zs[w, c, base:base + ZCOLS].rearrange("(s f u) -> f s u", s=ZB, f=ZF)
                            s_ = src[c * ZF:(c + 1) * ZF, n % 2, :].rearrange("p (s u) -> p s u", s=ZB)
                            sp.dma_start(dst, s_).then_inc(z_stored[n % 2], 16)
                for slot in z_stored:
                    sp.wait_ge(slot, ZN // 2 * 2 * CIN * 16)

            @block.scalar
            def _(act):
                act.dma_start(at[:], AT).then_inc(loaded, 16)
                act.dma_start(a_rows[:], A).then_inc(loaded, 16)
                act.dma_start(w0[:], W0T).then_inc(loaded, 16)
                act.dma_start(w1[:], W1).then_inc(loaded, 16)
                act.dma_start(w2[:], W2).then_inc(loaded, 16)
                for i, p_ in enumerate(par0):
                    act.dma_start(cols[:, 0, i:i + 1], p_.rearrange("(c one) -> c one", one=1)).then_inc(loaded, 16)
                for i, p_ in enumerate(par1):
                    act.dma_start(cols[:, 1, i:i + 1], p_.rearrange("(c one) -> c one", one=1)).then_inc(loaded, 16)
                for i, p_ in enumerate(par1):
                    act.dma_start(row1[:, i, :], p_.partition_broadcast(P)).then_inc(loaded, 16)
                for i, p_ in enumerate(par2):
                    act.dma_start(row2[:, i, :], p_.partition_broadcast(P)).then_inc(loaded, 16)
                act.wait_ge(var_ready, 3)
                nc.scalar.activation(rc[:, 1, :], rc[:, 0, :], ACT.Sqrt).then_inc(root_ready, 1)
                nc.scalar.activation(r1[:, 1, :], r1[:, 0, :], ACT.Sqrt).then_inc(root_ready, 1)
                nc.scalar.activation(r2[:, 1, :], r2[:, 0, :], ACT.Sqrt).then_inc(root_ready, 1)
                act.wait_ge(sz_ready, 1)
                for n in range(ZN):
                    act.wait_ge(z_ready, n + 1)
                    if n >= 2:
                        act.wait_ge(z_stored[n % 2], n // 2 * 2 * CIN * 16)
                    nc.scalar.activation(zhi[0:CIN * ZF, n % 2, :], ps[0:CIN * ZF, n % 2, 0:ZB * V], ACT.Identity,
                                         scale=sz[0:CIN * ZF, :]).then_inc(zhi_done, 1)

            @block.gpsimd
            def _(pool):
                pool.memset(ident[:], 0.0).then_inc(id_made, 1)
                pool.wait_ge(id_made, 1)
                pool.affine_select(out=ident[:], in_=ident[:], compare_op=ALU.not_equal, fill=1.0, base=0,
                                   pattern=[[-1, P]], channel_multiplier=1).then_inc(id_made, 1)
                pool.wait_ge(max_ready, 1)
                pool.partition_all_reduce(mxa[:], mx[:], P, RMAX).then_inc(max_all, 1)

            @block.vector
            def _(dve):
                done = [0]

                def link(ins):
                    done[0] += 1
                    ins.then_inc(chain, 1)
                    dve.wait_ge(chain, done[0])

                v_ = nc.vector
                v_.memset(band[:], 0.0).then_inc(band_clear, 1)
                link(v_.memset(mx[:], 0.0))
                link(v_.memset(ones[:], 1.0))
                link(v_.memset(stack[:], 0.0))
                link(v_.memset(abar[:], 0.0))
                link(v_.memset(W0K[:], 0.0))
                dve.wait_ge(loaded, NPAR * 16)
                v_.tensor_scalar(rc[:, 0, :], cols[:, :, 4], EPS, None, ALU.add).then_inc(var_ready, 1)
                v_.tensor_scalar(r1[:, 0, :], row1[:, 4, :], EPS, None, ALU.add).then_inc(var_ready, 1)
                v_.tensor_scalar(r2[:, 0, :], row2[:, 4, :], EPS, None, ALU.add).then_inc(var_ready, 1)
                dve.wait_ge(root_ready, 3)
                for r, g, b, be, m, bias in ((rc, cols[:, :, 1], cols[:, :, 0], cols[:, :, 2], cols[:, :, 3], bc[:]),
                                             (r1, row1[:, 1, :], row1[:, 0, :], row1[:, 2, :], row1[:, 3, :], b1r[:]),
                                             (r2, row2[:, 1, :], row2[:, 0, :], row2[:, 2, :], row2[:, 3, :], b2r[:])):
                    link(v_.reciprocal(r[:, 2, :], r[:, 1, :]))
                    link(v_.tensor_tensor(r[:, 3, :], r[:, 2, :], r[:, 2, :], ALU.mult))
                    link(v_.tensor_tensor(r[:, 3, :], r[:, 3, :], r[:, 0, :], ALU.mult))
                    link(v_.tensor_scalar(r[:, 3, :], r[:, 3, :], -0.5, 1.5, ALU.mult, ALU.add))
                    link(v_.tensor_tensor(r[:, 2, :], r[:, 2, :], r[:, 3, :], ALU.mult))
                    link(v_.tensor_tensor(r[:, 2, :], r[:, 2, :], g, ALU.mult))
                    link(v_.tensor_tensor(r[:, 3, :], b, m, ALU.subtract))
                    link(v_.tensor_tensor(r[:, 3, :], r[:, 3, :], r[:, 2, :], ALU.mult))
                    link(v_.tensor_tensor(bias, r[:, 3, :], be, ALU.add))
                link(v_.tensor_scalar(w0[:], w0[:], rc[:, 2, 0:1], None, ALU.mult))
                link(v_.tensor_tensor(w1[:], w1[:], r1[:, 2, :], ALU.mult))
                link(v_.tensor_tensor(w2[:], w2[:], r2[:, 2, :], ALU.mult))
                link(v_.tensor_reduce(mx[0:V, 0:1], a_rows[:], AX_X, ALU.add, apply_absolute_value=True))
                dve.wait_ge(x_loaded, QUART * 16)
                link(v_.tensor_reduce(mx[0:V, 1:2], xs[:].rearrange("p q s f -> p (q s f)"), AX_X, ALU.max,
                                      apply_absolute_value=True))
                link(v_.tensor_reduce(mx[:, 2:3], w0[:], AX_X, ALU.add, apply_absolute_value=True))
                link(v_.tensor_reduce(mx[:, 3:4], bc[:, 0:1], AX_X, ALU.max, apply_absolute_value=True))
                v_.tensor_reduce(mx[:, 4:5], w1[:], AX_X, ALU.max, apply_absolute_value=True).then_inc(max_ready, 1)
                dve.wait_ge(max_all, 1)
                link(v_.tensor_copy(sc[:, 0:1], mxa[:, 0:1]))
                link(v_.tensor_tensor(sc[:, 1:2], mxa[:, 1:2], mxa[:, 0:1], ALU.mult))
                link(v_.scalar_tensor_tensor(sc[:, 2:3], sc[:, 1:2], mxa[:, 2:3], mxa[:, 3:4], ALU.mult, ALU.add))
                link(v_.tensor_copy(sc[:, 3:4], mxa[:, 4:5]))
                link(v_.tensor_scalar(sc[:, 0:4], sc[:, 0:4], 1e-30, None, ALU.max))
                link(v_.reciprocal(sc[:, 8:12], sc[:, 0:4]))
                link(v_.tensor_scalar(sc[:, 4:8].bitcast(I32), sc[:, 8:12].bitcast(I32), 0x7F800000, None,
                                      ALU.bitwise_and))
                link(v_.tensor_scalar(sc[:, 4:5], sc[:, 4:5], 2.0 ** 7, None, ALU.mult))
                link(v_.tensor_scalar(sc[:, 5:7], sc[:, 5:7], 2.0 ** 8, None, ALU.mult))
                link(v_.tensor_scalar(sc[:, 7:8], sc[:, 7:8], 2.0 ** 4, None, ALU.mult))
                v_.tensor_copy(sz[:], sc[:, 5:6]).then_inc(sz_ready, 1)
                link(v_.reciprocal(sc[:, 12:13], sc[:, 5:6]))
                link(v_.tensor_tensor(sc[:, 12:13], sc[:, 12:13], sc[:, 6:7], ALU.mult))
                link(v_.tensor_tensor(sc[:, 13:14], sc[:, 4:5], sc[:, 6:7], ALU.mult))
                link(v_.tensor_tensor(sc[:, 13:14], sc[:, 13:14], sc[:, 7:8], ALU.mult))
                link(v_.reciprocal(sc[:, 14:15], sc[:, 13:14]))

                def z_low(n):
                    dve.wait_ge(zhi_done, n + 1)
                    v_.scalar_tensor_tensor(zlo[0:CIN * ZF, n % 2, :], ps[0:CIN * ZF, n % 2, 0:ZB * V],
                                            sz[0:CIN * ZF, :], zhi[0:CIN * ZF, n % 2, :],
                                            ALU.mult, ALU.subtract).then_inc(zlo_done, 1)
                for n in range(ZN):
                    if n >= 2:
                        dve.wait_ge(z_stored[n % 2], n // 2 * 2 * CIN * 16)
                    z_low(n)

                dve.wait_ge(band_loaded, len(pieces) * 16)
                link(v_.tensor_reduce(bandc[:], band[:].rearrange("p (f u) -> p f u", u=V), AX_X, ALU.add))
                at_col = 0
                for ph in range(PH):
                    f0, n = SPAN[ph]
                    link(v_.tensor_scalar(abar[:, ph, f0:f0 + n], bandc[:, at_col:at_col + n], 1.0 / V, None, ALU.mult))
                    at_col += n
                link(v_.tensor_scalar(band[:], band[:], sc[:, 4:5], None, ALU.mult))
                link(v_.tensor_copy(AThi[:], band[:]))
                link(v_.tensor_tensor(ATlo[:], band[:], AThi[:], ALU.subtract))
                link(v_.tensor_scalar(w1[:], w1[:], sc[:, 7:8], None, ALU.mult))
                link(v_.tensor_copy(W1hi[:], w1[:]))
                link(v_.tensor_tensor(W1lo[:], w1[:], W1hi[:], ALU.subtract))
                for ph in range(PH):
                    link(v_.tensor_scalar(negb1[:, ph, :], b1r[:], sc[:, 13:14], -1.0, ALU.mult, ALU.mult))
                link(v_.tensor_scalar(w0[:], w0[:], sc[:, 12:13], None, ALU.mult))
                link(v_.tensor_copy(part[:, 0, :], w0[:]))
                link(v_.tensor_tensor(part[:, 1, :], w0[:], part[:, 0, :], ALU.subtract))
                link(v_.tensor_tensor(bc[:, 0:1], bc[:, 0:1], sc[:, 6:7], ALU.mult))
                for i in range(3):
                    link(v_.tensor_copy(bpart[:, i:i + 1], bc[:, 0:1]))
                    link(v_.tensor_tensor(bc[:, 0:1], bc[:, 0:1], bpart[:, i:i + 1], ALU.subtract))
                for q in range(QUART):
                    for i, w in enumerate((0, 0, 1, 1)):
                        link(v_.tensor_copy(stack[:, 32 * q + 3 * i:32 * q + 3 * i + 3], part[:, w, :]))
                    link(v_.tensor_copy(stack[:, 32 * q + 12:32 * q + 15], bpart[:]))
                link(v_.tensor_reduce(acol[:, 0:1], at[:], AX_X, ALU.add))
                v_.tensor_scalar(acol[:, 1:2], acol[:, 0:1], 1.0 / V, None, ALU.mult).then_inc(abar_ready, 1)
                dve.wait_ge(asum_ready, 1)
                link(v_.tensor_copy(sc[:, 15:16], ps[:, 4, 0:1]))
                link(v_.tensor_tensor(sc[:, 15:16], sc[:, 15:16], bc[:, 1:2], ALU.mult))
                v_.tensor_copy(cvec[:], sc[:, 15:16].to_broadcast([P, P])).then_inc(cvec_ready, 1)
                v_.tensor_copy(stack[:, 15:16], stack[:, 15:16]).then_inc(stack_ready, 1)
                dve.wait_ge(stack_t, 1)
                for q in range(QUART):
                    link(v_.tensor_copy(W0K[32 * q:32 * q + 32, q, :], ps[32 * q:32 * q + 32, 5, 0:C]))
                dve.wait_ge(const_ready, 1)
                link(v_.tensor_tensor(b2row[:], ps[:, 6, 0:D], b2r[:], ALU.add))
                link(v_.tensor_scalar(W2s[:], w2[:], sc[:, 14:15], None, ALU.mult))

            @block.tensor
            def _(pe):
                pe.wait_ge(loaded, NPAR * 16)
                pe.wait_ge(x_loaded, QUART * 16)
                for n in range(ZN):
                    k, q = divmod(n, QUART)
                    if n >= 2:
                        pe.wait_ge(zlo_done, n - 1)
                    for s in range(ZB):
                        last = nc.tensor.matmul(ps[0:CIN * ZF, n % 2, s * V:(s + 1) * V],
                                                xs[:, q, k * ZB + s, :], at[:], start=True, stop=True)
                    last.then_inc(z_ready, 1)
                pe.wait_ge(abar_ready, 1)
                nc.tensor.matmul(ps[:, 4, 0:1], ones[0:V, :], acol[:, 1:2], start=True, stop=True).then_inc(asum_ready, 1)
                pe.wait_ge(cvec_ready, 1)
                nc.tensor.matmul(ps[:, 6, 0:D], cvec[:], w2[:], start=True, stop=True).then_inc(const_ready, 1)
                pe.wait_ge(stack_ready, 1)
                pe.wait_ge(id_made, 2)
                nc.tensor.transpose(ps[:, 5, 0:C], stack[:], ident[:]).then_inc(stack_t, 1)


def tokenise(nc, ps, zs, pooled_dram, AThi, ATlo, abar, W0K, W1hi, W1lo, negb1):
    with ExitStack() as ctx:
        def sb(name, shape, dt=F32):
            return ctx.enter_context(nc.sbuf_tensor(name, shape, dt))

        def sem(name):
            return ctx.enter_context(nc.semaphore(name))

        zk = sb("zk", [P, QROWS + ZPAD + 1], F16)
        y0hi = sb("y0hi", [P, 2, PH, QUART * C], F16)
        y0lo = sb("y0lo", [P, 2, PH, QUART * C], F16)
        z1hi = sb("z1hi", [P, QUART, PH * P], F16)
        z1lo = sb("z1lo", [P, QUART, PH * P], F16)
        y1 = sb("y1", [P, 2, QUART, PH * C])
        stage = sb("stage", [96, 2, QUART, C])

        filled = sem("ones_filled")
        loaded = sem("z_loaded")
        y0_ready = sem("y0_ready")
        y0hi_done = sem("y0hi_done")
        y0lo_done = sem("y0lo_done")
        z1_ready = sem("z1_ready")
        z1hi_done = sem("z1hi_done")
        z1lo_done = sem("z1lo_done")
        y1_ready = sem("y1_ready")
        y1_done = sem("y1_done")
        pooled_ready = sem("pooled_ready")
        staged = sem("staged")
        stored = [sem(f"pooled_stored{i}") for i in range(2)]

        Y0B, Z1B, Y1B, PLB = 0, 3, 5, 7
        LAST = GROUPS - 1
        CH = 5
        CW = (QROWS // CH + 1) // 2 * 2

        def steps(eng, body):
            for it in range(3):
                body(it, it % 2, (it - 1) // 2)
            with eng.Fori(1, LAST // 2 - 1) as k:
                body(k * 2 + 1, 1, k)
                body(k * 2 + 2, 0, k)
            body(LAST - 1, 1, LAST // 2 - 1)
            body(LAST, 0, LAST // 2 - 1, last=True)

        def late(n, k):
            return not isinstance(n, int) or n >= k

        with nc.Block() as block:
            @block.gpsimd
            def _(pool):
                for k in range(CH):
                    hi_ = QROWS + ZPAD + 1 if k == CH - 1 else (k + 1) * CW
                    pool.memset(zk[:, k * CW:hi_], 1.0).then_inc(filled, 1)

            @block.sync
            def _(sp):
                for k in range(CH):
                    sp.wait_ge(filled, k + 1)
                    for q in range(QUART):
                        for rep in range(2):
                            for w in range(2):
                                r0 = 32 * q + 6 * rep + 3 * w
                                end = min((k + 1) * CW, QROWS)
                                sp.dma_start(zk[r0:r0 + 3, k * CW:end],
                                             zs[w, :, q * QROWS + k * CW:q * QROWS + end]).then_inc(loaded, 16)

                def body(it, par, pair, last=False):
                    sp.wait_ge(staged, it + 1)
                    for ph in range(PH):
                        dst = pooled_dram[ph].rearrange("(q f) c -> f q c", q=QUART)[bass.ds(it * GF, GF)]
                        sp.dma_start(dst, stage[32 * ph:32 * ph + GF, par]).then_inc(stored[par], 16)
                steps(sp, body)
                for par in range(2):
                    sp.wait_ge(stored[par], (GROUPS + 1 - par) // 2 * PH * 16)

            @block.tensor
            def _(pe):
                def layer0(it, ph):
                    n = it * PH + ph
                    if late(n, PH):
                        pe.wait_ge(y0lo_done, n - PH + 1)
                    nc.tensor.matmul(ps[:, Y0B + ph, :], zk[:, bass.ds(it * GV + ph * R, P)],
                                     W0K[:].rearrange("p q c -> p (q c)"), start=True, stop=True).then_inc(y0_ready, 1)

                def mix(it, par, q):
                    if q == 0:
                        pe.wait_ge(y0hi_done, it * PH + PH)
                        pe.wait_ge(y0lo_done, it * PH + PH)
                    m = it * QUART + q
                    if late(m, 2):
                        pe.wait_ge(z1lo_done, m - 1)
                    for ph in range(PH):
                        w = SPAN[ph][1] * V
                        o = ps[:, Z1B + q % 2, SPAN[ph][0] * V:SPAN[ph][0] * V + w]
                        hi = y0hi[0:R, par, ph, q * C:(q + 1) * C]
                        lo = y0lo[0:R, par, ph, q * C:(q + 1) * C]
                        ahi = AThi[0:R, BAND0[ph]:BAND0[ph] + w]
                        alo = ATlo[0:R, BAND0[ph]:BAND0[ph] + w]
                        nc.tensor.matmul(o, hi, ahi, start=(ph == 0), stop=False, skip_group_check=True)
                        nc.tensor.matmul(o, hi, alo, start=False, stop=False, skip_group_check=True)
                        last = nc.tensor.matmul(o, lo, ahi, start=False, stop=(ph == PH - 1), skip_group_check=True)
                    last.then_inc(z1_ready, 1)

                def layer1(it, q):
                    m = it * QUART + q
                    pe.wait_ge(z1lo_done, m + 1)
                    if late(m, 2):
                        pe.wait_ge(y1_done, m - 1)
                    for ph in range(PH):
                        o = ps[:, Y1B + q % 2, ph * C:(ph + 1) * C]
                        hi = z1hi[:, q, ph * R:ph * R + P]
                        lo = z1lo[:, q, ph * R:ph * R + P]
                        nc.tensor.matmul(o, hi, W1hi[:], start=True, stop=False)
                        nc.tensor.matmul(o, hi, W1lo[:], start=False, stop=False)
                        last = nc.tensor.matmul(o, lo, W1hi[:], start=False, stop=True)
                    last.then_inc(y1_ready, 1)

                def pool_joints(it, par):
                    pe.wait_ge(y1_done, it * QUART + QUART)
                    if late(it, 1):
                        pe.wait_ge(staged, it)
                    for ph in range(PH):
                        last = nc.tensor.matmul(ps[32 * ph:32 * ph + 32, PLB, :].rearrange("p (q c) -> p q c", q=QUART),
                                                abar[0:R, ph, :], y1[0:R, par, :, ph * C:(ph + 1) * C],
                                                start=True, stop=True)
                    last.then_inc(pooled_ready, 1)

                pe.wait_ge(loaded, CH * QUART * 4 * 16)
                for ph in range(PH):
                    layer0(0, ph)

                def body(it, par, pair, last=False):
                    for q in range(QUART):
                        mix(it, par, q)
                        if q < PH and not last:
                            layer0(it + 1, q)
                        if q == QUART - 1 and late(it, 1):
                            pool_joints(it - 1, 1 - par)
                        if q >= 2:
                            layer1(it, q - 2)
                        elif late(it, 1):
                            layer1(it - 1, q + 2)
                steps(pe, body)
                layer1(LAST, 2)
                layer1(LAST, 3)
                pool_joints(LAST, 0)

            @block.scalar
            def _(act):
                def y0_high(it, par, ph):
                    act.wait_ge(y0_ready, it * PH + ph + 1)
                    nc.scalar.activation(y0hi[0:R, par, ph, :], ps[0:R, Y0B + ph, :], ACT.Relu).then_inc(y0hi_done, 1)

                def z1_high(it, q):
                    act.wait_ge(z1_ready, it * QUART + q + 1)
                    nc.scalar.activation(z1hi[:, q, 0:GV], ps[:, Z1B + q % 2, 0:GV],
                                         ACT.Identity).then_inc(z1hi_done, 1)

                def stage_pool(it, par, half):
                    act.wait_ge(pooled_ready, it + 1)
                    if late(half, 1):
                        act.wait_ge(stored[par], half * (PH * 16))
                    nc.scalar.activation(stage[:, par].rearrange("p q c -> p (q c)"), ps[0:96, PLB, :],
                                         ACT.Identity).then_inc(staged, 1)

                for ph in range(PH):
                    y0_high(0, 0, ph)

                def body(it, par, pair, last=False):
                    for q in range(QUART):
                        z1_high(it, q)
                        if q < PH and not last:
                            y0_high(it + 1, 1 - par, q)
                    if late(it, 1):
                        stage_pool(it - 1, 1 - par, pair)
                steps(act, body)
                stage_pool(LAST, 0, LAST // 2)

            @block.vector
            def _(dve):
                nc.vector.memset(z1hi[:, :, GV:PH * P], 0.0)
                nc.vector.memset(z1lo[:, :, GV:PH * P], 0.0)

                def y0_low(it, par, ph):
                    dve.wait_ge(y0hi_done, it * PH + ph + 1)
                    nc.vector.scalar_tensor_tensor(y0lo[0:R, par, ph, :], ps[0:R, Y0B + ph, :], 0.0,
                                                   y0hi[0:R, par, ph, :], ALU.max, ALU.subtract).then_inc(y0lo_done, 1)

                def z1_low(it, q):
                    dve.wait_ge(z1hi_done, it * QUART + q + 1)
                    nc.vector.tensor_tensor(z1lo[:, q, 0:GV], ps[:, Z1B + q % 2, 0:GV],
                                            z1hi[:, q, 0:GV], ALU.subtract).then_inc(z1lo_done, 1)

                def relu1(it, par, q):
                    dve.wait_ge(y1_ready, it * QUART + q + 1)
                    nc.vector.tensor_tensor(y1[0:R, par, q, :], ps[0:R, Y1B + q % 2, 0:PH * C],
                                            negb1[0:R].rearrange("p f c -> p (f c)"), ALU.max).then_inc(y1_done, 1)

                for ph in range(PH):
                    y0_low(0, 0, ph)

                def body(it, par, pair, last=False):
                    for q in range(QUART):
                        if q == QUART - 1:
                            relu1(it, par, 0)
                        elif late(it, 1):
                            relu1(it - 1, 1 - par, q + 1)
                        z1_low(it, q)
                        if q < PH and not last:
                            y0_low(it + 1, 1 - par, q)
                steps(dve, body)
                for q in range(1, QUART):
                    relu1(LAST, 0, q)


def fuse(nc, ps, pooled_dram, h2_dram, txt, attn, ffn, W2s, b2row, ident, out):
    Wq, bq, Wk, bk, Wv, bv = attn
    WfT, ln_w, ln_b, bf = ffn
    v_ = nc.vector
    with ExitStack() as keep:
        def kept(name, shape, dt=F32):
            return keep.enter_context(nc.sbuf_tensor(name, shape, dt))

        wq = kept("wq", [P, P])
        wk = kept("wk", [P, P])
        wv = kept("wv", [P, P])
        bqk = kept("bqk", [P, 2])
        bvrow = kept("bvrow", [P, D])
        wf = kept("wf", [P, P])
        bfrow = kept("bfrow", [P, D])
        h = kept("h", [S, B, D])

        tokens(nc, ps, pooled_dram, txt, attn, ffn, W2s, b2row, ident, wq, wk, wv, bqk, bvrow, wf, bfrow, h)
        attention(nc, ps, h2_dram, ident, wq, wk, wv, bqk, bvrow, h)
        feed_forward(nc, ps, h2_dram, ident, wf, bfrow, out)


def tokens(nc, ps, pooled_dram, txt, attn, ffn, W2s, b2row, ident, wq, wk, wv, bqk, bvrow, wf, bfrow, h):
    Wq, bq, Wk, bk, Wv, bv = attn
    WfT, ln_w, ln_b, bf = ffn
    v_ = nc.vector
    NT = FRAMES // P
    TG = 4
    BG = 8
    with ExitStack() as ctx:
        def sb(name, shape, dt=F32):
            return ctx.enter_context(nc.sbuf_tensor(name, shape, dt))

        def sem(name):
            return ctx.enter_context(nc.semaphore(name))

        parts = sb("parts", [P, PH, NT, C])
        pooledT = sb("pooledT", [P, FRAMES])
        halves = sb("halves", [P, P])
        lncol = sb("lncol", [P, 2])
        wfT = sb("wfT", [D, D])
        lbx = sb("lbx", [D, P])

        parts_loaded = [sem(f"parts_loaded{i}") for i in range(NT // TG)]
        w_clear = sem("w_clear")
        w_loaded = sem("w_loaded")
        txt_loaded = sem("txt_loaded")
        chain = sem("vector_chain2")
        summed = sem("summed")
        turned = sem("turned")
        turned_out = sem("turned_out")
        tok_ready = sem("tok_ready")
        tok_done = sem("tok_done")
        wl_ready = sem("wl_ready")
        mean_ready = sem("mean_ready")

        with nc.Block() as block:
            @block.sync
            def _(sp):
                for g in range(NT // TG):
                    for ph in range(PH):
                        src = pooled_dram[ph, g * TG * P:(g + 1) * TG * P, :].rearrange("(n p) c -> p n c", p=P)
                        sp.dma_start(parts[:, ph, g * TG:(g + 1) * TG], src).then_inc(parts_loaded[g], 16)
                sp.dma_start(h[T:S], txt.rearrange("b s d -> s b d")).then_inc(txt_loaded, 16)
                sp.wait_ge(txt_loaded, 16)

            @block.scalar
            def _(act):
                act.wait_ge(w_clear, 1)
                for w, src in ((wq, Wq), (wk, Wk), (wv, Wv), (wf, WfT)):
                    for i in range(2):
                        act.dma_start(w[D * i:D * i + D, D * i:D * i + D], src).then_inc(w_loaded, 16)
                for i in range(2):
                    for dst, src in ((bqk[:, 0:1], bq), (bqk[:, 1:2], bk), (lncol[:, 0:1], ln_w), (lncol[:, 1:2], ln_b)):
                        act.dma_start(dst[D * i:D * i + D], src.rearrange("(c one) -> c one", one=1)).then_inc(w_loaded, 16)
                act.dma_start(wfT[:], WfT).then_inc(w_loaded, 16)
                act.dma_start(bvrow[:], bv.partition_broadcast(P)).then_inc(w_loaded, 16)
                act.dma_start(bfrow[:], bf.partition_broadcast(P)).then_inc(w_loaded, 16)
                for g in range(NT // TG):
                    act.wait_ge(turned, g + 1)
                    nc.scalar.activation(pooledT[:, g * TG * P:(g + 1) * TG * P], ps[:, g % 2, :],
                                         ACT.Identity).then_inc(turned_out, 1)

            @block.vector
            def _(dve):
                done = [0]

                def link(ins):
                    done[0] += 1
                    ins.then_inc(chain, 1)
                    dve.wait_ge(chain, done[0])

                for w in (wq, wk, wv, wf, halves):
                    link(v_.memset(w[:], 0.0))
                for i in range(2):
                    link(v_.memset(halves[D * i:D * i + D, D * i:D * i + D], 1.0 / D))
                v_.memset(lbx[:], 0.0).then_inc(w_clear, 1)
                for g in range(NT // TG):
                    t = slice(g * TG, (g + 1) * TG)
                    dve.wait_ge(parts_loaded[g], PH * 16)
                    link(v_.tensor_tensor(parts[:, 0, t], parts[:, 0, t], parts[:, 1, t], ALU.add))
                    v_.tensor_tensor(parts[:, 0, t], parts[:, 0, t], parts[:, 2, t], ALU.add).then_inc(summed, 1)
                dve.wait_ge(w_loaded, (8 + 8 + 3) * 16)
                link(v_.tensor_scalar(wf[:], wf[:], lncol[:, 0:1], D ** 0.5, ALU.mult, ALU.mult))
                v_.tensor_copy(lbx[:], lncol[0:D, 1:2].to_broadcast([D, P])).then_inc(wl_ready, 1)
                dve.wait_ge(mean_ready, 1)
                link(v_.tensor_tensor(wf[:], wf[:], ps[:, 4, 0:P], ALU.subtract))
                dve.wait_ge(mean_ready, 2)
                link(v_.tensor_tensor(bfrow[:], bfrow[:], ps[:, 5, 0:D], ALU.add))
                for g in range(B // BG):
                    dve.wait_ge(tok_ready, g + 1)
                    v_.tensor_tensor(h[0:T, g * BG:(g + 1) * BG, :],
                                     ps[0:T, 2 + g % 2, :].rearrange("p (b d) -> p b d", b=BG),
                                     b2row[0:T].rearrange("p (one d) -> p one d", one=1).to_broadcast([T, BG, D]),
                                     ALU.add).then_inc(tok_done, 1)

            @block.tensor
            def _(pe):
                for g in range(NT // TG):
                    pe.wait_ge(summed, g + 1)
                    if g >= 2:
                        pe.wait_ge(turned_out, g - 1)
                    for j in range(TG):
                        last = nc.tensor.transpose(ps[:, g % 2, j * P:(j + 1) * P], parts[:, 0, g * TG + j, :], ident[:])
                    last.then_inc(turned, 1)
                pe.wait_ge(wl_ready, 1)
                nc.tensor.matmul(ps[:, 4, 0:P], halves[:], wf[:], start=True, stop=True).then_inc(mean_ready, 1)
                nc.tensor.matmul(ps[:, 5, 0:D], lbx[:], wfT[:], start=True, stop=True).then_inc(mean_ready, 1)
                for g in range(B // BG):
                    pe.wait_ge(turned_out, min(g * BG * T // (TG * P) + 1, NT // TG))
                    if g >= 2:
                        pe.wait_ge(tok_done, g - 1)
                    for j in range(BG):
                        b = g * BG + j
                        last = nc.tensor.matmul(ps[0:T, 2 + g % 2, j * D:(j + 1) * D], pooledT[:, b * T:(b + 1) * T],
                                                W2s[:], start=True, stop=True)
                    last.then_inc(tok_ready, 1)


def inverse_root(link, v_, root, x, out, tmp):
    link(v_.reciprocal(out, root))
    link(v_.tensor_tensor(tmp, out, out, ALU.mult))
    link(v_.tensor_tensor(tmp, tmp, x, ALU.mult))
    link(v_.tensor_scalar(tmp, tmp, -0.5, 1.5, ALU.mult, ALU.add))
    link(v_.tensor_tensor(out, out, tmp, ALU.mult))


def spread(ap, rows, n):
    return ap.rearrange("p (n one) -> p n one", one=1).to_broadcast([rows, n, D])


def attention(nc, ps, h2_dram, ident, wq, wk, wv, bqk, bvrow, h):
    v_ = nc.vector
    NG = 16
    GB = B // NG
    GP = GB // 2
    LC = 4
    LB = B // LC
    SCALE = float(D) ** -0.5
    with ExitStack() as ctx:
        def sb(name, shape, dt=F32):
            return ctx.enter_context(nc.sbuf_tensor(name, shape, dt))

        def sem(name):
            return ctx.enter_context(nc.semaphore(name))

        hc = sb("hc", [S, B, D])
        sq = sb("sq", [S, 2, LB * D])
        st = sb("st", [S, 6, B])
        hn = sb("hn", [S, GB, D])
        hT = sb("hT", [P, GP, S])
        qT = sb("qT", [P, GP, S])
        kT = sb("kT", [P, GP, S])
        val = sb("val", [S, B, D])
        dif = sb("dif", [S, GB, S])
        pr = sb("pr", [S, GB, S])
        prT = sb("prT", [S, GB, S])
        top = sb("top", [S, GB])
        den = sb("den", [S, B])
        inv = sb("inv", [S, B])
        h2 = sb("h2", [S, B, D])

        chain = sem("vector_chain3")
        centred = sem("centred")
        squared = sem("squared")
        var_ready = sem("var_ready2")
        root_ready = sem("root_ready2")
        hn_ready = sem("hn_ready")
        hT_ready = sem("hT_ready")
        hT_done = sem("hT_done")
        qk_ready = sem("qk_ready")
        val_ready = sem("val_ready")
        qk_done = sem("qk_done")
        val_done = sem("val_done")
        score_ready = sem("score_ready")
        top_done = sem("top_done")
        dif_done = sem("dif_done")
        exp_done = sem("exp_done")
        den_done = sem("den_done")
        inv_done = sem("inv_done")
        prT_ready = sem("prT_ready")
        prT_done = sem("prT_done")
        av_ready = sem("av_ready")
        av_done = sem("av_done")
        h2_done = sem("h2_done")
        stored = sem("h2_stored")

        HT, QK, VB, SC, PT, AV = 0, 1, 2, 3, 5, 6
        ORDER = [j for i in range(2) for j in range(i, GB, 2)]
        def steps(eng, body):
            for t in range(4):
                body(t, lambda lag, t=t: t - lag >= 0)
            with eng.Fori(4, NG) as t:
                body(t, lambda lag: True)
            for t in range(NG, NG + 4):
                body(t, lambda lag, t=t: t - lag < NG)

        def grp(g, n=GB):
            return bass.ds(g * n, n)

        with nc.Block() as block:
            @block.sync
            def _(sp):
                def body(g):
                    sp.wait_ge(h2_done, g + 1)
                    sp.dma_start(h2_dram.rearrange("(b s) d -> s b d", s=S)[:, grp(g)], h2[:, grp(g)]).then_inc(stored, 16)
                with sp.Fori(0, NG) as g:
                    body(g)
                sp.wait_ge(stored, NG * 16)

            @block.tensor
            def _(pe):
                def body(t, on):
                    if on(4):
                        g = t - 4
                        pe.wait_ge(prT_done, g + 1)
                        if not isinstance(g, int) or g >= 1:
                            pe.wait_ge(av_done, g)
                        for i, j in enumerate(ORDER):
                            last = nc.tensor.matmul(ps[0:S, AV, j * D:(j + 1) * D], prT[:, i, :], val[:, bass.ds(g * GB + j, 1), :].rearrange("p one d -> p (one d)"),
                                                    start=True, stop=True)
                        last.then_inc(av_ready, 1)
                    if on(3):
                        g = t - 3
                        pe.wait_ge(exp_done, g + 1)
                        if not isinstance(g, int) or g >= 1:
                            pe.wait_ge(prT_done, g)
                        for j in range(GB):
                            last = nc.tensor.transpose(ps[0:S, PT, j * S:(j + 1) * S], pr[:, j, :], ident[0:S, 0:S])
                        last.then_inc(prT_ready, 1)
                    if on(2):
                        g = t - 2
                        pe.wait_ge(qk_done, 2 * g + 2)
                        if not isinstance(g, int) or g >= 1:
                            pe.wait_ge(dif_done, g)
                        for j in ORDER:
                            half = slice(D * (j % 2), D * (j % 2) + D)
                            last = nc.tensor.matmul(ps[0:S, SC + j % 2, j // 2 * S:(j // 2 + 1) * S], qT[half, j // 2, :],
                                                    kT[half, j // 2, :], start=True, stop=True)
                        last.then_inc(score_ready, 1)
                    if on(1):
                        g = t - 1
                        pe.wait_ge(hT_done, g + 1)
                        if not isinstance(g, int) or g >= 1:
                            pe.wait_ge(qk_done, 2 * g)
                            pe.wait_ge(val_done, g)
                        for i, w in enumerate((wq, wk)):
                            last = nc.tensor.matmul(ps[:, QK, i * GP * S:(i + 1) * GP * S], w[:],
                                                    hT[:].rearrange("p g s -> p (g s)"), start=True, stop=True)
                        last.then_inc(qk_ready, 1)
                        for i in range(GP):
                            last = nc.tensor.matmul(ps[0:S, VB, i * P:(i + 1) * P], hT[:, i, :], wv[:], start=True, stop=True)
                        last.then_inc(val_ready, 1)
                    if on(0):
                        g = t
                        pe.wait_ge(hn_ready, g + 1)
                        if not isinstance(g, int) or g >= 1:
                            pe.wait_ge(hT_done, g)
                        for i in range(GP):
                            last = nc.tensor.transpose(ps[:, HT, i * S:(i + 1) * S],
                                                       hn[:, 2 * i:2 * i + 2, :].rearrange("p b d -> p (b d)"), ident[0:S, 0:S])
                        last.then_inc(hT_ready, 1)
                steps(pe, body)

            @block.scalar
            def _(act):
                for c in range(LC):
                    act.wait_ge(centred, c + 1)
                    if c >= 2:
                        act.wait_ge(var_ready, c - 1)
                    nc.scalar.activation(sq[:, c % 2, :], hc[:, c * LB:(c + 1) * LB, :].rearrange("p b d -> p (b d)"),
                                         ACT.Square).then_inc(squared, 1)
                act.wait_ge(var_ready, LC + 1)
                nc.scalar.activation(st[:, 2, :], st[:, 1, :], ACT.Sqrt).then_inc(root_ready, 1)

                def body(t, on):
                    if on(3):
                        g = t - 3
                        act.wait_ge(prT_ready, g + 1)
                        nc.scalar.activation(prT[:].rearrange("p b s -> p (b s)"), ps[0:S, PT, 0:GB * S],
                                             ACT.Identity).then_inc(prT_done, 1)
                    if on(2):
                        g = t - 2
                        act.wait_ge(dif_done, g + 1)
                        if not isinstance(g, int) or g >= 1:
                            act.wait_ge(den_done, g)
                        nc.scalar.activation(pr[:].rearrange("p b s -> p (b s)"), dif[:].rearrange("p b s -> p (b s)"),
                                             ACT.Exp, scale=SCALE).then_inc(exp_done, 1)
                    if on(1):
                        g = t - 1
                        act.wait_ge(qk_ready, g + 1)
                        for i, o in enumerate((qT, kT)):
                            nc.scalar.activation(o[:].rearrange("p g s -> p (g s)"), ps[:, QK, i * GP * S:(i + 1) * GP * S],
                                                 ACT.Identity, bias=bqk[:, i:i + 1]).then_inc(qk_done, 1)
                    if on(0):
                        g = t
                        act.wait_ge(hT_ready, g + 1)
                        nc.scalar.activation(hT[:].rearrange("p g s -> p (g s)"), ps[:, HT, 0:GP * S],
                                             ACT.Identity).then_inc(hT_done, 1)
                steps(act, body)

            @block.vector
            def _(dve):
                done = [0]

                def link(ins):
                    done[0] += 1
                    ins.then_inc(chain, 1)
                    dve.wait_ge(chain, done[0])

                for c in range(LC):
                    b = slice(c * LB, (c + 1) * LB)
                    link(v_.tensor_reduce(st[:, 0, b], h[:, b, :], AX_X, ALU.add))
                    link(v_.tensor_scalar(st[:, 0, b], st[:, 0, b], 1.0 / D, None, ALU.mult))
                    v_.tensor_tensor(hc[:, b, :], h[:, b, :], spread(st[:, 0, b], S, LB), ALU.subtract).then_inc(centred, 1)
                for c in range(LC):
                    b = slice(c * LB, (c + 1) * LB)
                    dve.wait_ge(squared, c + 1)
                    v_.tensor_reduce(st[:, 5, b], sq[:, c % 2, :].rearrange("p (b d) -> p b d", d=D), AX_X,
                                     ALU.add).then_inc(var_ready, 1)
                dve.wait_ge(var_ready, LC)
                v_.tensor_scalar(st[:, 1, :], st[:, 5, :], 1.0 / D, EPS, ALU.mult, ALU.add).then_inc(var_ready, 1)
                dve.wait_ge(root_ready, 1)
                inverse_root(link, v_, st[:, 2, :], st[:, 1, :], st[:, 3, :], st[:, 4, :])

                def normalise(g):
                    if not isinstance(g, int) or g >= 1:
                        dve.wait_ge(hT_ready, g)
                    v_.tensor_tensor(hn[:], hc[:, grp(g), :], spread(st[:, 3, grp(g)], S, GB),
                                     ALU.mult).then_inc(hn_ready, 1)

                normalise(0)

                def body(t, on):
                    if on(4):
                        g = t - 4
                        dve.wait_ge(av_ready, g + 1)
                        dve.wait_ge(inv_done, g + 1)
                        v_.tensor_tensor(h2[:, grp(g), :], ps[0:S, AV, 0:GB * D].rearrange("p (b d) -> p b d", d=D),
                                         spread(inv[:, grp(g)], S, GB), ALU.mult).then_inc(av_done, 1)
                    if on(2):
                        g = t - 2
                        scores = ps[0:S, SC:SC + 2, 0:GP * S].rearrange("p i (j s) -> p i j s", s=S)
                        dve.wait_ge(score_ready, g + 1)
                        v_.tensor_reduce(top[:].rearrange("p (i j) -> p i j", i=2), scores, AX_X, ALU.max).then_inc(top_done, 1)
                    if on(4):
                        g = t - 4
                        dve.wait_ge(av_done, g + 1)
                        v_.tensor_tensor(h2[:, grp(g), :], h2[:, grp(g), :], h[:, grp(g), :], ALU.add).then_inc(h2_done, 1)
                    if on(2):
                        g = t - 2
                        dve.wait_ge(top_done, g + 1)
                        if not isinstance(g, int) or g >= 1:
                            dve.wait_ge(exp_done, g)
                        v_.tensor_tensor(dif[:].rearrange("p (i j) s -> p i j s", i=2), scores,
                                         top[:].rearrange("p (i j one) -> p i j one", i=2, one=1).to_broadcast([S, 2, GP, S]),
                                         ALU.subtract).then_inc(dif_done, 1)
                    if on(1):
                        g = t - 1
                        dve.wait_ge(val_ready, g + 1)
                        v_.tensor_tensor(val[:, grp(g), :], ps[0:S, VB, 0:GB * D].rearrange("p (b d) -> p b d", d=D),
                                         bvrow[0:S].rearrange("p (one d) -> p one d", one=1).to_broadcast([S, GB, D]),
                                         ALU.add).then_inc(val_done, 1)
                    if on(-1):
                        normalise(t + 1)
                    if on(2):
                        g = t - 2
                        dve.wait_ge(exp_done, g + 1)
                        v_.tensor_reduce(den[:, grp(g)].rearrange("p (j i) -> p i j", i=2), pr[:].rearrange("p (i j) s -> p i j s", i=2),
                                         AX_X, ALU.add).then_inc(den_done, 1)
                        dve.wait_ge(den_done, g + 1)
                        v_.reciprocal(inv[:, grp(g)], den[:, grp(g)]).then_inc(inv_done, 1)

                for t in range(4):
                    body(t, lambda lag, t=t: t - lag >= 0)
                with dve.Fori(4, NG - 1) as t:
                    body(t, lambda lag: True)
                for t in range(NG - 1, NG + 4):
                    body(t, lambda lag, t=t: t - lag < NG)


def feed_forward(nc, ps, h2_dram, ident, wf, bfrow, out):
    v_ = nc.vector
    ROWS = B * S // P
    CH = 6
    CR = ROWS // CH
    CP = CR // 2
    W = CR * D
    TB = CH
    NG = 6
    N = ITERS * CH
    LAG = 5
    with ExitStack() as ctx:
        def sb(name, shape, dt=F32):
            return ctx.enter_context(nc.sbuf_tensor(name, shape, dt))

        def sem(name):
            return ctx.enter_context(nc.semaphore(name))

        h2 = sb("h2r", [P, CH, W])
        x0 = sb("x0", [P, CH, W])
        sq = sb("x0_squared", [P, 2, W])
        th = sb("th", [P, 2, W])
        g_ = sb("g", [P, NG, CR, D])
        gn = sb("gn", [P, 2, CP, P])
        gT = sb("gT", [P, 2, CP * P])
        bs = sb("bn_parts", [P, 2, CR, 6])
        dm = sb("dm", [P, 2, CR])
        s2 = sb("s2", [P, 2, CR])
        q2 = sb("q2", [P, 2, CR])
        var = sb("var64", [P, 2, CR])
        rs = sb("rs", [P, 2, CR])
        st = sb("st2", [P, 6, ROWS])
        expo = sb("expo", [P, CR])
        pct = sb("pct", [P, P])
        ones = sb("ones_b", [P, P], BF16)
        brow = sb("brow", [P, W], BF16)
        bres = sb("bres", [P, 2, D])
        bpart = sb("bias_part", [P, D], BF16)

        chain = sem("vector_chain4")
        loaded = sem("h2_loaded")
        centred = sem("centred2")
        squared = sem("squared2")
        var_ready = sem("var_ready3")
        root_ready = sem("root_ready3")
        expo_made = sem("expo_made")
        x0_ready = sem("x0_ready")
        weights_ready = sem("bias_parts_ready")
        x_ready = sem("x_ready")
        th_done = sem("th_done")
        y_ready = sem("y_ready")
        g_done = sem("g_done")
        bn_done = sem("bn_done")
        diff_done = sem("diff_done")
        parts_done = sem("parts_done")
        var_done = sem("var_done")
        rs_done = sem("rs_done")
        gn_done = sem("gn_done")
        gT_ready = sem("gT_ready")
        gT_done = sem("gT_done")
        out_done = sem("out_done")
        stored = sem("out_stored")

        def steps(eng, body):
            for s in range(CH):
                body(s, s, lambda lag, s=s: s - lag >= 0)
            with eng.Fori(1, ITERS) as it:
                for c in range(CH):
                    body(it * CH + c, c, lambda lag: True)
            for s in range(N, N + LAG):
                body(s, s - N, lambda lag, s=s: 0 <= s - lag < N)

        def late(n, k):
            return not isinstance(n, int) or n >= k

        rows = h2_dram.rearrange("(p n) d -> p (n d)", p=P)
        out_rows = out.rearrange("b s d -> (b s d)").rearrange("(p n) -> p n", p=P)

        with nc.Block() as block:
            @block.sync
            def _(sp):
                sp.dma_start(h2[:].rearrange("p c w -> p (c w)"), rows).then_inc(loaded, 16)
                for c in range(CH):
                    sp.wait_ge(out_done, c + 1)
                    sp.dma_start(out_rows[:, c * W:(c + 1) * W], h2[:, c, :]).then_inc(stored, 16)
                sp.wait_ge(stored, CH * 16)

            @block.gpsimd
            def _(pool):
                pool.memset(ones[:], 1.0)
                pool.memset(expo[:], -0.5).then_inc(expo_made, 1)
                pool.wait_ge(expo_made, 1)

                def body(s, c, on):
                    if on(2):
                        n, b = s - 2, c % 2
                        pool.wait_ge(parts_done, 2 * n + 2)
                        if late(n, 2):
                            pool.wait_ge(gn_done, n - 1)
                        nc.gpsimd.tensor_tensor(var[:, b, :], s2[:, b, :], q2[:, b, :], ALU.add).then_inc(var_done, 1)
                        pool.wait_ge(var_done, n + 1)
                        nc.gpsimd.tensor_tensor(rs[:, b, :], var[:, b, :], expo[:], ALU.pow).then_inc(rs_done, 1)
                steps(pool, body)

            @block.scalar
            def _(act):
                for c in range(CH):
                    act.wait_ge(centred, c + 1)
                    if c >= 2:
                        act.wait_ge(var_ready, c - 1)
                    nc.scalar.activation(sq[:, c % 2, :], x0[:, c, :], ACT.Square).then_inc(squared, 1)
                act.wait_ge(var_ready, CH + 1)
                nc.scalar.activation(st[:, 2, :], st[:, 1, :], ACT.Sqrt).then_inc(root_ready, 1)
                act.wait_ge(root_ready, 1)
                nc.scalar.activation(sq[:, 0, 0:1], st[:, 2, 0:1], ACT.Silu)

                def body(s, c, on):
                    if on(0):
                        act.wait_ge(x_ready, s + 1)
                        if late(s, 2):
                            act.wait_ge(y_ready, s - 1)
                        nc.scalar.activation(th[:, c % 2, :], ps[:, c, :], ACT.Tanh).then_inc(th_done, 1)
                    if on(1):
                        n, cn = s - 1, (c - 1) % CH
                        act.wait_ge(y_ready, n + 1)
                        if late(n, NG):
                            act.wait_ge(gn_done, n - NG + 1)
                        nc.scalar.activation(g_[:, cn % NG].rearrange("p r d -> p (r d)"), ps[:, cn, :],
                                             ACT.Silu).then_inc(g_done, 1)
                    if on(4):
                        n, b = s - 4, c % 2
                        act.wait_ge(gT_ready, n + 1)
                        if late(n, 2):
                            act.wait_ge(x_ready, n - 2 + CH + 1)
                        nc.scalar.activation(gT[:, b, :], ps[:, TB + b, :], ACT.Identity).then_inc(gT_done, 1)
                steps(act, body)

            @block.tensor
            def _(pe):
                for c in range(CH):
                    pe.wait_ge(x0_ready, c + 1)
                    nc.tensor.matmul(ps[:, c, :], ident[:], x0[:, c, :], start=True, stop=True,
                                     skip_group_check=True).then_inc(x_ready, 1)
                pe.wait_ge(weights_ready, 2)

                def body(s, c, on):
                    if on(5):
                        n, cn, b = s - 5, (c - 5) % CH, (c - 5) % 2
                        pe.wait_ge(gT_done, n + 1)
                        nc.tensor.matmul(ps[:, cn, :], ones[:], brow[:], start=True, stop=False, skip_group_check=True)
                        for j in range(CP):
                            last = nc.tensor.matmul(ps[:, cn, j * P:(j + 1) * P], gT[:, b, j * P:(j + 1) * P], wf[:],
                                                    start=False, stop=(j == CP - 1), skip_group_check=True)
                        last.then_inc(x_ready, 1)
                    if on(4):
                        n, b = s - 4, c % 2
                        pe.wait_ge(gn_done, n + 1)
                        if late(n, 2):
                            pe.wait_ge(gT_done, n - 1)
                        for j in range(CP):
                            last = nc.tensor.transpose(ps[:, TB + b, j * P:(j + 1) * P], gn[:, b, j, :], ident[:])
                        last.then_inc(gT_ready, 1)
                    if on(0):
                        pe.wait_ge(th_done, s + 1)
                        nc.tensor.matmul(ps[:, c, :], pct[:], th[:, c % 2, :], start=False, stop=True,
                                         skip_group_check=True).then_inc(y_ready, 1)
                steps(pe, body)

            @block.vector
            def _(dve):
                done = [0]

                def link(ins):
                    done[0] += 1
                    ins.then_inc(chain, 1)
                    dve.wait_ge(chain, done[0])

                v_.tensor_scalar(pct[:], ident[:], 0.01, None, ALU.mult).then_inc(weights_ready, 1)
                link(v_.memset(brow[:], 0.0))
                link(v_.tensor_copy(bres[:, 0, :], bfrow[:]))
                for i in range(3):
                    r = slice(32 * i, 32 * i + 1)
                    link(v_.tensor_copy(brow[r, :].rearrange("p (r d) -> p r d", d=D),
                                        bres[r, i % 2, :].rearrange("p (one d) -> p one d", one=1).to_broadcast([1, CR, D])))
                    if i < 2:
                        link(v_.tensor_copy(bpart[:], bres[:, i % 2, :]))
                        link(v_.tensor_tensor(bres[:, 1 - i % 2, :], bres[:, i % 2, :], bpart[:], ALU.subtract))
                v_.tensor_copy(bres[0:1, 0, 0:1], bres[0:1, 0, 0:1]).then_inc(weights_ready, 1)
                dve.wait_ge(loaded, 16)
                for c in range(CH):
                    r = slice(c * CR, (c + 1) * CR)
                    hv = h2[:, c, :].rearrange("p (r d) -> p r d", d=D)
                    link(v_.tensor_reduce(st[:, 0, r], hv, AX_X, ALU.add))
                    link(v_.tensor_scalar(st[:, 0, r], st[:, 0, r], 1.0 / D, None, ALU.mult))
                    v_.tensor_tensor(x0[:, c, :].rearrange("p (r d) -> p r d", d=D), hv, spread(st[:, 0, r], P, CR),
                                     ALU.subtract).then_inc(centred, 1)
                for c in range(CH):
                    r = slice(c * CR, (c + 1) * CR)
                    dve.wait_ge(squared, c + 1)
                    v_.tensor_reduce(st[:, 5, r], sq[:, c % 2, :].rearrange("p (r d) -> p r d", d=D), AX_X,
                                     ALU.add).then_inc(var_ready, 1)
                dve.wait_ge(var_ready, CH)
                v_.tensor_scalar(st[:, 1, :], st[:, 5, :], 1.0 / D, EPS, ALU.mult, ALU.add).then_inc(var_ready, 1)
                dve.wait_ge(root_ready, 1)
                inverse_root(link, v_, st[:, 2, :], st[:, 1, :], st[:, 3, :], st[:, 4, :])
                for c in range(CH):
                    r = slice(c * CR, (c + 1) * CR)
                    xv = x0[:, c, :].rearrange("p (r d) -> p r d", d=D)
                    v_.tensor_tensor(xv, xv, spread(st[:, 3, r], P, CR), ALU.mult).then_inc(x0_ready, 1)

                def body(s, c, on):
                    if on(4):
                        n, cn, b = s - 4, (c - 4) % CH, c % 2
                        dve.wait_ge(rs_done, n + 1)
                        if late(n, 2):
                            dve.wait_ge(gT_ready, n - 1)
                        v_.tensor_tensor(gn[:, b].rearrange("p j (i d) -> p (j i) d", i=2), g_[:, cn % NG],
                                         spread(rs[:, b, :], P, CR), ALU.mult).then_inc(gn_done, 1)
                    if on(2):
                        n, cn, b = s - 2, (c - 2) % CH, c % 2
                        dve.wait_ge(g_done, n + 1)
                        if late(n, 2):
                            dve.wait_ge(parts_done, 2 * n - 2)
                        for r in range(CR):
                            last = v_.bn_stats(bs[:, b, r, :], g_[:, cn % NG, r, :])
                        last.then_inc(bn_done, 1)
                    if on(2):
                        n, b = s - 2, c % 2
                        dve.wait_ge(bn_done, n + 1)
                        if late(n, 2):
                            dve.wait_ge(var_done, n - 1)
                        v_.tensor_tensor(dm[:, b, :], bs[:, b, :, 1], bs[:, b, :, 4], ALU.subtract).then_inc(diff_done, 1)
                        v_.scalar_tensor_tensor(s2[:, b, :], bs[:, b, :, 2], D * EPS, bs[:, b, :, 5], ALU.add,
                                                ALU.add).then_inc(parts_done, 1)
                        dve.wait_ge(diff_done, n + 1)
                        v_.scalar_tensor_tensor(q2[:, b, :], dm[:, b, :], D / 4.0, dm[:, b, :], ALU.mult,
                                                ALU.mult).then_inc(parts_done, 1)
                steps(dve, body)
                for c in range(CH):
                    dve.wait_ge(x_ready, N + c + 1)
                    v_.tensor_tensor(h2[:, c, :], h2[:, c, :], ps[:, c, :], ALU.add).then_inc(out_done, 1)


TOK = ["b", "g", "be", "m", "v"]


def kernel(**inputs):
    import concourse.bacc as _bacc
    from concourse.bass_utils import run_bass_kernel_spmd as _run

    a = {k: np.asarray(v) for k, v in inputs.items()}
    frames = a["x"].reshape(FRAMES, V, CIN)[np.minimum(np.arange(QUART * QF), FRAMES - 1)]
    x_v = frames.reshape(QUART, ZS, ZF, V, CIN).transpose(3, 0, 1, 4, 2).reshape(V, QUART, ZS, CIN * ZF)
    arrays = {
        "x_v": x_v,
        "txt": a["txt"],
        "AT": a["L0_tok_A"].T,
        "A": a["L0_tok_A"],
        "W0T": a["L0_tok_W0"].T,
        "W1": a["L0_tok_W1"],
        "W2": a["L0_tok_W2"],
    }
    for layer in range(3):
        for p in TOK:
            arrays[f"{p}{layer}"] = a[f"L0_tok_{p}{layer}"]
    for k in ("Wq", "bq", "Wk", "bk", "Wv", "bv"):
        arrays[k] = a[f"L0_attn_{k}"]
    arrays["WfT"] = a["L0_ffn_W"].T
    for k in ("ln_w", "ln_b", "b"):
        arrays[f"f_{k}"] = a[f"L0_ffn_{k}"]
    arrays = {k: np.ascontiguousarray(v) for k, v in arrays.items()}

    nc = _bacc.Bacc("TRN2", target_bir_lowering=False, num_devices=1)
    ap = {k: nc.dram_tensor(f"in_{k}", v.shape, mybir.dt.from_np(v.dtype), kind="ExternalInput").ap()
          for k, v in arrays.items()}
    out = nc.dram_tensor("out_0", (B, S, D), F32, kind="ExternalOutput").ap()
    build(nc, ap["x_v"], ap["txt"], ap["AT"], ap["A"], ap["W0T"], ap["W1"], ap["W2"],
          *[[ap[f"{p}{layer}"] for p in TOK] for layer in range(3)],
          [ap[k] for k in ("Wq", "bq", "Wk", "bk", "Wv", "bv")],
          [ap[k] for k in ("WfT", "f_ln_w", "f_ln_b", "f_b")], out)
    r = _run(nc, [{f"in_{k}": v for k, v in arrays.items()}], core_ids=[0])
    return r.results[0]["out_0"]
```

```python
from contextlib import ExitStack

import numpy as np

import concourse.bass as bass
from concourse import mybir

F32 = mybir.dt.float32
F16 = mybir.dt.float16
BF16 = mybir.dt.bfloat16
I32 = mybir.dt.int32
ALU = mybir.AluOpType
ACT = mybir.ActivationFunctionType
AX_X = mybir.AxisListType.X
RMAX = bass.bass_isa.ReduceOp.max

P = 128
B, T, V, CIN = 64, 64, 75, 3
FRAMES = B * T
C = 128
D = 64
TXT = 32
S = T + TXT
EPS = 1e-5
QUART = 4
GF = 5
PH = 3
R = GF * V // PH
GV = GF * V
GROUPS = 205
QF = GROUPS * GF
QROWS = QF * V
ZF = 41
ZK = GROUPS // ZF
ZN = ZK * QUART
ZROWS = ZF * GV
ZPAD = P - R
ZCOLS = (QROWS + ZPAD + 1) // 2 * 2
REGIONS = [(0, 2), (2, 4), (4, 5)]
XLOADS = 3
ITERS = 30
FCH = 6
FR = B * S // P // FCH
FW = FR * D
SPAN = [(0, 2), (1, 3), (3, 2)]
BAND0 = [0, 2 * V, 5 * V]
BANDW = 7 * V
PARTS = 2
MID = GF


def band_pieces():
    out = []
    for ph in range(PH):
        r = 0
        while r < R:
            flat = ph * R + r
            f, v = divmod(flat, V)
            n = min(V - v, R - r)
            out.append((ph, f, r, v, n))
            r += n
    return out


def build(nc, x_v, txt, AT, A, W0T, W1, W2, par01, par1, par2, weights, out):
    zs = nc.dram_tensor("z_parts", [ZK, QUART, 2, CIN, ZROWS], F16, kind="Internal").ap()
    h2_dram = nc.dram_tensor("h2_rows", [B * S, D], F32, kind="Internal").ap()
    pooled_dram = nc.dram_tensor("pooled_parts", [PARTS, QUART * QF, C], F32, kind="Internal").ap()
    ctx = ExitStack()

    def sb(name, shape, dt=F32):
        return ctx.enter_context(nc.sbuf_tensor(name, shape, dt))

    def sem(name):
        return ctx.enter_context(nc.semaphore(name))

    with ctx:
        ps = ctx.enter_context(nc.psum_tensor("ps", [P, 8, 512], F32))
        AThi = sb("AThi", [P, BANDW], F16)
        ATlo = sb("ATlo", [P, BANDW], F16)
        abar = sb("abar", [P, PH, 32])
        W0K = sb("W0K", [P, QUART, C], F16)
        W1hi = sb("W1hi", [P, C], F16)
        W1lo = sb("W1lo", [P, C], F16)
        negb1 = sb("negb1", [P, PH, C])
        W2s = sb("W2s", [P, D])
        b2row = sb("b2row", [P, D])
        ident = sb("ident", [P, P])
        z_loaded = [sem("z_near_loaded"), sem("z_far_loaded")]

        with nc.sbuf_tensor("zk", [P, ZCOLS], F16) as zk:
            setup(nc, ps, x_v, AT, A, W0T, W1, W2, par01, par1, par2, zs, zk, z_loaded,
                  AThi, ATlo, abar, W0K, W1hi, W1lo, negb1, W2s, b2row, ident)
            tokenise(nc, ps, zs, zk, z_loaded, pooled_dram, AThi, ATlo, abar, W0K, W1hi, W1lo, negb1)
        fuse(nc, ps, pooled_dram, h2_dram, txt, weights, W2s, b2row, ident, out)


def load_region(sp, zk, zs, i, done):
    k0, k1 = REGIONS[i]
    for q in range(QUART):
        for r0 in (32 * q, 32 * q + 6):
            sp.dma_start(zk[r0:r0 + 6, k0 * ZROWS:k1 * ZROWS].rearrange("r (k e) -> r k e", e=ZROWS),
                         zs[k0:k1, q].rearrange("k w c e -> (w c) k e")).then_inc(done, 16)


def setup(nc, ps, x_v, AT, A, W0T, W1, W2, par01, par1, par2, zs, zk, z_loaded,
          AThi, ATlo, abar, W0K, W1hi, W1lo, negb1, W2s, b2row, ident):
    with ExitStack() as ctx:
        def sb(name, shape, dt=F32):
            return ctx.enter_context(nc.sbuf_tensor(name, shape, dt))

        def sem(name):
            return ctx.enter_context(nc.semaphore(name))

        XW = QUART * GF * CIN * ZF
        XP = V * ZK // XLOADS
        xs = sb("xs", [P, 2, XW])
        at = sb("at", [V, V])
        a_rows = sb("a_rows", [V, V])
        band = sb("band", [P, BANDW])
        bandc = sb("bandc", [P, 7])
        w0 = sb("w0", [P, CIN])
        w1 = sb("w1", [P, C])
        w2 = sb("w2", [P, D])
        cols = sb("cols", [P, 2, 5])
        row1 = sb("row1", [P, 5, C])
        row2 = sb("row2", [P, 5, D])
        rc = sb("rc", [P, 4, 2])
        r1 = sb("r1", [P, 4, C])
        r2 = sb("r2", [P, 4, D])
        bc = sb("bc", [P, 2])
        b1r = sb("b1r", [P, C])
        b2r = sb("b2r", [P, D])
        mx = sb("mx", [P, 8])
        mxa = sb("mxa", [P, 8])
        sc = sb("sc", [P, 16])
        stack = sb("stack", [P, P])
        part = sb("part", [P, 2, CIN], F16)
        bpart = sb("bpart", [P, 3], F16)
        ones = sb("ones", [P, P])
        acol = sb("acol", [V, 2])
        cvec = sb("cvec", [P, P])
        SLOTS = 4
        BANKS = 7
        zp = sb("zp", [P, SLOTS, 2, GV + 1], F16)
        sz = sb("sz", [P, 1])

        loaded = sem("params_loaded")
        x_loaded = [sem(f"x_loaded{i}") for i in range(2)]
        x_reduced = sem("x_reduced")
        ones_filled = sem("ones_filled")
        band_clear = sem("band_clear")
        at_loaded = sem("at_loaded")
        band_loaded = sem("band_loaded")
        chain = sem("vector_chain")
        id_made = sem("ident_made")
        var_ready = sem("var_ready")
        root_ready = sem("root_ready")
        max_ready = sem("max_ready")
        max_all = sem("max_all")
        stack_ready = sem("stack_ready")
        stack_t = sem("stack_transposed")
        cvec_ready = sem("cvec_ready")
        const_ready = sem("const_ready")
        abar_ready = sem("abar_ready")
        asum_ready = sem("asum_ready")
        sz_ready = sem("sz_ready")
        z_ready = sem("z_product_ready")
        zhi_done = sem("z_hi_done")
        zlo_done = sem("z_lo_done")
        z_stored = [sem(f"z_stored{i}") for i in range(SLOTS)]

        pieces = band_pieces()
        NPAR = 7
        EARLY = REGIONS[0][1] * QUART

        with nc.Block() as block:
            @block.sync
            def _(sp):
                def load_x(j):
                    if j < XLOADS:
                        src = x_v.rearrange("v k w -> (v k w)").rearrange("(i p w) -> i p w", i=XLOADS, w=XW)[j]
                        dst = xs[0:XP, j % 2, :]
                    else:
                        src = x_v[:, j - XLOADS]
                        dst = xs[0:V, j % 2, :]
                    sp.dma_start(dst, src).then_inc(x_loaded[j % 2], 16)

                load_x(0)
                load_x(1)
                sp.wait_ge(band_clear, 1)
                for ph, f, r, v, n in pieces:
                    c0 = BAND0[ph] + (f - SPAN[ph][0]) * V
                    sp.dma_start(band[r:r + n, c0:c0 + V], AT[v:v + n, :]).then_inc(band_loaded, 16)
                for j in range(2, XLOADS + 2):
                    sp.wait_ge(x_reduced, j - 1)
                    load_x(j)
                for k in range(ZK):
                    for q in range(QUART):
                        n = k * QUART + q
                        sp.wait_ge(zhi_done, n + 1)
                        sp.wait_ge(zlo_done, n + 1)
                        sp.dma_start(zs[k, q].rearrange("w c (f e) -> (c f) w e", f=ZF),
                                     zp[0:CIN * ZF, n % SLOTS, :, 0:GV]).then_inc(z_stored[n % SLOTS], 16)
                    if k + 2 < ZK:
                        load_x(XLOADS + k + 2)
                    if k + 1 == REGIONS[0][1]:
                        sp.wait_ge(ones_filled, 1)
                        for slot in z_stored:
                            sp.wait_ge(slot, EARLY // SLOTS * 16)
                        load_region(sp, zk, zs, 0, z_loaded[0])
                for slot in z_stored:
                    sp.wait_ge(slot, ZN // SLOTS * 16)

            @block.scalar
            def _(act):
                act.dma_start(cols[:], par01).then_inc(loaded, 16)
                act.dma_start(w0[:], W0T).then_inc(loaded, 16)
                act.dma_start(at[:], AT).then_inc(at_loaded, 16)
                act.dma_start(a_rows[:], A).then_inc(loaded, 16)
                act.dma_start(w1[:], W1).then_inc(loaded, 16)
                act.dma_start(row1[:].rearrange("p i c -> p (i c)"),
                              par1.rearrange("i c -> (i c)").partition_broadcast(P)).then_inc(loaded, 16)
                act.dma_start(row2[:].rearrange("p i c -> p (i c)"),
                              par2.rearrange("i c -> (i c)").partition_broadcast(P)).then_inc(loaded, 16)
                act.dma_start(w2[:], W2).then_inc(loaded, 16)
                act.wait_ge(var_ready, 3)
                nc.scalar.activation(rc[:, 1, :], rc[:, 0, :], ACT.Sqrt).then_inc(root_ready, 1)
                nc.scalar.activation(r1[:, 1, :], r1[:, 0, :], ACT.Sqrt).then_inc(root_ready, 1)
                nc.scalar.activation(r2[:, 1, :], r2[:, 0, :], ACT.Sqrt).then_inc(root_ready, 1)
                act.wait_ge(sz_ready, 1)
                for n in range(ZN):
                    act.wait_ge(z_ready, n + 1)
                    if n >= SLOTS:
                        act.wait_ge(z_stored[n % SLOTS], n // SLOTS * 16)
                    nc.scalar.activation(zp[0:CIN * ZF, n % SLOTS, 0, 0:GV], ps[0:CIN * ZF, n % BANKS, 0:GV],
                                         ACT.Identity, scale=sz[0:CIN * ZF, :]).then_inc(zhi_done, 1)

            @block.gpsimd
            def _(pool):
                pool.memset(ident[:], 0.0).then_inc(id_made, 1)
                pool.wait_ge(id_made, 1)
                pool.affine_select(out=ident[:], in_=ident[:], compare_op=ALU.not_equal, fill=1.0, base=0,
                                   pattern=[[-1, P]], channel_multiplier=1).then_inc(id_made, 1)
                two = float(np.array([1.0, 1.0], np.float16).view(np.float32)[0])
                zk2 = zk[:].bitcast(F32)
                for i, (k0, k1) in enumerate(REGIONS):
                    if i == len(REGIONS) - 1:
                        pool.wait_ge(max_ready, 1)
                        pool.partition_all_reduce(mxa[:], mx[:], P, RMAX).then_inc(max_all, 1)
                    end = ZCOLS if k1 == ZK else k1 * ZROWS
                    pool.memset(zk2[:, k0 * ZROWS // 2:end // 2], two).then_inc(ones_filled, 1)

            @block.vector
            def _(dve):
                done = [0]

                def link(ins):
                    done[0] += 1
                    ins.then_inc(chain, 1)
                    dve.wait_ge(chain, done[0])

                def together(steps):
                    for ins in steps:
                        ins.then_inc(chain, 1)
                    done[0] += len(steps)
                    dve.wait_ge(chain, done[0])

                v_ = nc.vector
                v_.memset(band[:], 0.0).then_inc(band_clear, 1)
                link(v_.memset(mx[:], 0.0))
                link(v_.memset(ones[:], 1.0))
                link(v_.memset(stack[:], 0.0))
                link(v_.memset(abar[:], 0.0))
                link(v_.memset(W0K[:], 0.0))
                for j in range(XLOADS):
                    dve.wait_ge(x_loaded[j % 2], (j // 2 + 1) * 16)
                    v_.tensor_reduce(mx[0:XP, 5 + j:6 + j], xs[0:XP, j % 2, :], AX_X, ALU.max,
                                     apply_absolute_value=True).then_inc(x_reduced, 1)
                dve.wait_ge(x_reduced, XLOADS)
                link(v_.tensor_reduce(mx[0:XP, 1:2], mx[0:XP, 5:5 + XLOADS], AX_X, ALU.max))
                dve.wait_ge(loaded, NPAR * 16)
                v_.tensor_scalar(rc[:, 0, :], cols[:, :, 4], EPS, None, ALU.add).then_inc(var_ready, 1)
                v_.tensor_scalar(r1[:, 0, :], row1[:, 4, :], EPS, None, ALU.add).then_inc(var_ready, 1)
                v_.tensor_scalar(r2[:, 0, :], row2[:, 4, :], EPS, None, ALU.add).then_inc(var_ready, 1)
                dve.wait_ge(root_ready, 3)
                folds = ((rc, cols[:, :, 1], cols[:, :, 0], cols[:, :, 2], cols[:, :, 3], bc[:]),
                         (r1, row1[:, 1, :], row1[:, 0, :], row1[:, 2, :], row1[:, 3, :], b1r[:]),
                         (r2, row2[:, 1, :], row2[:, 0, :], row2[:, 2, :], row2[:, 3, :], b2r[:]))
                together([v_.reciprocal(r[:, 2, :], r[:, 1, :]) for r, g, b, be, m, bias in folds])
                together([v_.tensor_tensor(r[:, 3, :], r[:, 2, :], r[:, 2, :], ALU.mult) for r, g, b, be, m, bias in folds])
                together([v_.tensor_tensor(r[:, 3, :], r[:, 3, :], r[:, 0, :], ALU.mult) for r, g, b, be, m, bias in folds])
                together([v_.tensor_scalar(r[:, 3, :], r[:, 3, :], -0.5, 1.5, ALU.mult, ALU.add)
                          for r, g, b, be, m, bias in folds])
                together([v_.tensor_tensor(r[:, 2, :], r[:, 2, :], r[:, 3, :], ALU.mult) for r, g, b, be, m, bias in folds])
                together([v_.tensor_tensor(r[:, 2, :], r[:, 2, :], g, ALU.mult) for r, g, b, be, m, bias in folds])
                together([v_.tensor_tensor(r[:, 3, :], b, m, ALU.subtract) for r, g, b, be, m, bias in folds])
                together([v_.tensor_tensor(r[:, 3, :], r[:, 3, :], r[:, 2, :], ALU.mult) for r, g, b, be, m, bias in folds])
                together([v_.tensor_tensor(bias, r[:, 3, :], be, ALU.add) for r, g, b, be, m, bias in folds])
                together([v_.tensor_scalar(w0[:], w0[:], rc[:, 2, 0:1], None, ALU.mult),
                          v_.tensor_tensor(w1[:], w1[:], r1[:, 2, :], ALU.mult),
                          v_.tensor_tensor(w2[:], w2[:], r2[:, 2, :], ALU.mult)])
                together([v_.tensor_reduce(mx[0:V, 0:1], a_rows[:], AX_X, ALU.add, apply_absolute_value=True),
                          v_.tensor_reduce(mx[:, 2:3], w0[:], AX_X, ALU.add, apply_absolute_value=True),
                          v_.tensor_reduce(mx[:, 3:4], bc[:, 0:1], AX_X, ALU.max, apply_absolute_value=True)])
                v_.tensor_reduce(mx[:, 4:5], w1[:], AX_X, ALU.max, apply_absolute_value=True).then_inc(max_ready, 1)
                dve.wait_ge(max_all, 1)
                link(v_.tensor_copy(sc[:, 0:1], mxa[:, 0:1]))
                link(v_.tensor_tensor(sc[:, 1:2], mxa[:, 1:2], mxa[:, 0:1], ALU.mult))
                link(v_.scalar_tensor_tensor(sc[:, 2:3], sc[:, 1:2], mxa[:, 2:3], mxa[:, 3:4], ALU.mult, ALU.add))
                link(v_.tensor_copy(sc[:, 3:4], mxa[:, 4:5]))
                link(v_.tensor_scalar(sc[:, 0:4], sc[:, 0:4], 1e-30, None, ALU.max))
                link(v_.reciprocal(sc[:, 8:12], sc[:, 0:4]))
                link(v_.tensor_scalar(sc[:, 4:8].bitcast(I32), sc[:, 8:12].bitcast(I32), 0x7F800000, None,
                                      ALU.bitwise_and))
                link(v_.tensor_scalar(sc[:, 4:5], sc[:, 4:5], 2.0 ** 7, None, ALU.mult))
                link(v_.tensor_scalar(sc[:, 5:7], sc[:, 5:7], 2.0 ** 8, None, ALU.mult))
                link(v_.tensor_scalar(sc[:, 7:8], sc[:, 7:8], 2.0 ** 4, None, ALU.mult))
                v_.tensor_copy(sz[:], sc[:, 5:6]).then_inc(sz_ready, 1)
                link(v_.reciprocal(sc[:, 12:13], sc[:, 5:6]))
                link(v_.tensor_tensor(sc[:, 12:13], sc[:, 12:13], sc[:, 6:7], ALU.mult))
                link(v_.tensor_tensor(sc[:, 13:14], sc[:, 4:5], sc[:, 6:7], ALU.mult))
                link(v_.tensor_tensor(sc[:, 13:14], sc[:, 13:14], sc[:, 7:8], ALU.mult))
                link(v_.reciprocal(sc[:, 14:15], sc[:, 13:14]))

                def z_low(n):
                    dve.wait_ge(zhi_done, n + 1)
                    if n >= SLOTS:
                        dve.wait_ge(z_stored[n % SLOTS], n // SLOTS * 16)
                    v_.scalar_tensor_tensor(zp[0:CIN * ZF, n % SLOTS, 1, 0:GV], ps[0:CIN * ZF, n % BANKS, 0:GV],
                                            sz[0:CIN * ZF, :], zp[0:CIN * ZF, n % SLOTS, 0, 0:GV],
                                            ALU.mult, ALU.subtract).then_inc(zlo_done, 1)
                for n in range(EARLY):
                    z_low(n)

                dve.wait_ge(band_loaded, len(pieces) * 16)
                link(v_.tensor_reduce(bandc[:], band[:].rearrange("p (f u) -> p f u", u=V), AX_X, ALU.add))
                at_col = 0
                for ph in range(PH):
                    f0, n = SPAN[ph]
                    if n == 2:
                        v_.tensor_scalar(abar[:, ph, f0:f0 + n], bandc[:, at_col:at_col + n], 1.0 / V, None, ALU.mult)
                    else:
                        v_.tensor_scalar(abar[:, ph, f0:f0 + n:2], bandc[:, at_col:at_col + n:2], 1.0 / V, None, ALU.mult)
                        v_.tensor_scalar(abar[:, ph, MID:MID + 1], bandc[:, at_col + 1:at_col + 2], 1.0 / V, None, ALU.mult)
                    at_col += n
                z_low(EARLY + 0)
                link(v_.tensor_scalar(band[:], band[:], sc[:, 4:5], None, ALU.mult))
                z_low(EARLY + 1)
                link(v_.tensor_copy(AThi[:], band[:]))
                z_low(EARLY + 2)
                link(v_.tensor_tensor(ATlo[:], band[:], AThi[:], ALU.subtract))
                z_low(EARLY + 3)
                link(v_.tensor_scalar(w1[:], w1[:], sc[:, 7:8], None, ALU.mult))
                link(v_.tensor_copy(W1hi[:], w1[:]))
                z_low(EARLY + 4)
                link(v_.tensor_tensor(W1lo[:], w1[:], W1hi[:], ALU.subtract))
                z_low(EARLY + 5)
                for ph in range(PH):
                    link(v_.tensor_scalar(negb1[:, ph, :], b1r[:], sc[:, 13:14], -1.0, ALU.mult, ALU.mult))
                z_low(EARLY + 6)
                link(v_.tensor_scalar(w0[:], w0[:], sc[:, 12:13], None, ALU.mult))
                z_low(EARLY + 7)
                link(v_.tensor_copy(part[:, 0, :], w0[:]))
                link(v_.tensor_tensor(part[:, 1, :], w0[:], part[:, 0, :], ALU.subtract))
                z_low(EARLY + 8)
                link(v_.tensor_tensor(bc[:, 0:1], bc[:, 0:1], sc[:, 6:7], ALU.mult))
                for i in range(3):
                    link(v_.tensor_copy(bpart[:, i:i + 1], bc[:, 0:1]))
                    link(v_.tensor_tensor(bc[:, 0:1], bc[:, 0:1], bpart[:, i:i + 1], ALU.subtract))
                    z_low(EARLY + 9 + i)
                for i, src in enumerate((part[:, 0, :], part[:, 0, :], part[:, 1, :], part[:, 1, :], bpart[:])):
                    v_.tensor_copy(stack[:].rearrange("p (q r) -> p q r", q=QUART)[:, :, 3 * i:3 * i + 3],
                                   src.rearrange("p (one r) -> p one r", one=1).to_broadcast([P, QUART, 3])).then_inc(stack_ready, 1)
                dve.wait_ge(at_loaded, 16)
                link(v_.tensor_reduce(acol[:, 0:1], at[:], AX_X, ALU.add))
                v_.tensor_scalar(acol[:, 1:2], acol[:, 0:1], 1.0 / V, None, ALU.mult).then_inc(abar_ready, 1)
                dve.wait_ge(asum_ready, 1)
                link(v_.tensor_copy(sc[:, 15:16], ps[:, BANKS, 0:1]))
                link(v_.tensor_tensor(sc[:, 15:16], sc[:, 15:16], bc[:, 1:2], ALU.mult))
                v_.tensor_copy(cvec[:], sc[:, 15:16].to_broadcast([P, P])).then_inc(cvec_ready, 1)
                dve.wait_ge(stack_t, 1)
                for q in range(QUART):
                    v_.tensor_copy(W0K[32 * q:32 * q + 32, q, :], ps[32 * q:32 * q + 32, BANKS, C:2 * C])
                dve.wait_ge(const_ready, 1)
                link(v_.tensor_tensor(b2row[:], ps[:, BANKS, D:2 * D], b2r[:], ALU.add))
                link(v_.tensor_scalar(W2s[:], w2[:], sc[:, 14:15], None, ALU.mult))
            @block.tensor
            def _(pe):
                pe.wait_ge(at_loaded, 16)

                def mix_input(n):
                    k, q = divmod(n, QUART)
                    j = XLOADS + k
                    pe.wait_ge(x_loaded[j % 2], (j // 2 + 1) * 16)
                    if n >= BANKS:
                        pe.wait_ge(zlo_done, n - BANKS + 1)
                    for s in range(GF):
                        at_ = (q * GF + s) * CIN * ZF
                        last = nc.tensor.matmul(ps[0:CIN * ZF, n % BANKS, s * V:(s + 1) * V],
                                                xs[0:V, j % 2, at_:at_ + CIN * ZF], at[:], start=True, stop=True)
                    last.then_inc(z_ready, 1)
                for n in range(ZN):
                    mix_input(n)
                pe.wait_ge(abar_ready, 1)
                nc.tensor.matmul(ps[:, BANKS, 0:1], ones[0:V, :], acol[:, 1:2], start=True, stop=True).then_inc(asum_ready, 1)
                pe.wait_ge(cvec_ready, 1)
                nc.tensor.matmul(ps[:, BANKS, D:2 * D], cvec[:], w2[:], start=True, stop=True).then_inc(const_ready, 1)
                pe.wait_ge(stack_ready, 5)
                pe.wait_ge(id_made, 2)
                nc.tensor.transpose(ps[:, BANKS, C:2 * C], stack[:], ident[:]).then_inc(stack_t, 1)


def tokenise(nc, ps, zs, zk, z_loaded, pooled_dram, AThi, ATlo, abar, W0K, W1hi, W1lo, negb1):
    with ExitStack() as ctx:
        def sb(name, shape, dt=F32):
            return ctx.enter_context(nc.sbuf_tensor(name, shape, dt))

        def sem(name):
            return ctx.enter_context(nc.semaphore(name))

        y0hi = sb("y0hi", [P, 2, PH, QUART * C], F16)
        y0lo = sb("y0lo", [P, 2, PH, QUART * C], F16)
        z1hi = sb("z1hi", [P, QUART, PH * P], F16)
        z1lo = sb("z1lo", [P, QUART, PH * P], F16)
        y1 = sb("y1", [P, 2, QUART, PH * C])
        stage = sb("stage", [96, 2, QUART, C])

        y0_ready = sem("y0_ready")
        y0hi_done = sem("y0hi_done")
        y0lo_done = sem("y0lo_done")
        z1_ready = sem("z1_ready")
        z1hi_done = sem("z1hi_done")
        z1lo_done = sem("z1lo_done")
        y1_ready = sem("y1_ready")
        y1_done = sem("y1_done")
        pooled_ready = sem("pooled_ready")
        staged = sem("staged")
        stored = [sem(f"pooled_stored{i}") for i in range(2)]

        STORES = [(0, 0, 2, 0), (0, 2, 1, 32 + MID), (0, 3, 2, 64 + 3), (1, 0, GF, 32)]
        Y0B, Z1B, Y1B, PLB = 0, 3, 5, 7
        LAST = GROUPS - 1
        NEAR = (REGIONS[0][1] * ZF - 3) // 2

        def steps(eng, body, cut=None):
            for it in range(3):
                body(it, it % 2, (it - 1) // 2)
            first = 1
            if cut:
                first = cut[0]
                with eng.Fori(1, first) as k:
                    body(k * 2 + 1, 1, k)
                    body(k * 2 + 2, 0, k)
                cut[1]()
            with eng.Fori(first, LAST // 2 - 1) as k:
                body(k * 2 + 1, 1, k)
                body(k * 2 + 2, 0, k)
            body(LAST - 1, 1, LAST // 2 - 1)
            body(LAST, 0, LAST // 2 - 1, last=True)

        def late(n, k):
            return not isinstance(n, int) or n >= k

        with nc.Block() as block:
            @block.sync
            def _(sp):
                for i in range(1, len(REGIONS)):
                    load_region(sp, zk, zs, i, z_loaded[1])

                def body(it, par, pair, last=False):
                    sp.wait_ge(staged, it + 1)
                    for part, f0, n, row in STORES:
                        dst = pooled_dram[part].rearrange("(q f) c -> f q c", q=QUART)[bass.ds(it * GF + f0, n)]
                        sp.dma_start(dst, stage[row:row + n, par]).then_inc(stored[par], 16)
                steps(sp, body)
                for par in range(2):
                    sp.wait_ge(stored[par], (GROUPS + 1 - par) // 2 * len(STORES) * 16)

            @block.tensor
            def _(pe):
                def layer0(it, ph):
                    n = it * PH + ph
                    if late(n, PH):
                        pe.wait_ge(y0lo_done, n - PH + 1)
                    nc.tensor.matmul(ps[:, Y0B + ph, :], zk[:, bass.ds(it * GV + ph * R, P)],
                                     W0K[:].rearrange("p q c -> p (q c)"), start=True, stop=True).then_inc(y0_ready, 1)

                def mix(it, par, q):
                    if q == 0:
                        pe.wait_ge(y0hi_done, it * PH + PH)
                        pe.wait_ge(y0lo_done, it * PH + PH)
                    m = it * QUART + q
                    if late(m, 2):
                        pe.wait_ge(z1lo_done, m - 1)
                    for ph in range(PH):
                        w = SPAN[ph][1] * V
                        o = ps[:, Z1B + q % 2, SPAN[ph][0] * V:SPAN[ph][0] * V + w]
                        hi = y0hi[0:R, par, ph, q * C:(q + 1) * C]
                        lo = y0lo[0:R, par, ph, q * C:(q + 1) * C]
                        ahi = AThi[0:R, BAND0[ph]:BAND0[ph] + w]
                        alo = ATlo[0:R, BAND0[ph]:BAND0[ph] + w]
                        nc.tensor.matmul(o, hi, ahi, start=(ph == 0), stop=False, skip_group_check=True)
                        nc.tensor.matmul(o, hi, alo, start=False, stop=False, skip_group_check=True)
                        last = nc.tensor.matmul(o, lo, ahi, start=False, stop=(ph == PH - 1), skip_group_check=True)
                    last.then_inc(z1_ready, 1)

                def layer1(it, q):
                    m = it * QUART + q
                    pe.wait_ge(z1lo_done, m + 1)
                    if late(m, 2):
                        pe.wait_ge(y1_done, m - 1)
                    for ph in range(PH):
                        o = ps[:, Y1B + q % 2, ph * C:(ph + 1) * C]
                        hi = z1hi[:, q, ph * R:ph * R + P]
                        lo = z1lo[:, q, ph * R:ph * R + P]
                        nc.tensor.matmul(o, hi, W1hi[:], start=True, stop=False)
                        nc.tensor.matmul(o, hi, W1lo[:], start=False, stop=False)
                        last = nc.tensor.matmul(o, lo, W1hi[:], start=False, stop=True)
                    last.then_inc(y1_ready, 1)

                def pool_joints(it, par):
                    pe.wait_ge(y1_done, it * QUART + QUART)
                    if late(it, 1):
                        pe.wait_ge(staged, it)
                    for ph in range(PH):
                        last = nc.tensor.matmul(ps[32 * ph:32 * ph + 32, PLB, :].rearrange("p (q c) -> p q c", q=QUART),
                                                abar[0:R, ph, :], y1[0:R, par, :, ph * C:(ph + 1) * C],
                                                start=True, stop=True)
                    last.then_inc(pooled_ready, 1)

                pe.wait_ge(z_loaded[0], QUART * 2 * 16)
                for ph in range(PH):
                    layer0(0, ph)

                def body(it, par, pair, last=False):
                    for q in range(QUART):
                        mix(it, par, q)
                        if q < PH and not last:
                            layer0(it + 1, q)
                        if q == QUART - 1 and late(it, 1):
                            pool_joints(it - 1, 1 - par)
                        if q >= 2:
                            layer1(it, q - 2)
                        elif late(it, 1):
                            layer1(it - 1, q + 2)
                steps(pe, body, (NEAR, lambda: pe.wait_ge(z_loaded[1], (len(REGIONS) - 1) * QUART * 2 * 16)))
                layer1(LAST, 2)
                layer1(LAST, 3)
                pool_joints(LAST, 0)

            @block.scalar
            def _(act):
                def y0_high(it, par, ph):
                    act.wait_ge(y0_ready, it * PH + ph + 1)
                    nc.scalar.activation(y0hi[0:R, par, ph, :], ps[0:R, Y0B + ph, :], ACT.Relu).then_inc(y0hi_done, 1)

                def z1_high(it, q):
                    act.wait_ge(z1_ready, it * QUART + q + 1)
                    nc.scalar.activation(z1hi[:, q, 0:GV], ps[:, Z1B + q % 2, 0:GV],
                                         ACT.Identity).then_inc(z1hi_done, 1)

                def stage_pool(it, par, half):
                    act.wait_ge(pooled_ready, it + 1)
                    if late(half, 1):
                        act.wait_ge(stored[par], half * (len(STORES) * 16))
                    nc.scalar.activation(stage[:, par].rearrange("p q c -> p (q c)"), ps[0:96, PLB, :],
                                         ACT.Identity).then_inc(staged, 1)

                for ph in range(PH):
                    y0_high(0, 0, ph)

                def body(it, par, pair, last=False):
                    for q in range(QUART):
                        z1_high(it, q)
                        if q < PH and not last:
                            y0_high(it + 1, 1 - par, q)
                    if late(it, 1):
                        stage_pool(it - 1, 1 - par, pair)
                steps(act, body)
                stage_pool(LAST, 0, LAST // 2)

            @block.vector
            def _(dve):
                nc.vector.memset(z1hi[:, :, GV:PH * P], 0.0)
                nc.vector.memset(z1lo[:, :, GV:PH * P], 0.0)

                def y0_low(it, par, ph):
                    dve.wait_ge(y0hi_done, it * PH + ph + 1)
                    nc.vector.scalar_tensor_tensor(y0lo[0:R, par, ph, :], ps[0:R, Y0B + ph, :], 0.0,
                                                   y0hi[0:R, par, ph, :], ALU.max, ALU.subtract).then_inc(y0lo_done, 1)

                def z1_low(it, q):
                    dve.wait_ge(z1hi_done, it * QUART + q + 1)
                    nc.vector.tensor_tensor(z1lo[:, q, 0:GV], ps[:, Z1B + q % 2, 0:GV],
                                            z1hi[:, q, 0:GV], ALU.subtract).then_inc(z1lo_done, 1)

                def relu1(it, par, q):
                    dve.wait_ge(y1_ready, it * QUART + q + 1)
                    nc.vector.tensor_tensor(y1[0:R, par, q, :], ps[0:R, Y1B + q % 2, 0:PH * C],
                                            negb1[0:R].rearrange("p f c -> p (f c)"), ALU.max).then_inc(y1_done, 1)

                for ph in range(PH):
                    y0_low(0, 0, ph)

                def body(it, par, pair, last=False):
                    for q in range(QUART):
                        if q == QUART - 1:
                            relu1(it, par, 0)
                        elif late(it, 1):
                            relu1(it - 1, 1 - par, q + 1)
                        z1_low(it, q)
                        if q < PH and not last:
                            y0_low(it + 1, 1 - par, q)
                steps(dve, body)
                for q in range(1, QUART):
                    relu1(LAST, 0, q)


def fuse(nc, ps, pooled_dram, h2_dram, txt, weights, W2s, b2row, ident, out):
    with ExitStack() as keep:
        def kept(name, shape, dt=F32):
            return keep.enter_context(nc.sbuf_tensor(name, shape, dt))

        w4 = kept("w4", [P, 4, P])
        wq, wk, wv, wf = (w4[:, i, :] for i in range(4))
        wcol = kept("wcol", [P, 4])
        wrow = kept("wrow", [P, 2, D])
        bqk, bvrow = wcol[:, 0:2], wrow[:, 0, :]
        pct = kept("pct", [P, P])
        ones = kept("ones_b", [P, P], BF16)
        brow = kept("brow", [P, FW], BF16)
        h2r = kept("h2r", [P, FCH, FW])
        h2_loaded = keep.enter_context(nc.semaphore("h2_loaded"))
        h = kept("h", [S, B, D])
        mean = kept("mean", [S, B])
        rstd = kept("rstd", [S, B])

        tokens(nc, ps, pooled_dram, txt, weights, W2s, b2row, ident, w4, wcol, wrow,
               pct, ones, brow, h, mean, rstd)
        attention(nc, ps, h2_dram, h2r, h2_loaded, ident, wq, wk, wv, bqk, bvrow, h, mean, rstd)
        feed_forward(nc, ps, h2r, h2_loaded, ident, wf, pct, ones, brow, out)


def tokens(nc, ps, pooled_dram, txt, weights, W2s, b2row, ident, w4, wcol, wrow,
           pct, ones, brow, h, mean, rstd):
    W4, w_cols, w_rows = weights
    wf, ln_w, ln_b, bf = w4[:, 3, :], wcol[:, 2:3], wcol[:, 3:4], wrow[:, 1, :]
    v_ = nc.vector
    NT = FRAMES // P
    TG = 4
    BG = 8
    with ExitStack() as ctx:
        def sb(name, shape, dt=F32):
            return ctx.enter_context(nc.sbuf_tensor(name, shape, dt))

        def sem(name):
            return ctx.enter_context(nc.semaphore(name))

        parts = sb("parts", [P, PARTS, NT, C])
        pooledT = sb("pooledT", [P, FRAMES])
        halves = sb("halves", [P, P])
        wfT = sb("wfT", [D, D])
        lbx = sb("lbx", [D, P])
        bres = sb("bres", [P, 2, D])
        bpart = sb("bias_part", [P, D], BF16)
        bs = sb("bn_parts_h", [S, B, 6])
        st = sb("st", [S, 6, B])

        parts_loaded = [sem(f"parts_loaded{i}") for i in range(NT // TG)]
        w_clear = sem("w_clear")
        w_loaded = sem("w_loaded")
        txt_loaded = sem("txt_loaded")
        chain = sem("vector_chain2")
        summed = sem("summed")
        turned = sem("turned")
        turned_out = sem("turned_out")
        tok_ready = sem("tok_ready")
        tok_done = sem("tok_done")
        wl_ready = sem("wl_ready")
        mean_ready = sem("mean_ready")
        var_ready = sem("var_ready2")
        root_ready = sem("root_ready2")

        with nc.Block() as block:
            @block.sync
            def _(sp):
                sp.dma_start(h[T:S], txt.rearrange("b s d -> s b d")).then_inc(txt_loaded, 16)
                for g in range(NT // TG):
                    for part in range(PARTS):
                        src = pooled_dram[part, g * TG * P:(g + 1) * TG * P, :].rearrange("(n p) c -> p n c", p=P)
                        sp.dma_start(parts[:, part, g * TG:(g + 1) * TG], src).then_inc(parts_loaded[g], 16)

            @block.scalar
            def _(act):
                act.wait_ge(w_clear, 1)
                for i in range(2):
                    half = slice(D * i, D * i + D)
                    act.dma_start(w4[half, :, half], W4).then_inc(w_loaded, 16)
                    act.dma_start(wcol[half, :], w_cols).then_inc(w_loaded, 16)
                act.dma_start(wfT[:], W4[:, 3, :]).then_inc(w_loaded, 16)
                act.dma_start(wrow[:].rearrange("p i d -> p (i d)"), w_rows.partition_broadcast(P)).then_inc(w_loaded, 16)
                for g in range(NT // TG):
                    act.wait_ge(turned, g + 1)
                    nc.scalar.activation(pooledT[:, g * TG * P:(g + 1) * TG * P], ps[:, g % 2, :],
                                         ACT.Identity).then_inc(turned_out, 1)
                act.wait_ge(var_ready, 1)
                nc.scalar.activation(st[:, 2, :], st[:, 1, :], ACT.Sqrt).then_inc(root_ready, 1)

            @block.vector
            def _(dve):
                done = [0]

                def link(ins):
                    done[0] += 1
                    ins.then_inc(chain, 1)
                    dve.wait_ge(chain, done[0])

                v_.memset(w4[:], 0.0).then_inc(w_clear, 1)
                link(v_.memset(halves[:], 0.0))
                for i in range(2):
                    link(v_.memset(halves[D * i:D * i + D, D * i:D * i + D], 1.0 / D))
                v_.memset(ones[:], 1.0)
                v_.tensor_scalar(pct[:], ident[:], 0.01, None, ALU.mult)
                link(v_.memset(brow[:], 0.0))
                dve.wait_ge(txt_loaded, 16)

                def sum_parts(g):
                    t = slice(g * TG, (g + 1) * TG)
                    dve.wait_ge(parts_loaded[g], PARTS * 16)
                    v_.tensor_tensor(parts[:, 0, t], parts[:, 0, t], parts[:, 1, t], ALU.add).then_inc(summed, 1)

                def fold_weights():
                    dve.wait_ge(w_loaded, 6 * 16)
                    link(v_.tensor_scalar(wf, wf, ln_w, D ** 0.5, ALU.mult, ALU.mult))
                    v_.tensor_copy(lbx[:], ln_b[0:D].to_broadcast([D, P])).then_inc(wl_ready, 1)
                    dve.wait_ge(mean_ready, 1)
                    link(v_.tensor_tensor(wf, wf, ps[:, 4, 0:P], ALU.subtract))
                    dve.wait_ge(mean_ready, 2)
                    link(v_.tensor_tensor(bres[:, 0, :], bf, ps[:, 5, 0:D], ALU.add))
                    for i in range(3):
                        r = slice(32 * i, 32 * i + 1)
                        v_.tensor_copy(brow[r, :].rearrange("p (r d) -> p r d", d=D),
                                       bres[r, i % 2, :].rearrange("p (one d) -> p one d", one=1).to_broadcast([1, FR, D]))
                        if i < 2:
                            link(v_.tensor_copy(bpart[:], bres[:, i % 2, :]))
                            link(v_.tensor_tensor(bres[:, 1 - i % 2, :], bres[:, i % 2, :], bpart[:], ALU.subtract))

                def finish(g):
                    dve.wait_ge(tok_ready, g + 1)
                    v_.tensor_tensor(h[0:T, g * BG:(g + 1) * BG, :],
                                     ps[0:T, 2 + g % 2, :].rearrange("p (b d) -> p b d", b=BG),
                                     b2row[0:T].rearrange("p (one d) -> p one d", one=1).to_broadcast([T, BG, D]),
                                     ALU.add).then_inc(tok_done, 1)
                    dve.wait_ge(tok_done, g + 1)
                    for b in range(g * BG, (g + 1) * BG):
                        last = v_.bn_stats(bs[:, b, :], h[:, b, :])
                    return last

                for g in range(NT // TG):
                    sum_parts(g)
                    if g == 2:
                        fold_weights()
                    if g >= 2:
                        finish(g - 2)
                finish(NT // TG - 2)
                link(finish(NT // TG - 1))
                v_.tensor_tensor(st[:, 0, :], bs[:, :, 1], bs[:, :, 4], ALU.add).then_inc(chain, 1)
                v_.tensor_tensor(st[:, 5, :], bs[:, :, 2], bs[:, :, 5], ALU.add).then_inc(chain, 1)
                done[0] += 2
                link(v_.tensor_tensor(st[:, 3, :], bs[:, :, 1], bs[:, :, 4], ALU.subtract))
                v_.tensor_scalar(mean[:], st[:, 0, :], 0.5, None, ALU.mult)
                link(v_.scalar_tensor_tensor(st[:, 4, :], st[:, 3, :], D / 4.0, st[:, 3, :], ALU.mult, ALU.mult))
                link(v_.tensor_tensor(st[:, 5, :], st[:, 5, :], st[:, 4, :], ALU.add))
                v_.tensor_scalar(st[:, 1, :], st[:, 5, :], 1.0 / D, EPS, ALU.mult, ALU.add).then_inc(var_ready, 1)
                dve.wait_ge(root_ready, 1)
                inverse_root(link, v_, st[:, 2, :], st[:, 1, :], rstd[:], st[:, 4, :])

            @block.tensor
            def _(pe):
                def turn(g):
                    pe.wait_ge(summed, g + 1)
                    if g >= 2:
                        pe.wait_ge(turned_out, g - 1)
                    for j in range(TG):
                        last = nc.tensor.transpose(ps[:, g % 2, j * P:(j + 1) * P], parts[:, 0, g * TG + j, :], ident[:])
                    last.then_inc(turned, 1)

                def means():
                    pe.wait_ge(wl_ready, 1)
                    nc.tensor.matmul(ps[:, 4, 0:P], halves[:], wf, start=True, stop=True).then_inc(mean_ready, 1)
                    nc.tensor.matmul(ps[:, 5, 0:D], lbx[:], wfT[:], start=True, stop=True).then_inc(mean_ready, 1)

                def make_tokens(g):
                    pe.wait_ge(turned_out, g + 1)
                    if g >= 2:
                        pe.wait_ge(tok_done, g - 1)
                    for j in range(BG):
                        b = g * BG + j
                        last = nc.tensor.matmul(ps[0:T, 2 + g % 2, j * D:(j + 1) * D], pooledT[:, b * T:(b + 1) * T],
                                                W2s[:], start=True, stop=True)
                    last.then_inc(tok_ready, 1)

                for g in range(NT // TG):
                    turn(g)
                    if g == 2:
                        means()
                    if g >= 1:
                        make_tokens(g - 1)
                make_tokens(NT // TG - 1)


def inverse_root(link, v_, root, x, out, tmp):
    link(v_.reciprocal(out, root))
    link(v_.tensor_tensor(tmp, out, out, ALU.mult))
    link(v_.tensor_tensor(tmp, tmp, x, ALU.mult))
    link(v_.tensor_scalar(tmp, tmp, -0.5, 1.5, ALU.mult, ALU.add))
    link(v_.tensor_tensor(out, out, tmp, ALU.mult))


def spread(ap, rows, n):
    return ap.rearrange("p (n one) -> p n one", one=1).to_broadcast([rows, n, D])


def attention(nc, ps, h2_dram, h2r, h2_loaded, ident, wq, wk, wv, bqk, bvrow, h, mean, rstd):
    v_ = nc.vector
    NG = 16
    GB = B // NG
    GP = GB // 2
    SCALE = float(D) ** -0.5
    with ExitStack() as ctx:
        def sb(name, shape, dt=F32):
            return ctx.enter_context(nc.sbuf_tensor(name, shape, dt))

        def sem(name):
            return ctx.enter_context(nc.semaphore(name))

        hc = sb("hc", [S, GB, D])
        hn = sb("hn", [S, GB, D])
        hT = sb("hT", [P, GP, S])
        qT = sb("qT", [P, GP, S])
        kT = sb("kT", [P, GP, S])
        val = sb("val", [S, B, D])
        dif = sb("dif", [S, GB, S])
        pr = sb("pr", [S, GB, S])
        prT = sb("prT", [S, GB, S])
        top = sb("top", [S, GB])
        den = sb("den", [S, B])
        inv = sb("inv", [S, B])
        h2 = sb("h2", [S, B, D])

        centred = sem("centred")
        hn_ready = sem("hn_ready")
        hT_ready = sem("hT_ready")
        hT_done = sem("hT_done")
        qk_ready = sem("qk_ready")
        val_ready = sem("val_ready")
        qk_done = sem("qk_done")
        val_done = sem("val_done")
        score_ready = sem("score_ready")
        top_done = sem("top_done")
        dif_done = sem("dif_done")
        exp_done = sem("exp_done")
        den_done = sem("den_done")
        inv_done = sem("inv_done")
        prT_ready = sem("prT_ready")
        prT_done = sem("prT_done")
        av_ready = sem("av_ready")
        av_done = sem("av_done")
        h2_done = sem("h2_done")
        stored = sem("h2_stored")

        HT, QK, VB, SC, PT, AV = 0, 1, 2, 3, 5, 6
        ORDER = [j for i in range(2) for j in range(i, GB, 2)]
        def steps(eng, body):
            for t in range(4):
                body(t, lambda lag, t=t: t - lag >= 0)
            with eng.Fori(4, NG) as t:
                body(t, lambda lag: True)
            for t in range(NG, NG + 4):
                body(t, lambda lag, t=t: t - lag < NG)

        def grp(g, n=GB):
            return bass.ds(g * n, n)

        with nc.Block() as block:
            @block.sync
            def _(sp):
                ready = 0
                for c in range(FCH):
                    need = -(-(c + 1) * P * FR // (GB * S))
                    with sp.Fori(ready, need) as g:
                        sp.wait_ge(h2_done, g + 1)
                        sp.dma_start(h2_dram.rearrange("(b s) d -> s b d", s=S)[:, grp(g)], h2[:, grp(g)]).then_inc(stored, 16)
                    sp.wait_ge(stored, need * 16)
                    if c >= 1:
                        sp.wait_ge(h2_loaded, c * 16)
                    sp.dma_start(h2r[:, c, :], h2_dram.rearrange("(c p n) d -> c p (n d)", c=FCH, p=P)[c]).then_inc(h2_loaded, 16)
                    ready = need

            @block.gpsimd
            def _(pool):
                def body(t, on):
                    if on(0):
                        g = t
                        if not isinstance(g, int) or g >= 1:
                            pool.wait_ge(hn_ready, g)
                        nc.gpsimd.tensor_tensor(hc[:], h[:, grp(g), :], spread(mean[:, grp(g)], S, GB),
                                                ALU.subtract).then_inc(centred, 1)
                        pool.wait_ge(centred, g + 1)
                        if not isinstance(g, int) or g >= 1:
                            pool.wait_ge(hT_ready, g)
                        nc.gpsimd.tensor_tensor(hn[:], hc[:], spread(rstd[:, grp(g)], S, GB), ALU.mult).then_inc(hn_ready, 1)
                    if on(4):
                        g = t - 4
                        pool.wait_ge(av_done, g + 1)
                        nc.gpsimd.tensor_tensor(h2[:, grp(g), :], h2[:, grp(g), :], h[:, grp(g), :],
                                                ALU.add).then_inc(h2_done, 1)
                steps(pool, body)

            @block.tensor
            def _(pe):
                def body(t, on):
                    if on(4):
                        g = t - 4
                        pe.wait_ge(prT_done, g + 1)
                        if not isinstance(g, int) or g >= 1:
                            pe.wait_ge(av_done, g)
                        for i, j in enumerate(ORDER):
                            last = nc.tensor.matmul(ps[0:S, AV, j * D:(j + 1) * D], prT[:, i, :], val[:, bass.ds(g * GB + j, 1), :].rearrange("p one d -> p (one d)"),
                                                    start=True, stop=True)
                        last.then_inc(av_ready, 1)
                    if on(2):
                        g = t - 2
                        pe.wait_ge(qk_done, 2 * g + 2)
                        if not isinstance(g, int) or g >= 1:
                            pe.wait_ge(dif_done, g)
                        for j in ORDER:
                            half = slice(D * (j % 2), D * (j % 2) + D)
                            last = nc.tensor.matmul(ps[0:S, SC + j % 2, j // 2 * S:(j // 2 + 1) * S], qT[half, j // 2, :],
                                                    kT[half, j // 2, :], start=True, stop=True)
                        last.then_inc(score_ready, 1)
                    if on(3):
                        g = t - 3
                        pe.wait_ge(exp_done, g + 1)
                        if not isinstance(g, int) or g >= 1:
                            pe.wait_ge(prT_done, g)
                        for j in range(GB):
                            last = nc.tensor.transpose(ps[0:S, PT, j * S:(j + 1) * S], pr[:, j, :], ident[0:S, 0:S])
                        last.then_inc(prT_ready, 1)
                    if on(1):
                        g = t - 1
                        pe.wait_ge(hT_done, g + 1)
                        if not isinstance(g, int) or g >= 1:
                            pe.wait_ge(qk_done, 2 * g)
                            pe.wait_ge(val_done, g)
                        for i, w in enumerate((wq, wk)):
                            last = nc.tensor.matmul(ps[:, QK, i * GP * S:(i + 1) * GP * S], w,
                                                    hT[:].rearrange("p g s -> p (g s)"), start=True, stop=True)
                        last.then_inc(qk_ready, 1)
                        for i in range(GP):
                            last = nc.tensor.matmul(ps[0:S, VB, i * P:(i + 1) * P], hT[:, i, :], wv, start=True, stop=True)
                        last.then_inc(val_ready, 1)
                    if on(0):
                        g = t
                        pe.wait_ge(hn_ready, g + 1)
                        if not isinstance(g, int) or g >= 1:
                            pe.wait_ge(hT_done, g)
                        for i in range(GP):
                            last = nc.tensor.transpose(ps[:, HT, i * S:(i + 1) * S],
                                                       hn[:, 2 * i:2 * i + 2, :].rearrange("p b d -> p (b d)"), ident[0:S, 0:S])
                        last.then_inc(hT_ready, 1)
                steps(pe, body)

            @block.scalar
            def _(act):
                def body(t, on):
                    if on(3):
                        g = t - 3
                        act.wait_ge(prT_ready, g + 1)
                        nc.scalar.activation(prT[:].rearrange("p b s -> p (b s)"), ps[0:S, PT, 0:GB * S],
                                             ACT.Identity).then_inc(prT_done, 1)
                    if on(1):
                        g = t - 1
                        act.wait_ge(qk_ready, g + 1)
                        for i, o in enumerate((qT, kT)):
                            nc.scalar.activation(o[:].rearrange("p g s -> p (g s)"), ps[:, QK, i * GP * S:(i + 1) * GP * S],
                                                 ACT.Identity, bias=bqk[:, i:i + 1]).then_inc(qk_done, 1)
                    if on(0):
                        g = t
                        act.wait_ge(hT_ready, g + 1)
                        nc.scalar.activation(hT[:].rearrange("p g s -> p (g s)"), ps[:, HT, 0:GP * S],
                                             ACT.Identity).then_inc(hT_done, 1)
                    if on(2):
                        g = t - 2
                        act.wait_ge(dif_done, g + 1)
                        if not isinstance(g, int) or g >= 1:
                            act.wait_ge(den_done, g)
                        nc.scalar.activation(pr[:].rearrange("p b s -> p (b s)"), dif[:].rearrange("p b s -> p (b s)"),
                                             ACT.Exp, scale=SCALE).then_inc(exp_done, 1)
                steps(act, body)

            @block.vector
            def _(dve):
                def body(t, on):
                    if on(4):
                        g = t - 4
                        dve.wait_ge(av_ready, g + 1)
                        dve.wait_ge(inv_done, g + 1)
                        v_.tensor_tensor(h2[:, grp(g), :], ps[0:S, AV, 0:GB * D].rearrange("p (b d) -> p b d", d=D),
                                         spread(inv[:, grp(g)], S, GB), ALU.mult).then_inc(av_done, 1)
                    if on(2):
                        g = t - 2
                        scores = ps[0:S, SC:SC + 2, 0:GP * S].rearrange("p i (j s) -> p i j s", s=S)
                        dve.wait_ge(score_ready, g + 1)
                        v_.tensor_reduce(top[:].rearrange("p (i j) -> p i j", i=2), scores, AX_X, ALU.max).then_inc(top_done, 1)
                    if on(3):
                        g = t - 3
                        dve.wait_ge(exp_done, g + 1)
                        v_.tensor_reduce(den[:, grp(g)].rearrange("p (j i) -> p i j", i=2), pr[:].rearrange("p (i j) s -> p i j s", i=2),
                                         AX_X, ALU.add).then_inc(den_done, 1)
                    if on(2):
                        g = t - 2
                        dve.wait_ge(top_done, g + 1)
                        if not isinstance(g, int) or g >= 1:
                            dve.wait_ge(exp_done, g)
                        v_.tensor_tensor(dif[:].rearrange("p (i j) s -> p i j s", i=2), scores,
                                         top[:].rearrange("p (i j one) -> p i j one", i=2, one=1).to_broadcast([S, 2, GP, S]),
                                         ALU.subtract).then_inc(dif_done, 1)
                    if on(1):
                        g = t - 1
                        dve.wait_ge(val_ready, g + 1)
                        v_.tensor_tensor(val[:, grp(g), :], ps[0:S, VB, 0:GB * D].rearrange("p (b d) -> p b d", d=D),
                                         bvrow[0:S].rearrange("p (one d) -> p one d", one=1).to_broadcast([S, GB, D]),
                                         ALU.add).then_inc(val_done, 1)
                    if on(3):
                        g = t - 3
                        dve.wait_ge(den_done, g + 1)
                        v_.reciprocal(inv[:, grp(g)], den[:, grp(g)]).then_inc(inv_done, 1)

                steps(dve, body)


def feed_forward(nc, ps, h2, h2_loaded, ident, wf, pct, ones, brow, out):
    v_ = nc.vector
    CH, CR, W = FCH, FR, FW
    CP = CR // 2
    TB = CH
    NG = 6
    N = ITERS * CH
    LAG = 5
    with ExitStack() as ctx:
        def sb(name, shape, dt=F32):
            return ctx.enter_context(nc.sbuf_tensor(name, shape, dt))

        def sem(name):
            return ctx.enter_context(nc.semaphore(name))

        x0 = sb("x0", [P, CH, W])
        x0c = sb("x0_centred", [P, 2, W])
        th = sb("th", [P, 2, W])
        g_ = sb("g", [P, NG, CR, D])
        gn = sb("gn", [P, 2, CP, P])
        gT = sb("gT", [P, 2, CP * P])
        sm = sb("sm", [P, 2, CR])
        bs, bs0 = (sb(f"bn_parts{i}", [P, 2, CR, 6]) for i in range(2))
        dm, dm0 = (sb(f"dm_{i}", [P, 2, CR]) for i in range(2))
        s2, s20 = (sb(f"s2_{i}", [P, 2, CR]) for i in range(2))
        q2, q20 = (sb(f"q2_{i}", [P, 2, CR]) for i in range(2))
        var, var0 = (sb(f"var64_{i}", [P, 2, CR]) for i in range(2))
        rs, rs0 = (sb(f"rs_{i}", [P, 2, CR]) for i in range(2))
        expo = sb("expo", [P, CR])
        warm = sb("warm", [P, 1])

        sum_done = sem("sum_done0")
        diff0 = sem("diff_done0")
        bn0 = sem("bn_done0")
        parts0_done = sem("parts_done0")
        var0_done = sem("var_done0")
        rs0_done = sem("rs_done0")
        centred = sem("centred0")
        expo_made = sem("expo_made")
        x0_ready = sem("x0_ready")
        x_ready = sem("x_ready")
        th_done = sem("th_done")
        y_ready = sem("y_ready")
        g_done = sem("g_done")
        bn_done = sem("bn_done")
        diff_done = sem("diff_done")
        parts_done = sem("parts_done")
        var_done = sem("var_done")
        rs_done = sem("rs_done")
        gn_done = sem("gn_done")
        gT_ready = sem("gT_ready")
        gT_done = sem("gT_done")
        out_done = sem("out_done")
        stored = sem("out_stored")

        def steps(eng, body, before=None):
            for s in range(CH):
                if before:
                    before(s)
                body(s, s, lambda lag, s=s: s - lag >= 0)
            with eng.Fori(1, ITERS) as it:
                for c in range(CH):
                    body(it * CH + c, c, lambda lag: True)
            for s in range(N, N + LAG):
                body(s, s - N, lambda lag, s=s: 0 <= s - lag < N)

        def late(n, k):
            return not isinstance(n, int) or n >= k

        out_rows = out.rearrange("b s d -> (b s d)").rearrange("(c p n) -> c p n", c=CH, p=P)

        with nc.Block() as block:
            @block.sync
            def _(sp):
                for c in range(CH):
                    sp.wait_ge(out_done, c + 1)
                    sp.dma_start(out_rows[c], h2[:, c, :]).then_inc(stored, 16)
                sp.wait_ge(stored, CH * 16)

            @block.gpsimd
            def _(pool):
                pool.memset(expo[:], -0.5).then_inc(expo_made, 1)
                pool.wait_ge(expo_made, 1)

                def inverse_roots(s2, q2, var, rs, b, n, added, rooted):
                    nc.gpsimd.tensor_tensor(var[:, b, :], s2[:, b, :], q2[:, b, :], ALU.add).then_inc(added, 1)
                    pool.wait_ge(added, n + 1)
                    nc.gpsimd.tensor_tensor(rs[:, b, :], var[:, b, :], expo[:], ALU.pow).then_inc(rooted, 1)

                def first(c):
                    if c < CH:
                        pool.wait_ge(parts0_done, 2 * c + 2)
                        if c >= 2:
                            pool.wait_ge(x0_ready, c - 1)
                        inverse_roots(s20, q20, var0, rs0, c % 2, c, var0_done, rs0_done)
                first(0)

                def body(s, c, on):
                    if on(2):
                        n, b = s - 2, c % 2
                        pool.wait_ge(parts_done, 2 * n + 2)
                        if late(n, 2):
                            pool.wait_ge(gn_done, n - 1)
                        inverse_roots(s2, q2, var, rs, b, n, var_done, rs_done)
                steps(pool, body, lambda s: first(s + 1))

            @block.scalar
            def _(act):
                nc.scalar.activation(warm[:], ident[:, 0:1], ACT.Silu)

                def body(s, c, on):
                    if on(0):
                        act.wait_ge(x_ready, s + 1)
                        if late(s, 2):
                            act.wait_ge(y_ready, s - 1)
                        nc.scalar.activation(th[:, c % 2, :], ps[:, c, :], ACT.Tanh).then_inc(th_done, 1)
                    if on(1):
                        n, cn = s - 1, (c - 1) % CH
                        act.wait_ge(y_ready, n + 1)
                        if late(n, NG):
                            act.wait_ge(gn_done, n - NG + 1)
                        nc.scalar.activation(g_[:, cn % NG].rearrange("p r d -> p (r d)"), ps[:, cn, :],
                                             ACT.Silu).then_inc(g_done, 1)
                    if on(4):
                        n, b = s - 4, c % 2
                        act.wait_ge(gT_ready, n + 1)
                        if late(n, 2):
                            act.wait_ge(x_ready, n - 2 + CH + 1)
                        nc.scalar.activation(gT[:, b, :], ps[:, TB + b, :], ACT.Identity).then_inc(gT_done, 1)
                steps(act, body)

            @block.tensor
            def _(pe):
                def first(c):
                    pe.wait_ge(x0_ready, c + 1)
                    nc.tensor.matmul(ps[:, c, :], ident[:], x0[:, c, :], start=True, stop=True,
                                     skip_group_check=True).then_inc(x_ready, 1)

                def body(s, c, on):
                    if on(5):
                        n, cn, b = s - 5, (c - 5) % CH, (c - 5) % 2
                        pe.wait_ge(gT_done, n + 1)
                        nc.tensor.matmul(ps[:, cn, :], ones[:], brow[:], start=True, stop=False, skip_group_check=True)
                        for j in range(CP):
                            last = nc.tensor.matmul(ps[:, cn, j * P:(j + 1) * P], gT[:, b, j * P:(j + 1) * P], wf,
                                                    start=False, stop=(j == CP - 1), skip_group_check=True)
                        last.then_inc(x_ready, 1)
                    if on(4):
                        n, b = s - 4, c % 2
                        pe.wait_ge(gn_done, n + 1)
                        if late(n, 2):
                            pe.wait_ge(gT_done, n - 1)
                        for j in range(CP):
                            last = nc.tensor.transpose(ps[:, TB + b, j * P:(j + 1) * P], gn[:, b, j, :], ident[:])
                        last.then_inc(gT_ready, 1)
                    if on(0):
                        pe.wait_ge(th_done, s + 1)
                        nc.tensor.matmul(ps[:, c, :], pct[:], th[:, c % 2, :], start=False, stop=True,
                                         skip_group_check=True).then_inc(y_ready, 1)
                steps(pe, body, first)

            @block.vector
            def _(dve):
                def statistics(bs, dm, s2, q2, b, n, diffs, made, bns):
                    dve.wait_ge(bns, n + 1)
                    v_.tensor_tensor(dm[:, b, :], bs[:, b, :, 1], bs[:, b, :, 4], ALU.subtract).then_inc(diffs, 1)
                    v_.scalar_tensor_tensor(s2[:, b, :], bs[:, b, :, 2], D * EPS, bs[:, b, :, 5], ALU.add,
                                            ALU.add).then_inc(made, 1)
                    dve.wait_ge(diffs, n + 1)
                    v_.scalar_tensor_tensor(q2[:, b, :], dm[:, b, :], D / 4.0, dm[:, b, :], ALU.mult,
                                            ALU.mult).then_inc(made, 1)

                def centre(c):
                    b = c % 2
                    dve.wait_ge(h2_loaded, (c + 1) * 16)
                    if c >= 2:
                        dve.wait_ge(var0_done, c - 1)
                    for r in range(CR):
                        last = v_.bn_stats(bs0[:, b, r, :], h2[:, c, r * D:(r + 1) * D])
                    last.then_inc(bn0, 1)
                    statistics(bs0, dm0, s20, q20, b, c, diff0, parts0_done, bn0)
                    v_.tensor_tensor(sm[:, b, :], bs0[:, b, :, 1], bs0[:, b, :, 4], ALU.add).then_inc(sum_done, 1)
                    dve.wait_ge(sum_done, c + 1)
                    v_.scalar_tensor_tensor(x0c[:, b, :].rearrange("p (r d) -> p r d", d=D), spread(sm[:, b, :], P, CR),
                                            -0.5, h2[:, c, :].rearrange("p (r d) -> p r d", d=D), ALU.mult,
                                            ALU.add).then_inc(centred, 1)

                def first(c):
                    if c + 1 < CH:
                        centre(c + 1)
                    dve.wait_ge(centred, c + 1)
                    dve.wait_ge(rs0_done, c + 1)
                    v_.scalar_tensor_tensor(x0[:, c, :].rearrange("p (r d) -> p r d", d=D),
                                            x0c[:, c % 2, :].rearrange("p (r d) -> p r d", d=D), D ** 0.5,
                                            spread(rs0[:, c % 2, :], P, CR), ALU.mult, ALU.mult).then_inc(x0_ready, 1)
                centre(0)

                def body(s, c, on):
                    if on(4):
                        n, cn, b = s - 4, (c - 4) % CH, c % 2
                        dve.wait_ge(rs_done, n + 1)
                        if late(n, 2):
                            dve.wait_ge(gT_ready, n - 1)
                        v_.tensor_tensor(gn[:, b].rearrange("p j (i d) -> p (j i) d", i=2), g_[:, cn % NG],
                                         spread(rs[:, b, :], P, CR), ALU.mult).then_inc(gn_done, 1)
                    if on(2):
                        n, cn, b = s - 2, (c - 2) % CH, c % 2
                        dve.wait_ge(g_done, n + 1)
                        if late(n, 2):
                            dve.wait_ge(parts_done, 2 * n - 2)
                        for r in range(CR):
                            last = v_.bn_stats(bs[:, b, r, :], g_[:, cn % NG, r, :])
                        last.then_inc(bn_done, 1)
                    if on(2):
                        n, b = s - 2, c % 2
                        if late(n, 2):
                            dve.wait_ge(var_done, n - 1)
                        statistics(bs, dm, s2, q2, b, n, diff_done, parts_done, bn_done)
                steps(dve, body, first)
                for c in range(CH):
                    dve.wait_ge(x_ready, N + c + 1)
                    v_.tensor_tensor(h2[:, c, :], h2[:, c, :], ps[:, c, :], ALU.add).then_inc(out_done, 1)


TOK = ["b", "g", "be", "m", "v"]


def kernel(**inputs):
    import concourse.bacc as _bacc
    from concourse.bass_utils import run_bass_kernel_spmd as _run

    a = {k: np.asarray(v) for k, v in inputs.items()}
    frames = a["x"].reshape(FRAMES, V, CIN)[np.minimum(np.arange(QUART * QF), FRAMES - 1)]
    x_v = frames.reshape(QUART, ZK, ZF, GF, V, CIN).transpose(4, 1, 0, 3, 5, 2).reshape(V, ZK, QUART * GF * CIN * ZF)
    arrays = {
        "x_v": x_v,
        "txt": a["txt"],
        "AT": a["L0_tok_A"].T,
        "A": a["L0_tok_A"],
        "W0T": a["L0_tok_W0"].T,
        "W1": a["L0_tok_W1"],
        "W2": a["L0_tok_W2"],
    }
    arrays["par01"] = np.stack([[a[f"L0_tok_{p}{layer}"] for p in TOK] for layer in range(2)]).transpose(2, 0, 1)
    arrays["par1"] = np.stack([a[f"L0_tok_{p}1"] for p in TOK])
    arrays["par2"] = np.stack([a[f"L0_tok_{p}2"] for p in TOK])
    att, ff = (lambda k: a[f"L0_attn_{k}"]), (lambda k: a[f"L0_ffn_{k}"])
    arrays["W4"] = np.stack([att("Wq"), att("Wk"), att("Wv"), ff("W").T], axis=1)
    arrays["w_cols"] = np.stack([att("bq"), att("bk"), ff("ln_w"), ff("ln_b")], axis=1)
    arrays["w_rows"] = np.concatenate([att("bv"), ff("b")])
    arrays = {k: np.ascontiguousarray(v) for k, v in arrays.items()}

    nc = _bacc.Bacc("TRN2", target_bir_lowering=False, num_devices=1)
    ap = {k: nc.dram_tensor(f"in_{k}", v.shape, mybir.dt.from_np(v.dtype), kind="ExternalInput").ap()
          for k, v in arrays.items()}
    out = nc.dram_tensor("out_0", (B, S, D), F32, kind="ExternalOutput").ap()
    build(nc, ap["x_v"], ap["txt"], ap["AT"], ap["A"], ap["W0T"], ap["W1"], ap["W2"],
          ap["par01"], ap["par1"], ap["par2"],
          (ap["W4"], ap["w_cols"], ap["w_rows"]), out)
    r = _run(nc, [{f"in_{k}": v for k, v in arrays.items()}], core_ids=[0])
    return r.results[0]["out_0"]
```
